# Optimizing a Trainium2 kernel written in Bass

```python
import numpy as np
import jax
import jax.numpy as jnp

def _softmax(x, axis=-1):
    return jax.nn.softmax(x, axis=axis)

def _gelu(x):
    return jax.nn.gelu(x, approximate=True)

def _silu(x):
    return jax.nn.silu(x)

def _sigmoid(x):
    return jax.nn.sigmoid(x)

def _layernorm(x, axis=-1, eps=1e-05):
    m = jnp.mean(x, axis=axis, keepdims=True)
    v = jnp.var(x, axis=axis, keepdims=True)
    return (x - m) / jnp.sqrt(v + eps)

def _scatter_add(tgt, idx, src, axis=0):
    return tgt.at[idx].add(src)

def _segment_sum(src, seg, n):
    return jax.ops.segment_sum(src, seg, n)
kernel_name = 'mk_seq_postln_d1_jaxref_r8_b83ff8'

def setup_inputs(seed: int=0):
    np.random.seed(seed)
    _w = jnp.asarray

    def _L0_attn_setup():
        import jax, jax.numpy as jnp
        import numpy as np
        HIDDEN = 128
        HEADS = 16
        HEAD_DIM = HIDDEN // HEADS
        B, S = (4, 256)
        key = jax.random.key(seed)
        ks = jax.random.split(key, 10)
        scale = 1.0 / np.sqrt(HIDDEN)

        def lin(k):
            return jax.random.uniform(k, (HIDDEN, HIDDEN), jnp.float32, -scale, scale)
        return {'x': jax.random.normal(ks[0], (B, S, HIDDEN), jnp.float32), 'Wq': lin(ks[1]), 'bq': jnp.zeros((HIDDEN,), jnp.float32), 'Wk': lin(ks[2]), 'bk': jnp.zeros((HIDDEN,), jnp.float32), 'Wv': lin(ks[3]), 'bv': jnp.zeros((HIDDEN,), jnp.float32), 'Wo': lin(ks[4]), 'bo': jnp.zeros((HIDDEN,), jnp.float32), 'head_mask': jnp.ones((HEADS,), jnp.float32)}
    _L0_attn_in = _L0_attn_setup()

    def _L0_ffn_setup():
        import jax, jax.numpy as jnp
        import numpy as np
        import math
        N_EMBD = 128
        HIDDEN = 4 * N_EMBD
        N_EXPERTS = 8
        TOP_K = 2
        B, T = (4, 256)

        def new_gelu(x):
            c = math.sqrt(2.0 / math.pi)
            return 0.5 * x * (1.0 + jnp.tanh(c * (x + 0.044715 * x * x * x)))

        def _moe_forward(x, Wfc_s, bfc_s, Wproj_s, bproj_s, Wr, Wfc, bfc, Wproj, bproj):
            Bb, Tt, C = x.shape
            xf = x.reshape(Bb * Tt, C)
            N = Bb * Tt
            shared = new_gelu(xf @ Wfc_s + bfc_s) @ Wproj_s + bproj_s
            logits = xf @ Wr
            probs = jax.nn.softmax(logits, axis=-1)
            topk_p, topk_i = jax.lax.top_k(probs, TOP_K)
            topk_p = topk_p / jnp.sum(topk_p, axis=-1, keepdims=True)
            gate = jnp.zeros((N, N_EXPERTS), dtype=xf.dtype)
            gate = gate.at[jnp.arange(N)[:, None], topk_i].add(topk_p)
            routed = jnp.zeros_like(xf)
            for e in range(N_EXPERTS):
                h = new_gelu(xf @ Wfc[e] + bfc[e]) @ Wproj[e] + bproj[e]
                routed = routed + h * gate[:, e:e + 1]
            return (shared + routed).reshape(Bb, Tt, C)
        key = jax.random.key(seed)
        ks = jax.random.split(key, 10)
        s = 0.02
        return {'x': jax.random.normal(ks[0], (B, T, N_EMBD), dtype=jnp.float32), 'Wfc_s': jax.random.normal(ks[1], (N_EMBD, HIDDEN), dtype=jnp.float32) * s, 'bfc_s': jnp.zeros((HIDDEN,), dtype=jnp.float32), 'Wproj_s': jax.random.normal(ks[2], (HIDDEN, N_EMBD), dtype=jnp.float32) * s, 'bproj_s': jnp.zeros((N_EMBD,), dtype=jnp.float32), 'Wr': jax.random.normal(ks[3], (N_EMBD, N_EXPERTS), dtype=jnp.float32) * s, 'Wfc': jax.random.normal(ks[4], (N_EXPERTS, N_EMBD, HIDDEN), dtype=jnp.float32) * s, 'bfc': jnp.zeros((N_EXPERTS, HIDDEN), dtype=jnp.float32), 'Wproj': jax.random.normal(ks[5], (N_EXPERTS, HIDDEN, N_EMBD), dtype=jnp.float32) * s, 'bproj': jnp.zeros((N_EXPERTS, N_EMBD), dtype=jnp.float32)}
    _L0_ffn_in = _L0_ffn_setup()
    _d = {'L0_attn_x': _L0_attn_in['x'], 'L0_attn_Wq': _L0_attn_in['Wq'], 'L0_attn_bq': _L0_attn_in['bq'], 'L0_attn_Wk': _L0_attn_in['Wk'], 'L0_attn_bk': _L0_attn_in['bk'], 'L0_attn_Wv': _L0_attn_in['Wv'], 'L0_attn_bv': _L0_attn_in['bv'], 'L0_attn_Wo': _L0_attn_in['Wo'], 'L0_attn_bo': _L0_attn_in['bo'], 'L0_attn_head_mask': _L0_attn_in['head_mask'], 'L0_ffn_Wfc_s': _L0_ffn_in['Wfc_s'], 'L0_ffn_bfc_s': _L0_ffn_in['bfc_s'], 'L0_ffn_Wproj_s': _L0_ffn_in['Wproj_s'], 'L0_ffn_bproj_s': _L0_ffn_in['bproj_s'], 'L0_ffn_Wr': _L0_ffn_in['Wr'], 'L0_ffn_Wfc': _L0_ffn_in['Wfc'], 'L0_ffn_bfc': _L0_ffn_in['bfc'], 'L0_ffn_Wproj': _L0_ffn_in['Wproj'], 'L0_ffn_bproj': _L0_ffn_in['bproj']}
    _x0 = _d['L0_attn_x']
    _d['L0_attn_x'] = jax.random.normal(jax.random.fold_in(jax.random.key(seed), 1), (16, 256, 128), dtype=_x0.dtype)
    del _x0
    return _d

def reference(L0_attn_x, L0_attn_Wq, L0_attn_bq, L0_attn_Wk, L0_attn_bk, L0_attn_Wv, L0_attn_bv, L0_attn_Wo, L0_attn_bo, L0_attn_head_mask, L0_ffn_Wfc_s, L0_ffn_bfc_s, L0_ffn_Wproj_s, L0_ffn_bproj_s, L0_ffn_Wr, L0_ffn_Wfc, L0_ffn_bfc, L0_ffn_Wproj, L0_ffn_bproj):

    def _L0_attn_ref(x, Wq, bq, Wk, bk, Wv, bv, Wo, bo, head_mask):
        import jax, jax.numpy as jnp
        import numpy as np
        HIDDEN = 128
        HEADS = 16
        HEAD_DIM = HIDDEN // HEADS
        B, S = (4, 256)
        b, s, _ = x.shape
        q = (x @ Wq.T + bq).reshape(b, s, HEADS, HEAD_DIM)
        k = (x @ Wk.T + bk).reshape(b, s, HEADS, HEAD_DIM)
        v = (x @ Wv.T + bv).reshape(b, s, HEADS, HEAD_DIM)
        attn = jnp.einsum('bqhd,bkhd->bhqk', q, k) / np.sqrt(HEAD_DIM).astype(np.float32)
        attn = jax.nn.softmax(attn, axis=-1)
        attn = attn * head_mask[None, :, None, None]
        out = jnp.einsum('bhqk,bkhd->bqhd', attn, v).reshape(b, s, HIDDEN)
        return out @ Wo.T + bo

    def _L0_ffn_ref(x, Wfc_s, bfc_s, Wproj_s, bproj_s, Wr, Wfc, bfc, Wproj, bproj):
        import jax, jax.numpy as jnp
        import numpy as np
        import math
        N_EMBD = 128
        HIDDEN = 4 * N_EMBD
        N_EXPERTS = 8
        TOP_K = 2
        B, T = (4, 256)

        def new_gelu(x):
            c = math.sqrt(2.0 / math.pi)
            return 0.5 * x * (1.0 + jnp.tanh(c * (x + 0.044715 * x * x * x)))

        def _moe_forward(x, Wfc_s, bfc_s, Wproj_s, bproj_s, Wr, Wfc, bfc, Wproj, bproj):
            Bb, Tt, C = x.shape
            xf = x.reshape(Bb * Tt, C)
            N = Bb * Tt
            shared = new_gelu(xf @ Wfc_s + bfc_s) @ Wproj_s + bproj_s
            logits = xf @ Wr
            probs = jax.nn.softmax(logits, axis=-1)
            topk_p, topk_i = jax.lax.top_k(probs, TOP_K)
            topk_p = topk_p / jnp.sum(topk_p, axis=-1, keepdims=True)
            gate = jnp.zeros((N, N_EXPERTS), dtype=xf.dtype)
            gate = gate.at[jnp.arange(N)[:, None], topk_i].add(topk_p)
            routed = jnp.zeros_like(xf)
            for e in range(N_EXPERTS):
                h = new_gelu(xf @ Wfc[e] + bfc[e]) @ Wproj[e] + bproj[e]
                routed = routed + h * gate[:, e:e + 1]
            return (shared + routed).reshape(Bb, Tt, C)
        return _moe_forward(x, Wfc_s, bfc_s, Wproj_s, bproj_s, Wr, Wfc, bfc, Wproj, bproj)
    x = L0_attn_x
    x = _layernorm(x + _L0_attn_ref(x, L0_attn_Wq, L0_attn_bq, L0_attn_Wk, L0_attn_bk, L0_attn_Wv, L0_attn_bv, L0_attn_Wo, L0_attn_bo, L0_attn_head_mask), axis=-1)
    x = _layernorm(x + _L0_ffn_ref(x, L0_ffn_Wfc_s, L0_ffn_bfc_s, L0_ffn_Wproj_s, L0_ffn_bproj_s, L0_ffn_Wr, L0_ffn_Wfc, L0_ffn_bfc, L0_ffn_Wproj, L0_ffn_bproj), axis=-1)
    return x

_drawn_inputs = setup_inputs


def setup_inputs(seed=0):
    import zlib

    import numpy as np

    out = dict(_drawn_inputs(seed))
    spreads = {'L0_attn_bq': (0.0, 0.8),
     'L0_attn_bk': (0.0, 0.8),
     'L0_attn_bv': (0.0, 0.1),
     'L0_attn_bo': (0.0, 0.1),
     'L0_ffn_bfc_s': (0.0, 0.314),
     'L0_ffn_bproj_s': (0.0, 0.1),
     'L0_ffn_bfc': (0.0, 0.485),
     'L0_ffn_bproj': (0.0, 0.1)}
    factors = {'L0_attn_Wq': 3.991, 'L0_attn_Wk': 3.917}
    for name, (base, spread) in spreads.items():
        noise = np.random.default_rng([zlib.crc32(name.encode()), seed]).standard_normal(out[name].shape)
        drawn = base * np.exp(spread * noise) if base else spread * noise
        out[name] = jnp.asarray(drawn.astype(out[name].dtype))
    for name, factor in factors.items():
        out[name] = (out[name] * factor).astype(out[name].dtype)
    return out
```

```python
from contextlib import ExitStack

import concourse.bass as bass
from concourse import mybir

F32 = mybir.dt.float32
BF16 = mybir.dt.bfloat16
ACT = mybir.ActivationFunctionType
ALU = mybir.AluOpType
AX_X = mybir.AxisListType.X

P = 128
D = 128
HEADS = 16
DH = D // HEADS
BATCHES = 16
SEQ = 256
TOKENS = BATCHES * SEQ
TILES = SEQ // P
HALF = HEADS // 2
PAIRS = HEADS // 2
QUADS = HEADS // 4
EPS = 1e-5
SCORE_SCALE = float(DH) ** -0.5
ROW_MAX = 6 * DH
FIRST_LOOP, LOOPS = 2, 5


PASSED = [None]


class Batch:

    def __init__(self, u, c, back):
        self.half = u + (c - back) // 2
        self.par = (c - back) % 2
        self.n = self.half * 2 + self.par
        self.fixed = isinstance(u, int)

    def exists(self):
        return not self.fixed or 0 <= self.n < BATCHES

    def since(self, n):
        return not self.fixed or self.n >= n


def wait_first(eng, semaphore, value):
    eng.wait_ge(semaphore, value)
    if not isinstance(value, int):
        eng.sem_inc(PASSED[0], 1)


def run_steps(eng, step):
    for t in range(2 * FIRST_LOOP):
        step(t // 2, t % 2)
    with eng.Fori(FIRST_LOOP, FIRST_LOOP + LOOPS) as u:
        step(u, 0)
        step(u, 1)
    for t in range(2 * (FIRST_LOOP + LOOPS), BATCHES + 3):
        step(t // 2, t % 2)


def build_attention(nc, a):
    ctx = ExitStack()
    with ctx:
        def sb(name, shape, dt=F32):
            return ctx.enter_context(nc.sbuf_tensor(name, shape, dt))

        def ps(name, shape, dt=F32):
            return ctx.enter_context(nc.psum_tensor(name, shape, dt))

        def sem(name):
            return ctx.enter_context(nc.semaphore(name))

        q_rows = nc.dram_tensor("q_rows", [2, ROW_MAX + 3, HEADS, SEQ], BF16, kind="Internal").ap()
        k_rows = nc.dram_tensor("k_rows", [2, ROW_MAX, HEADS, SEQ], BF16, kind="Internal").ap()
        x1_rows = a["x1_rows"]

        wq = sb("wq", [D, D])
        wk = sb("wk", [D, D])
        wv = sb("wv", [D, D])
        wo = sb("wo", [D, D])
        bq = sb("bq", [D, 1])
        bk = sb("bk", [D, 1])
        bv = sb("bv", [D, 1])
        mask_col = sb("mask_col", [D, 1])
        mask_row = sb("mask_row", [P, HEADS])
        bo_row = sb("bo_row", [P, D])
        bv_masked = sb("bv_masked", [D, P])
        out_bias = sb("out_bias", [P, D])
        ident = sb("ident", [P, P])
        ident16 = sb("ident16", [P, P], BF16)
        zero_rows = sb("zero_rows", [3, HEADS * SEQ], BF16)
        one_rows = sb("one_rows", [3, HEADS * SEQ], BF16)
        minus_half = sb("minus_half", [P, TILES])

        x_t = sb("x_t", [D, 2, SEQ])
        x_in = sb("x_in", [P, 2, TILES, D])
        xb = sb("xb", [P, TILES, D])
        qk = sb("qk", [D, 2, SEQ])
        qk_rest = sb("qk_rest", [D, 2, SEQ])
        qk_parts = sb("qk_parts", [D, 2, 2, 3, SEQ], BF16)
        q_stack = sb("q_stack", [P, 2, HEADS, SEQ], BF16)
        k_stack = sb("k_stack", [P, 2, HEADS, SEQ], BF16)
        v_aug = sb("v_aug", [P, 2, TILES, HEADS, 32])
        row_max = sb("row_max", [P, HEADS, TILES])
        max_rest = sb("max_rest", [P, 2, HALF * TILES])
        max_parts = sb("max_parts", [P, 2, 3, HALF * TILES], BF16)
        max_t = sb("max_t", [3 * HALF * TILES, 2, P], BF16)
        probs = sb("probs", [P, 4, 2, TILES, SEQ])
        av = sb("av", [P, 2, SEQ])
        sum_inv = sb("sum_inv", [P, 2 * HEADS])
        sum_scale = sb("sum_scale", [P, 2 * HEADS])
        heads_out = sb("heads_out", [P, TILES, D])
        heads_t = sb("heads_t", [D, SEQ])
        stats = sb("stats", [P, TILES, 6])
        mean_var = sb("mean_var", [P, TILES, 2])
        var_eps = sb("var_eps", [P, TILES])
        rstd = sb("rstd", [P, TILES])
        scaled_mean = sb("scaled_mean", [P, TILES])
        shift = sb("shift", [P, TILES])
        x1 = sb("x1", [P, TILES, D])

        s1_ps = ps("s1_ps", [P, 2, TILES, SEQ])
        st_ps = ps("st_ps", [P, 2, 2, TILES, SEQ])
        av_ps = ps("av_ps", [P, 2, SEQ])
        misc_ps = ps("misc_ps", [P, 512])
        misc16 = misc_ps[:].bitcast(BF16)

        weights_in = sem("weights_in")
        bcast_in = sem("bcast_in")
        consts_made = sem("consts_made")
        zeros_out = sem("zeros_out")
        bv_made = sem("bv_made")
        bias_ps = sem("bias_ps")
        bias_made = sem("bias_made")
        xt_in = [sem("xt_in0"), sem("xt_in1")]
        x_loaded = [sem("x_loaded0"), sem("x_loaded1")]
        qk_projected = sem("qk_projected")
        qk_evacuated = sem("qk_evacuated")
        qk_split = sem("qk_split")
        rows_out = [sem("rows_out0"), sem("rows_out1")]
        stacks_in = [sem("stacks_in0"), sem("stacks_in1")]
        scores_ready = sem("scores_ready")
        max_done = sem("max_done")
        max_split = sem("max_split")
        max_turned = sem("max_turned")
        max_evacuated = sem("max_evacuated")
        max_in = [sem("max_in0"), sem("max_in1")]
        shifted_ready = sem("shifted_ready")
        exp_done = sem("exp_done")
        v_projected = sem("v_projected")
        v_evacuated = sem("v_evacuated")
        quad_done = sem("quad_done")
        av_evacuated = sem("av_evacuated")
        av_turned = sem("av_turned")
        normalised = sem("normalised")
        heads_turned = sem("heads_turned")
        heads_evacuated = sem("heads_evacuated")
        xb_made = sem("xb_made")
        y_ready = sem("y_ready")
        stats_done = sem("stats_done")
        scale_done = sem("scale_done")
        x1_made = sem("x1_made")
        x1_out = sem("x1_out")

        block = ctx.enter_context(nc.Block())

        @block.sync
        def _(sp):
            for tile, name in ((wq, "wq_t"), (wk, "wk_t"), (wv, "wv_t"), (wo, "wo_t"), (bq, "bq"), (bk, "bk"),
                               (bv, "bv")):
                sp.dma_start(tile[:], a[name]).then_inc(weights_in, 16)
            sp.dma_start(mask_col[:], a["mask"].unsqueeze(1).to_broadcast([HEADS, DH])).then_inc(weights_in, 16)

            def load_xt(b):
                sp.dma_start(x_t[:, b.par], a["x_t"][:, bass.ds(b.n * SEQ, SEQ)]).then_inc(xt_in[b.par], 16)

            load_xt(Batch(0, 0, 0))
            sp.dma_start(mask_row[:], a["mask"].partition_broadcast(P)).then_inc(bcast_in, 16)
            sp.dma_start(bo_row[:], a["bo"].partition_broadcast(P)).then_inc(bcast_in, 16)
            sp.wait_ge(consts_made, 5)
            for par in range(2):
                sp.dma_start(q_rows[par, ROW_MAX:ROW_MAX + 3].rearrange("r h t -> r (h t)"), zero_rows[:]).then_inc(zeros_out, 16)
                sp.dma_start(k_stack[ROW_MAX:ROW_MAX + 3, par].rearrange("r h t -> r (h t)"), one_rows[:]).then_inc(zeros_out, 16)
            sp.wait_ge(zeros_out, 64)

            def load_max(b, half):
                sp.wait_ge(max_evacuated, 2 * b.n + half + 1)
                for part in range(3):
                    rows = HALF * TILES
                    sp.dma_start(q_stack[ROW_MAX + part:ROW_MAX + part + 1, b.par, half * HALF:(half + 1) * HALF, :]
                                 .rearrange("o h (t q) -> o (h t) q", t=TILES),
                                 max_t[part * rows:(part + 1) * rows, half, :]).then_inc(max_in[half], 16)

            def step(u, c):
                b = Batch(u, c, 2)
                if b.exists():
                    load_max(b, 1)
                b = Batch(u, c, -1)
                if b.exists():
                    if b.since(2):
                        sp.wait_ge(v_projected, b.n - 1)
                    load_xt(b)
                b = Batch(u, c, 2)
                if b.exists():
                    if b.since(2):
                        sp.wait_ge(xb_made, b.n - 1)
                    sp.dma_start(x_in[:, b.par], a["x"][bass.ds(b.n * SEQ, SEQ), :].rearrange("(t p) d -> p t d", p=P))\
                      .then_inc(x_loaded[b.par], 16)
                b = Batch(u, c, 0)
                if b.exists():
                    q_to = q_rows[b.par, 0:ROW_MAX].rearrange("(r d) h t -> (d h) r t", r=6)
                    k_to = k_rows[b.par].rearrange("(r d) h t -> (d h) r t", r=6)
                    q_part, k_part = qk_parts[:, b.par, 0], qk_parts[:, b.par, 1]
                    if b.since(2):
                        sp.wait_ge(stacks_in[b.par], 32 * b.half)
                    sp.wait_ge(qk_split, 4 * b.n + 1)
                    for r in range(3):
                        sp.dma_start(k_to[:, r:r + 1], k_part[:, 0:1]).then_inc(rows_out[b.par], 16)
                    sp.wait_ge(qk_split, 4 * b.n + 3)
                    for r in range(3, 5):
                        sp.dma_start(k_to[:, r:r + 1], k_part[:, 1:2]).then_inc(rows_out[b.par], 16)
                    sp.wait_ge(qk_split, 4 * b.n + 4)
                    sp.dma_start(q_to[:, 0:3], q_part[:, 0:3]).then_inc(rows_out[b.par], 16)
                    sp.dma_start(q_to[:, 3:5], q_part[:, 0:2]).then_inc(rows_out[b.par], 16)
                    sp.dma_start(q_to[:, 5:6], q_part[:, 0:1]).then_inc(rows_out[b.par], 16)
                    sp.dma_start(k_to[:, 5:6], k_part[:, 2:3]).then_inc(rows_out[b.par], 16)
                    if b.since(2):
                        sp.wait_ge(shifted_ready, PAIRS * (b.n - 1))
                    sp.wait_ge(rows_out[b.par], 144 * (b.half + 1))
                    sp.dma_start(q_stack[0:ROW_MAX + 3, b.par], q_rows[b.par]).then_inc(stacks_in[b.par], 16)
                    sp.dma_start(k_stack[0:ROW_MAX, b.par], k_rows[b.par]).then_inc(stacks_in[b.par], 16)
                b = Batch(u, c, 1)
                if b.exists():
                    load_max(b, 0)
                b = Batch(u, c, 3)
                if b.exists():
                    sp.wait_ge(x1_made, 2 * b.n + 2)
                    sp.dma_start(x1_rows[bass.ds(b.n * SEQ, SEQ), :].rearrange("(t p) d -> p t d", p=P), x1[:])\
                      .then_inc(x1_out, 16)

            run_steps(sp, step)
            sp.wait_ge(x1_out, 16 * BATCHES)

        @block.gpsimd
        def _(pool):
            nc.gpsimd.memset(zero_rows[:], 0.0).then_inc(consts_made, 1)
            nc.gpsimd.memset(one_rows[:], 1.0).then_inc(consts_made, 1)
            nc.gpsimd.memset(ident[:], 0.0).then_inc(consts_made, 1)
            nc.gpsimd.memset(q_stack[:], 0.0).then_inc(consts_made, 1)
            nc.gpsimd.memset(k_stack[:], 0.0).then_inc(consts_made, 1)
            nc.gpsimd.memset(minus_half[:], -0.5).then_inc(consts_made, 1)
            pool.wait_ge(consts_made, 6)
            nc.gpsimd.affine_select(out=ident[:], in_=ident[:], compare_op=ALU.not_equal, fill=1.0, base=0,
                                    pattern=[[-1, P]], channel_multiplier=1).then_inc(consts_made, 1)
            pool.wait_ge(consts_made, 7)
            nc.gpsimd.tensor_copy(ident16[:], ident[:]).then_inc(consts_made, 1)

            def split_max(b, half):
                heads = slice(half * HALF, (half + 1) * HALF)
                largest = row_max[:, heads].rearrange("p h t -> p (h t)")
                rest, parts = max_rest[:, half], max_parts[:, half]
                done = (2 * b.n + half) * 4
                wait_first(pool, max_done, HEADS * b.n + (half + 1) * HALF)
                if b.since(1):
                    wait_first(pool, max_turned, 2 * b.n + half - 1)
                nc.gpsimd.tensor_scalar(parts[:, 0], largest, 1.0, 1.0, ALU.mult, ALU.mult).then_inc(max_split, 1)
                pool.wait_ge(max_split, done + 1)
                nc.gpsimd.tensor_tensor(rest, largest, parts[:, 0], ALU.subtract).then_inc(max_split, 1)
                wait_first(pool, max_split, done + 2)
                nc.gpsimd.tensor_scalar(parts[:, 1], rest, 1.0, 1.0, ALU.mult, ALU.mult).then_inc(max_split, 1)
                pool.wait_ge(max_split, done + 3)
                nc.gpsimd.tensor_tensor(parts[:, 2], rest, parts[:, 1], ALU.subtract).then_inc(max_split, 1)

            def split_qk(b):
                parts = qk_parts[:, b.par]
                wait_first(pool, qk_evacuated, 2 * b.n + 2)
                if b.since(2):
                    wait_first(pool, rows_out[b.par], 144 * b.half)
                nc.gpsimd.tensor_scalar(parts[:, :, 0], qk[:], 1.0, 1.0, ALU.mult, ALU.mult).then_inc(qk_split, 1)
                pool.wait_ge(qk_split, 4 * b.n + 1)
                nc.gpsimd.tensor_tensor(qk_rest[:], qk[:], parts[:, :, 0], ALU.subtract).then_inc(qk_split, 1)
                wait_first(pool, qk_split, 4 * b.n + 2)
                nc.gpsimd.tensor_scalar(parts[:, :, 1], qk_rest[:], 1.0, 1.0, ALU.mult, ALU.mult).then_inc(qk_split, 1)
                pool.wait_ge(qk_split, 4 * b.n + 3)
                nc.gpsimd.tensor_tensor(parts[:, :, 2], qk_rest[:], parts[:, :, 1], ALU.subtract).then_inc(qk_split, 1)

            def step(u, c):
                b = Batch(u, c, 2)
                if b.exists():
                    split_max(b, 1)
                b = Batch(u, c, 0)
                if b.exists():
                    split_qk(b)
                b = Batch(u, c, 3)
                if b.exists():
                    pool.wait_ge(x_loaded[b.par], 16 * (b.half + 1))
                    if b.since(1):
                        pool.wait_ge(y_ready, b.n)
                    else:
                        pool.wait_ge(bias_made, 1)
                    nc.gpsimd.tensor_tensor(xb[:], x_in[:, b.par], out_bias[:].unsqueeze(1).to_broadcast([P, TILES, D]),
                                            ALU.add).then_inc(xb_made, 1)
                b = Batch(u, c, 1)
                if b.exists():
                    split_max(b, 0)
                b = Batch(u, c, 3)
                if b.exists():
                    wait_first(pool, stats_done, 4 * b.n + 4)
                    if b.since(1):
                        wait_first(pool, x1_made, 2 * b.n)
                    nc.gpsimd.tensor_scalar(var_eps[:], mean_var[:, :, 1], EPS, None, ALU.add).then_inc(scale_done, 1)
                    pool.wait_ge(scale_done, 4 * b.n + 1)
                    nc.gpsimd.tensor_tensor(rstd[:], var_eps[:], minus_half[:], ALU.pow).then_inc(scale_done, 1)
                    pool.wait_ge(scale_done, 4 * b.n + 2)
                    nc.gpsimd.tensor_tensor(scaled_mean[:], mean_var[:, :, 0], rstd[:], ALU.mult).then_inc(scale_done, 1)
                    wait_first(pool, scale_done, 4 * b.n + 3)
                    nc.gpsimd.tensor_scalar(shift[:], scaled_mean[:], -1.0, 1.0, ALU.mult, ALU.mult).then_inc(scale_done, 1)

            run_steps(pool, step)

        @block.scalar
        def _(act):
            def exp_pair(b, p):
                act.wait_ge(shifted_ready, PAIRS * b.n + p + 1)
                if b.since(1) or p >= 4:
                    act.wait_ge(quad_done, 4 * b.n + p // 2 - 1)
                nc.scalar.activation(probs[:, p % 4], st_ps[:, p % 2], ACT.Exp, scale=SCORE_SCALE).then_inc(exp_done, 1)

            def evacuate_max(b, half):
                rows = 3 * HALF * TILES
                act.wait_ge(max_turned, 2 * b.n + half + 1)
                if b.since(1):
                    act.wait_ge(max_in[half], 48 * b.n)
                nc.scalar.activation(max_t[:, half], misc16[0:rows, 0:P], ACT.Copy).then_inc(max_evacuated, 1)

            def step(u, c):
                b = Batch(u, c, 0)
                if b.exists():
                    act.wait_ge(qk_projected, b.n + 1)
                    if b.since(1):
                        act.wait_ge(qk_split, 4 * b.n)
                    for side, bias in ((0, bq), (1, bk)):
                        nc.scalar.activation(qk[:, side], misc_ps[:, side * SEQ:(side + 1) * SEQ], ACT.Identity,
                                             bias=bias[:]).then_inc(qk_evacuated, 1)
                now, last = Batch(u, c, 2), Batch(u, c, 3)
                if now.exists():
                    exp_pair(now, 0)
                    evacuate_max(now, 1)
                if last.exists():
                    act.wait_ge(quad_done, 4 * last.n + 4)
                    if last.since(1):
                        act.wait_ge(av_turned, last.n)
                    nc.scalar.activation(av[:], av_ps[:], ACT.Copy).then_inc(av_evacuated, 1)
                b = Batch(u, c, 1)
                if b.exists():
                    act.wait_ge(v_projected, b.n + 1)
                    if b.since(2):
                        act.wait_ge(quad_done, 4 * (b.n - 1))
                    for s in range(2):
                        to = v_aug[:, b.par, :, s * HALF:(s + 1) * HALF, 16 * s:16 * s + DH]
                        of = misc_ps[:, 0:SEQ].rearrange("p (t s h d) -> p t s h d", t=TILES, s=2, d=DH)[:, :, s]
                        nc.scalar.activation(to, of, ACT.Copy).then_inc(v_evacuated, 1)
                if now.exists():
                    exp_pair(now, 1)
                    exp_pair(now, 2)
                if last.exists():
                    act.wait_ge(heads_turned, last.n + 1)
                    if last.since(1):
                        act.wait_ge(y_ready, last.n)
                    nc.scalar.activation(heads_t[:], misc_ps[:, 0:SEQ], ACT.Copy).then_inc(heads_evacuated, 1)
                if now.exists():
                    exp_pair(now, 3)
                    exp_pair(now, 4)
                if b.exists():
                    evacuate_max(b, 0)
                if now.exists():
                    exp_pair(now, 5)
                    exp_pair(now, 6)
                if last.exists():
                    act.wait_ge(scale_done, 4 * last.n + 4)
                    if last.since(1):
                        act.wait_ge(x1_out, 16 * last.n)
                    for t in range(TILES):
                        nc.scalar.activation(x1[:, t], misc_ps[:, t * D:(t + 1) * D], ACT.Identity,
                                             scale=rstd[:, t:t + 1], bias=shift[:, t:t + 1]).then_inc(x1_made, 1)
                if now.exists():
                    exp_pair(now, 7)

            act.wait_ge(weights_in, 128)
            run_steps(act, step)

        @block.vector
        def _(dve):
            nc.vector.memset(v_aug[:], 0.0).then_inc(bv_made, 1)
            dve.wait_ge(bv_made, 1)
            for s in range(2):
                nc.vector.memset(v_aug[:, :, :, s * HALF:(s + 1) * HALF, 16 * s + DH:16 * s + DH + 1], 1.0).then_inc(bv_made, 1)
            dve.wait_ge(weights_in, 128)
            nc.vector.tensor_tensor(bv_masked[:], bv[:].to_broadcast([D, P]), mask_col[:].to_broadcast([D, P]), ALU.mult)\
              .then_inc(bv_made, 1)
            dve.wait_ge(bias_ps, 1)
            dve.wait_ge(bcast_in, 32)
            nc.vector.tensor_tensor(out_bias[:], misc_ps[:, 0:D], bo_row[:], ALU.add).then_inc(bias_made, 1)

            def maxima(b, heads):
                for h in heads:
                    dve.wait_ge(scores_ready, HEADS * b.n + h + 1)
                    if h % HALF == 0 and b.since(1):
                        dve.wait_ge(max_split, (2 * b.n + h // HALF - 1) * 4)
                    nc.vector.tensor_reduce(row_max[:, h], s1_ps[:, h % 2], AX_X, ALU.max, negate=True).then_inc(max_done, 1)

            def step(u, c):
                now, last = Batch(u, c, 1), Batch(u, c, 3)
                if now.exists():
                    maxima(now, range(5))
                if last.exists():
                    blocks = misc_ps[:].rearrange("p (n r) -> p n r", r=16)
                    dve.wait_ge(av_turned, last.n + 1)
                    if last.since(1):
                        dve.wait_ge(heads_turned, last.n)
                    nc.vector.reciprocal(sum_inv[:].unsqueeze(2), blocks[:, :, DH:DH + 1]).then_inc(normalised, 1)
                    dve.wait_ge(normalised, 3 * last.n + 1)
                    nc.vector.tensor_tensor(sum_scale[:].rearrange("p (t h) -> p t h", t=TILES),
                                            sum_inv[:].rearrange("p (t h) -> p t h", t=TILES),
                                            mask_row[:].unsqueeze(1).to_broadcast([P, TILES, HEADS]), ALU.mult)\
                      .then_inc(normalised, 1)
                    dve.wait_ge(normalised, 3 * last.n + 2)
                    nc.vector.tensor_tensor(heads_out[:].rearrange("p t (h d) -> p (t h) d", d=DH), blocks[:, :, 0:DH],
                                            sum_scale[:].unsqueeze(2).to_broadcast([P, 2 * HEADS, DH]), ALU.mult)\
                      .then_inc(normalised, 1)
                if now.exists():
                    maxima(now, range(5, 12))
                if last.exists():
                    dve.wait_ge(y_ready, last.n + 1)
                    if last.since(1):
                        dve.wait_ge(scale_done, 4 * last.n)
                    for t in range(TILES):
                        nc.vector.bn_stats(stats[:, t], misc_ps[:, t * D:(t + 1) * D]).then_inc(stats_done, 1)
                    wait_first(dve, stats_done, 4 * last.n + 2)
                    for t in range(TILES):
                        nc.vector.bn_aggr(mean_var[:, t], stats[:, t]).then_inc(stats_done, 1)
                if now.exists():
                    maxima(now, range(12, HEADS))

            run_steps(dve, step)

        @block.tensor
        def _(pe):
            pe.wait_ge(bv_made, 4)
            pe.wait_ge(weights_in, 128)
            nc.tensor.matmul(misc_ps[:, 0:D], bv_masked[:], wo[:], start=True, stop=True).then_inc(bias_ps, 1)

            def scores(b, h):
                if h == 0:
                    pe.wait_ge(stacks_in[b.par], 32 * (b.half + 1))
                if b.since(1) or h >= 2:
                    pe.wait_ge(max_done, HEADS * b.n + h - 1)
                for t in range(TILES):
                    mm = nc.tensor.matmul(s1_ps[:, h % 2, t], q_stack[:, b.par, h, t * P:(t + 1) * P], k_stack[:, b.par, h],
                                          start=True, stop=True)
                mm.then_inc(scores_ready, 1)

            def shifted_scores(b, h):
                p = h // 2
                if h % HALF == 0:
                    pe.wait_ge(max_in[h // HALF], 48 * (b.n + 1))
                if h % 2 == 0 and (b.since(1) or p >= 2):
                    pe.wait_ge(exp_done, PAIRS * b.n + p - 1)
                for t in range(TILES):
                    mm = nc.tensor.matmul(st_ps[:, p % 2, h % 2, t], k_stack[:, b.par, h, t * P:(t + 1) * P],
                                          q_stack[:, b.par, h], start=True, stop=True)
                if h % 2:
                    mm.then_inc(shifted_ready, 1)

            def quad(b, g):
                r, s = g // 2, g % 2
                pe.wait_ge(exp_done, PAIRS * b.n + 2 * g + 2)
                if g == 0:
                    pe.wait_ge(v_evacuated, 2 * b.n + 2)
                    if b.since(1):
                        pe.wait_ge(av_evacuated, b.n)
                for t in range(TILES):
                    for j in range(4):
                        mm = nc.tensor.matmul(av_ps[32 * j:32 * j + 32, r], v_aug[:, b.par, t, s * HALF + r * 4 + j],
                                              probs[:, (2 * g + j // 2) % 4, j % 2, t], start=(s == 0 and t == 0),
                                              stop=(s == 1 and t == 1))
                mm.then_inc(quad_done, 1)

            def turn_max(b, half):
                rows = 3 * HALF * TILES
                wait_first(pe, max_split, (2 * b.n + half) * 4 + 4)
                nc.tensor.transpose(misc16[0:rows, 0:P], max_parts[:, half].rearrange("p r n -> p (r n)"), ident16[:])\
                  .then_inc(max_turned, 1)

            def step(u, c):
                new, now, late, last = (Batch(u, c, back) for back in range(4))
                for slot in range(HEADS):
                    if slot == 0 and new.exists():
                        pe.wait_ge(xt_in[new.par], 16 * (new.half + 1))
                        if last.exists():
                            pe.wait_ge(x1_made, 2 * last.n)
                        if late.exists():
                            pe.wait_ge(max_evacuated, 2 * late.n + 1)
                        elif now.exists():
                            pe.wait_ge(qk_evacuated, 2 * new.n)
                        else:
                            pe.wait_ge(bias_made, 1)
                        nc.tensor.matmul(misc_ps[:, 0:SEQ], wq[:], x_t[:, new.par], start=True, stop=True)
                        nc.tensor.matmul(misc_ps[:, SEQ:2 * SEQ], wk[:], x_t[:, new.par], start=True, stop=True)\
                          .then_inc(qk_projected, 1)
                    if slot == 1 and late.exists():
                        if new.exists():
                            pe.wait_ge(qk_evacuated, 2 * new.n + 2)
                        else:
                            pe.wait_ge(max_evacuated, 2 * late.n + 1)
                            if last.exists():
                                pe.wait_ge(x1_made, 2 * last.n)
                        turn_max(late, 1)
                    if slot == 2 and last.exists():
                        quad(last, 3)
                    if slot == 3 and now.exists():
                        if late.exists():
                            pe.wait_ge(max_evacuated, 2 * late.n + 2)
                        elif new.exists():
                            pe.wait_ge(qk_evacuated, 2 * new.n + 2)
                        for t in range(TILES):
                            mm = nc.tensor.matmul(misc_ps[:, t * D:(t + 1) * D], x_t[:, now.par, t * P:(t + 1) * P], wv[:],
                                                  start=True, stop=True)
                        mm.then_inc(v_projected, 1)
                    if slot == 5 and last.exists():
                        if now.exists():
                            pe.wait_ge(v_evacuated, 2 * now.n + 2)
                        elif late.exists():
                            pe.wait_ge(max_evacuated, 2 * late.n + 2)
                        else:
                            pe.wait_ge(x1_made, 2 * last.n)
                        pe.wait_ge(av_evacuated, last.n + 1)
                        for t in range(TILES):
                            for r in range(2):
                                mm = nc.tensor.transpose(misc_ps[:, (t * 2 + r) * P:(t * 2 + r + 1) * P],
                                                         av[:, r, t * P:(t + 1) * P], ident[:])
                        mm.then_inc(av_turned, 1)
                    if slot == 8 and last.exists():
                        pe.wait_ge(normalised, 3 * last.n + 3)
                        for t in range(TILES):
                            mm = nc.tensor.transpose(misc_ps[:, t * P:(t + 1) * P], heads_out[:, t], ident[:])
                        mm.then_inc(heads_turned, 1)
                    if slot == 10 and now.exists():
                        if last.exists():
                            pe.wait_ge(heads_evacuated, last.n + 1)
                        else:
                            pe.wait_ge(v_evacuated, 2 * now.n + 2)
                        turn_max(now, 0)
                    if slot == 12 and last.exists():
                        pe.wait_ge(heads_evacuated, last.n + 1)
                        if now.exists():
                            pe.wait_ge(max_evacuated, 2 * now.n + 1)
                        pe.wait_ge(xb_made, last.n + 1)
                        for t in range(TILES):
                            nc.tensor.matmul(misc_ps[:, t * D:(t + 1) * D], heads_t[:, t * P:(t + 1) * P], wo[:],
                                             start=True, stop=False)
                            mm = nc.tensor.matmul(misc_ps[:, t * D:(t + 1) * D], ident[:], xb[:, t], start=False, stop=True)
                        mm.then_inc(y_ready, 1)
                    if now.exists():
                        scores(now, slot)
                    if late.exists():
                        shifted_scores(late, slot)
                        if slot in (6, 10, 14):
                            quad(late, (slot - 6) // 4)

            pe.wait_ge(consts_made, 8)
            run_steps(pe, step)

EXPERTS = 8
HIDDEN = 512
CHUNKS = HIDDEN // P
BLOCK = 512
BLOCK_TILES = BLOCK // P
BLOCKS = TOKENS // BLOCK
ALL = EXPERTS + 1
TINY_STEPS = 8


def build_ffn(nc, a, ctx):
    def sb(name, shape, dt=F32):
        return ctx.enter_context(nc.sbuf_tensor(name, shape, dt))

    def ps(name, shape, dt=F32):
        return ctx.enter_context(nc.psum_tensor(name, shape, dt))

    def sem(name):
        return ctx.enter_context(nc.semaphore(name))

    w_fc = sb("w_fc", [D, ALL, HIDDEN])
    w_proj = sb("w_proj", [P, ALL, CHUNKS, D])
    b_fc = sb("b_fc", [P, ALL * CHUNKS])
    w_r = sb("w_r", [D, EXPERTS])
    b_proj = sb("b_proj", [EXPERTS, D])
    b_shared = sb("b_shared", [P, D])
    ident2 = sb("ident2", [P, P])
    index = sb("index", [P, EXPERTS], mybir.dt.int32)
    index_f = sb("index_f", [P, EXPERTS])
    half2 = sb("half2", [P, BLOCK_TILES])
    xr = sb("xr", [P, BLOCK_TILES, D])
    xs_t = sb("xs_t", [D, BLOCK])
    x_bias = sb("x_bias", [P, BLOCK_TILES, D])
    logits = sb("logits", [P, BLOCK_TILES, EXPERTS])
    best = sb("best", [P, BLOCK_TILES, 8])
    best_at = sb("best_at", [P, BLOCK_TILES, 8], mybir.dt.uint32)
    best_f = sb("best_f", [P, BLOCK_TILES, 2])
    delta = sb("delta", [P, BLOCK_TILES, 2])
    e_two = sb("e_two", [P, BLOCK_TILES, 2])
    e_sum = sb("e_sum", [P, BLOCK_TILES])
    e_inv = sb("e_inv", [P, BLOCK_TILES])
    g_two = sb("g_two", [P, BLOCK_TILES, 2])
    hot = sb("hot", [P, 2, BLOCK_TILES, EXPERTS])
    gate = sb("gate", [P, BLOCK_TILES, EXPERTS])
    gate_t = sb("gate_t", [EXPERTS, BLOCK])
    hid = sb("hid", [P, 2, CHUNKS, BLOCK])
    acc = sb("acc", [P, BLOCK_TILES, D])
    stats2 = sb("stats2", [P, BLOCK_TILES, 6])
    mv2 = sb("mv2", [P, BLOCK_TILES, 2])
    ve2 = sb("ve2", [P, BLOCK_TILES])
    rstd2 = sb("rstd2", [P, BLOCK_TILES])
    y_out = sb("y_out", [P, BLOCK_TILES, D])

    fc_ps = ps("fc_ps", [P, 4, 512])
    pr_ps = ps("pr_ps", [P, 2, BLOCK_TILES, D])
    turn_ps = ps("turn_ps", [P, 512])
    gate_ps = ps("gate_ps", [P, 512])

    w_in, x_in2, made, turned, evac = sem("w_in"), sem("x_in2"), sem("made"), sem("turned"), sem("evac")
    logit_ps, route, exped, gt_ps, gt_sb = sem("logit_ps"), sem("route"), sem("exped"), sem("gt_ps"), sem("gt_sb")
    bias_done, fc_done, gelu_done, proj_done, acc_done = sem("bias_done"), sem("fc_done"), sem("gelu_done"), sem("proj_done"), sem("acc_done")
    xb_done, pooled, written = sem("xb_done"), sem("pooled"), sem("written")
    ROUTE = 2 * BLOCK_TILES + 11
    ACC = ALL + 1 + 2 * BLOCK_TILES + BLOCK_TILES

    block = ctx.enter_context(nc.Block())

    @block.sync
    def _(sp):
        for to, of in ((w_fc[:], a["w_fc"]), (w_proj[:], a["w_proj"]), (b_fc[:], a["b_fc"]), (w_r[:], a["w_r"]), (b_proj[:], a["b_proj"]),
                       (b_shared[:], a["b_shared"].partition_broadcast(P))):
            sp.dma_start(to, of).then_inc(w_in, 16)
        def one(b, first):
            if not first:
                sp.wait_ge(xb_done, b)
            sp.dma_start(xr[:], a["x1_rows"][bass.ds(b * BLOCK, BLOCK), :].rearrange("(t p) d -> p t d", p=P)).then_inc(x_in2, 16)
            sp.wait_ge(acc_done, ACC * b + ACC)
            sp.dma_start(a["out"][bass.ds(b * BLOCK, BLOCK), :].rearrange("(t p) d -> p t d", p=P), y_out[:]).then_inc(written, 16)
        one(0, True)
        with sp.Fori(1, BLOCKS) as b:
            one(b, False)
        sp.wait_ge(written, 16 * BLOCKS)

    @block.gpsimd
    def _(pool):
        nc.gpsimd.memset(ident2[:], 0.0).then_inc(made, 1)
        nc.gpsimd.iota(index[:], pattern=[[1, EXPERTS]], base=0, channel_multiplier=0).then_inc(made, 1)
        nc.gpsimd.memset(half2[:], -0.5).then_inc(made, 1)
        pool.wait_ge(made, 3)
        nc.gpsimd.affine_select(out=ident2[:], in_=ident2[:], compare_op=ALU.not_equal, fill=1.0, base=0,
                                pattern=[[-1, P]], channel_multiplier=1).then_inc(made, 1)
        nc.gpsimd.tensor_copy(index_f[:], index[:]).then_inc(made, 1)
        pool.wait_ge(w_in, 96)
        def one(b, first):
            pool.wait_ge(x_in2, 16 * b + 16)
            if not first:
                pool.wait_ge(acc_done, ACC * b)
            pool.wait_ge(turned, b + 1)
            nc.gpsimd.tensor_tensor(x_bias[:], xr[:], b_shared[:].unsqueeze(1).to_broadcast([P, BLOCK_TILES, D]), ALU.add).then_inc(xb_done, 1)
            wait_first(pool, acc_done, ACC * b + ALL + 1 + 2 * BLOCK_TILES)
            nc.gpsimd.tensor_scalar(ve2[:], mv2[:, :, 1], EPS, None, ALU.add).then_inc(pooled, 1)
            pool.wait_ge(pooled, 2 * b + 1)
            nc.gpsimd.tensor_tensor(rstd2[:], ve2[:], half2[:], ALU.pow).then_inc(pooled, 1)
        one(0, True)
        with pool.Fori(1, BLOCKS) as b:
            one(b, False)

    @block.vector
    def _(dve):
        dve.wait_ge(made, 5)
        dve.wait_ge(w_in, 96)
        def one(b, first):
            n = [0]
            def link(ins):
                n[0] += 1
                ins.then_inc(route, 1)
                wait_first(dve, route, ROUTE * b + n[0])
            dve.wait_ge(turned, b + 1)
            if not first:
                dve.wait_ge(logit_ps, b)
            nc.vector.tensor_copy(xs_t[:], turn_ps[:]).then_inc(evac, 1)
            dve.wait_ge(logit_ps, b + 1)
            link(nc.vector.tensor_copy(logits[:], gate_ps[:, 0:BLOCK_TILES * EXPERTS].rearrange("p (t e) -> p t e", e=EXPERTS)))
            for t in range(BLOCK_TILES):
                link(nc.vector.max(best[:, t], logits[:, t]))
                link(nc.vector.max_index(best_at[:, t], best[:, t], logits[:, t]))
            link(nc.vector.tensor_copy(best_f[:], best_at[:, :, 0:2]))
            link(nc.vector.tensor_tensor(delta[:], best[:, :, 0:2], best[:, :, 0:1].to_broadcast([P, BLOCK_TILES, 2]), ALU.subtract))
            dve.wait_ge(exped, b + 1)
            link(nc.vector.tensor_reduce(e_sum[:], e_two[:], AX_X, ALU.add))
            link(nc.vector.reciprocal(e_inv[:], e_sum[:]))
            link(nc.vector.tensor_tensor(g_two[:], e_two[:], e_inv[:].unsqueeze(2).to_broadcast([P, BLOCK_TILES, 2]), ALU.mult))
            for k in range(2):
                link(nc.vector.tensor_tensor(hot[:, k], index_f[:].unsqueeze(1).to_broadcast([P, BLOCK_TILES, EXPERTS]),
                                             best_f[:, :, k:k + 1].to_broadcast([P, BLOCK_TILES, EXPERTS]), ALU.is_equal))
                link(nc.vector.tensor_tensor(hot[:, k], hot[:, k], g_two[:, :, k:k + 1].to_broadcast([P, BLOCK_TILES, EXPERTS]), ALU.mult))
            link(nc.vector.tensor_tensor(gate[:], hot[:, 0], hot[:, 1], ALU.add))
            assert n[0] == ROUTE, n[0]
            dve.wait_ge(gt_ps, b + 1)
            nc.vector.tensor_copy(gate_t[:], gate_ps[0:EXPERTS, :]).then_inc(gt_sb, 1)
            dve.wait_ge(bias_done, b + 1)
            dve.wait_ge(xb_done, b + 1)
            base = ACC * b
            nc.vector.tensor_tensor(acc[:], turn_ps[:].rearrange("p (t d) -> p t d", d=D), x_bias[:], ALU.add).then_inc(acc_done, 1)
            dve.wait_ge(acc_done, base + 1)
            for e in range(ALL):
                dve.wait_ge(proj_done, ALL * b + e + 1)
                if e == 0:
                    nc.vector.tensor_tensor(acc[:], pr_ps[:, e % 2], acc[:], ALU.add).then_inc(acc_done, 1)
                else:
                    for t in range(BLOCK_TILES):
                        r = nc.vector.scalar_tensor_tensor(out=acc[:, t], in0=pr_ps[:, e % 2, t], scalar=gate[:, t, e - 1:e],
                                                           in1=acc[:, t], op0=ALU.mult, op1=ALU.add)
                    r.then_inc(acc_done, 1)
                dve.wait_ge(acc_done, base + 2 + e)
            for t in range(BLOCK_TILES):
                nc.vector.bn_stats(stats2[:, t], acc[:, t]).then_inc(acc_done, 1)
            wait_first(dve, acc_done, base + ALL + 1 + BLOCK_TILES)
            for t in range(BLOCK_TILES):
                nc.vector.bn_aggr(mv2[:, t], stats2[:, t]).then_inc(acc_done, 1)
            dve.wait_ge(pooled, 2 * b + 2)
            if not first:
                dve.wait_ge(written, 16 * b)
            for t in range(BLOCK_TILES):
                nc.vector.tensor_scalar(y_out[:, t], acc[:, t], mv2[:, t, 0:1], rstd2[:, t:t + 1], ALU.subtract, ALU.mult).then_inc(acc_done, 1)
        one(0, True)
        with dve.Fori(1, BLOCKS) as b:
            one(b, False)

    @block.scalar
    def _(act):
        act.wait_ge(w_in, 96)
        def one(b, first):
            act.wait_ge(route, ROUTE * b + 2 * BLOCK_TILES + 3)
            nc.scalar.activation(e_two[:], delta[:], ACT.Exp).then_inc(exped, 1)
            for e in range(ALL):
                for c in range(CHUNKS):
                    k = e * CHUNKS + c
                    act.wait_ge(fc_done, ALL * CHUNKS * b + k + 1)
                    if not first or e >= 2:
                        act.wait_ge(proj_done, ALL * b + e - 1)
                    nc.scalar.activation(hid[:, e % 2, c], fc_ps[:, k % 4], ACT.Gelu_apprx_tanh, bias=b_fc[:, k:k + 1]).then_inc(gelu_done, 1)
        one(0, True)
        with act.Fori(1, BLOCKS) as b:
            one(b, False)

    @block.tensor
    def _(pe):
        pe.wait_ge(made, 5)
        pe.wait_ge(w_in, 96)
        def one(b, first):
            pe.wait_ge(x_in2, 16 * b + 16)
            if not first:
                pe.wait_ge(acc_done, ACC * b - ACC + 1)
                pe.wait_ge(gt_sb, b)
            for t in range(BLOCK_TILES):
                mm = nc.tensor.transpose(turn_ps[:, t * P:(t + 1) * P], xr[:, t], ident2[:])
            mm.then_inc(turned, 1)
            pe.wait_ge(evac, b + 1)
            for t in range(BLOCK_TILES):
                mm = nc.tensor.matmul(gate_ps[:, t * EXPERTS:(t + 1) * EXPERTS], xs_t[:, t * P:(t + 1) * P], w_r[:], start=True, stop=True)
            mm.then_inc(logit_ps, 1)
            def fc(e):
                for c in range(CHUNKS):
                    k = e * CHUNKS + c
                    if not first or k >= 4:
                        pe.wait_ge(gelu_done, ALL * CHUNKS * b + k - 3)
                    nc.tensor.matmul(fc_ps[:, k % 4], w_fc[:, e, c * P:(c + 1) * P], xs_t[:], start=True, stop=True).then_inc(fc_done, 1)
            def proj(e):
                pe.wait_ge(gelu_done, ALL * CHUNKS * b + CHUNKS * (e + 1))
                if not first or e >= 2:
                    pe.wait_ge(acc_done, ACC * b + e) if e >= 2 else pe.wait_ge(acc_done, ACC * b)
                for t in range(BLOCK_TILES):
                    for c in range(CHUNKS):
                        mm = nc.tensor.matmul(pr_ps[:, e % 2, t], hid[:, e % 2, c, t * P:(t + 1) * P], w_proj[:, e, c],
                                              start=(c == 0), stop=(c == CHUNKS - 1))
                mm.then_inc(proj_done, 1)
            fc(0)
            pe.wait_ge(route, ROUTE * b + ROUTE)
            for t in range(BLOCK_TILES):
                mm = nc.tensor.transpose(gate_ps[0:EXPERTS, t * P:(t + 1) * P], gate[:, t], ident2[:])
            mm.then_inc(gt_ps, 1)
            pe.wait_ge(gt_sb, b + 1)
            for t in range(BLOCK_TILES):
                mm = nc.tensor.matmul(turn_ps[:, t * D:(t + 1) * D], gate_t[:, t * P:(t + 1) * P], b_proj[:], start=True, stop=True)
            mm.then_inc(bias_done, 1)
            for e in range(1, ALL):
                fc(e)
                proj(e - 1)
            proj(ALL - 1)
        one(0, True)
        with pe.Fori(1, BLOCKS) as b:
            one(b, False)


def build_program(nc, a):
    a["x1_rows"] = nc.dram_tensor("x1_rows", [TOKENS, D], F32, kind="Internal").ap()
    with ExitStack() as ctx:
        PASSED[0] = ctx.enter_context(nc.semaphore("passed"))
        build_attention(nc, a)
        build_ffn(nc, a, ctx)


def kernel(L0_attn_x, L0_attn_Wq, L0_attn_bq, L0_attn_Wk, L0_attn_bk, L0_attn_Wv, L0_attn_bv, L0_attn_Wo, L0_attn_bo,
           L0_attn_head_mask, L0_ffn_Wfc_s, L0_ffn_bfc_s, L0_ffn_Wproj_s, L0_ffn_bproj_s, L0_ffn_Wr, L0_ffn_Wfc,
           L0_ffn_bfc, L0_ffn_Wproj, L0_ffn_bproj):
    import numpy as np
    import concourse.bacc as bacc
    from concourse.bass_utils import run_bass_kernel_spmd

    def by_dim(w):
        return np.asarray(w).reshape(HEADS, DH, -1).transpose(1, 0, 2).reshape(D, -1)

    def by_quad(w):
        return np.asarray(w).reshape(2, 2, 4, DH, -1).transpose(1, 0, 2, 3, 4).reshape(D, -1)

    def by_column_tile(w):
        w = np.asarray(w)
        n = w.shape[0] // HEADS
        return w.reshape(2, 2, 4, n, -1).transpose(0, 2, 1, 3, 4).reshape(w.shape[0], -1)

    x = np.asarray(L0_attn_x).reshape(TOKENS, D)
    w_fc = np.concatenate([np.asarray(L0_ffn_Wfc_s)[None], np.asarray(L0_ffn_Wfc)])
    b_fc = np.concatenate([np.asarray(L0_ffn_bfc_s)[None], np.asarray(L0_ffn_bfc)])
    w_proj = np.concatenate([np.asarray(L0_ffn_Wproj_s)[None], np.asarray(L0_ffn_Wproj)])
    arrays = {
        "x": x,
        "x_t": x.T,
        "wq_t": by_dim(L0_attn_Wq).T,
        "wk_t": by_dim(L0_attn_Wk).T,
        "wv_t": by_quad(L0_attn_Wv).T,
        "wo_t": by_column_tile(np.asarray(L0_attn_Wo).T),
        "bq": by_dim(L0_attn_bq),
        "bk": by_dim(L0_attn_bk),
        "bv": by_column_tile(L0_attn_bv),
        "mask": by_column_tile(L0_attn_head_mask).reshape(HEADS),
        "bo": np.asarray(L0_attn_bo),
        "w_fc": w_fc.transpose(1, 0, 2),
        "b_fc": b_fc.reshape(ALL * CHUNKS, P).T,
        "w_proj": w_proj.reshape(ALL, CHUNKS, P, D).transpose(2, 0, 1, 3),
        "w_r": np.asarray(L0_ffn_Wr),
        "b_proj": np.asarray(L0_ffn_bproj),
        "b_shared": np.asarray(L0_ffn_bproj_s),
    }
    nc = bacc.Bacc("TRN2", target_bir_lowering=False, num_devices=1)
    maps, a = {}, {}
    for name, array in arrays.items():
        maps[f"in_{name}"] = np.ascontiguousarray(array)
        a[name] = nc.dram_tensor(f"in_{name}", maps[f"in_{name}"].shape, F32, kind="ExternalInput").ap()
    a["out"] = nc.dram_tensor("result", [TOKENS, D], F32, kind="ExternalOutput").ap()
    build_program(nc, a)
    r = run_bass_kernel_spmd(nc, [maps], core_ids=[0])
    return r.results[0]["result"].reshape(BATCHES, SEQ, D)
```

```python
from contextlib import ExitStack

import concourse.bass as bass
from concourse import mybir

F32 = mybir.dt.float32
BF16 = mybir.dt.bfloat16
ACT = mybir.ActivationFunctionType
ALU = mybir.AluOpType
AX_X = mybir.AxisListType.X

P = 128
D = 128
HEADS = 16
DH = D // HEADS
BATCHES = 16
SEQ = 256
TOKENS = BATCHES * SEQ
TILES = SEQ // P
HALF = HEADS // 2
PAIRS = HEADS // 2
QUADS = HEADS // 4
EPS = 1e-5
SCORE_SCALE = float(DH) ** -0.5
ROW_MAX = 6 * DH
FIRST_LOOP, LOOPS = 2, 5


PASSED = [None]


class Batch:

    def __init__(self, u, c, back):
        self.half = u + (c - back) // 2
        self.par = (c - back) % 2
        self.n = self.half * 2 + self.par
        self.fixed = isinstance(u, int)

    def exists(self):
        return not self.fixed or 0 <= self.n < BATCHES

    def since(self, n):
        return not self.fixed or self.n >= n


def wait_first(eng, semaphore, value):
    eng.wait_ge(semaphore, value)
    if not isinstance(value, int):
        eng.sem_inc(PASSED[0], 1)


def run_steps(eng, step):
    for t in range(2 * FIRST_LOOP):
        step(t // 2, t % 2)
    with eng.Fori(FIRST_LOOP, FIRST_LOOP + LOOPS) as u:
        step(u, 0)
        step(u, 1)
    for t in range(2 * (FIRST_LOOP + LOOPS), BATCHES + 3):
        step(t // 2, t % 2)


def build_attention(nc, a):
    ctx = ExitStack()
    with ctx:
        def sb(name, shape, dt=F32):
            return ctx.enter_context(nc.sbuf_tensor(name, shape, dt))

        def ps(name, shape, dt=F32):
            return ctx.enter_context(nc.psum_tensor(name, shape, dt))

        def sem(name):
            return ctx.enter_context(nc.semaphore(name))

        q_rows = nc.dram_tensor("q_rows", [2, ROW_MAX + 3, HEADS, SEQ], BF16, kind="Internal").ap()
        k_rows = nc.dram_tensor("k_rows", [2, ROW_MAX, HEADS, SEQ], BF16, kind="Internal").ap()

        wq = sb("wq", [D, D])
        wk = sb("wk", [D, D])
        wv = sb("wv", [D, D])
        wo = sb("wo", [D, D])
        bq = sb("bq", [D, 1])
        bk = sb("bk", [D, 1])
        bv = sb("bv", [D, 1])
        mask_col = sb("mask_col", [D, 1])
        mask_row = sb("mask_row", [P, HEADS])
        bo_row = sb("bo_row", [P, D])
        bv_masked = sb("bv_masked", [D, P])
        out_bias = sb("out_bias", [P, D])
        ident = sb("ident", [P, P])
        ident16 = sb("ident16", [P, P], BF16)
        zero_rows = sb("zero_rows", [3, SEQ], BF16)
        one_rows = sb("one_rows", [3, SEQ], BF16)
        minus_half = sb("minus_half", [P, TILES])

        x_t = sb("x_t", [D, 2, SEQ])
        x_in = sb("x_in", [P, 2, TILES, D])
        xb = sb("xb", [P, TILES, D])
        z = sb("z", [P, TILES, D])
        qk = sb("qk", [D, 2, SEQ])
        qk_rest = sb("qk_rest", [D, 2, SEQ])
        qk_parts = sb("qk_parts", [D, 2, 2, 3, SEQ], BF16)
        q_stack = sb("q_stack", [P, 2, HEADS, SEQ], BF16)
        k_stack = sb("k_stack", [P, 2, HEADS, SEQ], BF16)
        v_aug = sb("v_aug", [P, 2, TILES, HEADS, 32])
        row_max = sb("row_max", [P, HEADS, TILES])
        max_rest = sb("max_rest", [P, 2, HALF * TILES])
        max_parts = sb("max_parts", [P, 2, 3, HALF * TILES], BF16)
        max_t = sb("max_t", [3 * HALF * TILES, 2, P], BF16)
        probs = sb("probs", [P, 4, 2, TILES, SEQ])
        av = sb("av", [P, 2, SEQ])
        sum_inv = sb("sum_inv", [P, 2 * HEADS])
        sum_scale = sb("sum_scale", [P, 2 * HEADS])
        heads_out = sb("heads_out", [P, TILES, D])
        heads_t = sb("heads_t", [D, SEQ])
        stats = sb("stats", [P, TILES, 6])
        mean_var = sb("mean_var", [P, TILES, 2])
        var_eps = sb("var_eps", [P, TILES])
        rstd = sb("rstd", [P, TILES])
        scaled_mean = sb("scaled_mean", [P, TILES])
        shift = sb("shift", [P, TILES])
        x1_all = a["x1_all"]

        s1_ps = ps("s1_ps", [P, 2, TILES, SEQ])
        st_ps = ps("st_ps", [P, 2, 2, TILES, SEQ])
        av_ps = ps("av_ps", [P, 2, SEQ])
        misc_ps = ps("misc_ps", [P, 512])
        misc16 = misc_ps[:].bitcast(BF16)

        weights_in = sem("weights_in")
        bcast_in = sem("bcast_in")
        consts_made = sem("consts_made")
        k_cleared = sem("k_cleared")
        zeros_out = sem("zeros_out")
        bv_made = sem("bv_made")
        bias_ps = sem("bias_ps")
        bias_made = sem("bias_made")
        xt_in = [sem("xt_in0"), sem("xt_in1")]
        x_loaded = [sem("x_loaded0"), sem("x_loaded1")]
        qk_projected = sem("qk_projected")
        qk_evacuated = sem("qk_evacuated")
        qk_split = sem("qk_split")
        rows_out = [sem("rows_out0"), sem("rows_out1")]
        stacks_in = [[sem(f"stacks_in{par}{half}") for half in range(2)] for par in range(2)]
        scores_ready = sem("scores_ready")
        max_done = sem("max_done")
        max_split = sem("max_split")
        max_turned = sem("max_turned")
        max_evacuated = sem("max_evacuated")
        max_in = [sem("max_in0"), sem("max_in1")]
        shifted_ready = sem("shifted_ready")
        exp_done = sem("exp_done")
        v_projected = sem("v_projected")
        v_evacuated = sem("v_evacuated")
        quad_done = sem("quad_done")
        av_evacuated = sem("av_evacuated")
        av_turned = sem("av_turned")
        normalised = sem("normalised")
        heads_turned = sem("heads_turned")
        heads_evacuated = sem("heads_evacuated")
        xb_made = sem("xb_made")
        y_ready = sem("y_ready")
        z_made = sem("z_made")
        stats_done = sem("stats_done")
        scale_done = sem("scale_done")
        x1_made = sem("x1_made")

        block = ctx.enter_context(nc.Block())

        @block.sync
        def _(sp):
            for tile, name in ((wq, "wq_t"), (wk, "wk_t"), (bq, "bq"), (bk, "bk"), (wv, "wv_t"), (wo, "wo_t"),
                               (bv, "bv")):
                sp.dma_start(tile[:], a[name]).then_inc(weights_in, 16)
            sp.dma_start(mask_col[:], a["mask"].unsqueeze(1).to_broadcast([HEADS, DH])).then_inc(weights_in, 16)

            def load_xt(b):
                sp.dma_start(x_t[:, b.par], a["x_t"][:, bass.ds(b.n * SEQ, SEQ)]).then_inc(xt_in[b.par], 16)

            load_xt(Batch(0, 0, 0))
            sp.dma_start(mask_row[:], a["mask"].partition_broadcast(P)).then_inc(bcast_in, 16)
            sp.dma_start(bo_row[:], a["bo"].partition_broadcast(P)).then_inc(bcast_in, 16)
            sp.wait_ge(consts_made, 4)
            sp.wait_ge(k_cleared, 1)
            for par in range(2):
                sp.dma_start(q_rows[par, ROW_MAX:ROW_MAX + 3], zero_rows[:].unsqueeze(1).to_broadcast([3, HEADS, SEQ])).then_inc(zeros_out, 16)
                sp.dma_start(k_stack[ROW_MAX:ROW_MAX + 3, par], one_rows[:].unsqueeze(1).to_broadcast([3, HEADS, SEQ])).then_inc(zeros_out, 16)
            sp.wait_ge(zeros_out, 64)

            def load_max(b, half):
                sp.wait_ge(max_evacuated, 2 * b.n + half + 1)
                for part in range(3):
                    rows = HALF * TILES
                    sp.dma_start(q_stack[ROW_MAX + part:ROW_MAX + part + 1, b.par, half * HALF:(half + 1) * HALF, :]
                                 .rearrange("o h (t q) -> o (h t) q", t=TILES),
                                 max_t[part * rows:(part + 1) * rows, half, :]).then_inc(max_in[half], 16)

            def load_stacks(b, half):
                heads = slice(half * HALF, (half + 1) * HALF)
                if b.since(2):
                    sp.wait_ge(shifted_ready, PAIRS * (b.n - 2) + (half + 1) * PAIRS // 2)
                sp.dma_start(q_stack[0:ROW_MAX + 3, b.par, heads], q_rows[b.par, :, heads]).then_inc(stacks_in[b.par][half], 16)
                sp.dma_start(k_stack[0:ROW_MAX, b.par, heads], k_rows[b.par, :, heads]).then_inc(stacks_in[b.par][half], 16)

            def step(u, c):
                b = Batch(u, c, 2)
                if b.exists():
                    load_max(b, 1)
                b = Batch(u, c, -1)
                if b.exists():
                    if b.since(2):
                        sp.wait_ge(v_projected, b.n - 1)
                    load_xt(b)
                b = Batch(u, c, 2)
                if b.exists():
                    if b.since(2):
                        sp.wait_ge(xb_made, b.n - 1)
                    sp.dma_start(x_in[:, b.par], a["x"][bass.ds(b.n * SEQ, SEQ), :].rearrange("(t p) d -> p t d", p=P))\
                      .then_inc(x_loaded[b.par], 16)
                b = Batch(u, c, 0)
                if b.exists():
                    q_to = q_rows[b.par, 0:ROW_MAX].rearrange("(r d) h t -> (d h) r t", r=6)
                    k_to = k_rows[b.par].rearrange("(r d) h t -> (d h) r t", r=6)
                    q_part, k_part = qk_parts[:, b.par, 0], qk_parts[:, b.par, 1]
                    if b.since(2):
                        for half in range(2):
                            sp.wait_ge(stacks_in[b.par][half], 32 * b.half)
                    sp.wait_ge(qk_split, 4 * b.n + 1)
                    for r in range(3):
                        sp.dma_start(k_to[:, r:r + 1], k_part[:, 0:1]).then_inc(rows_out[b.par], 16)
                    sp.wait_ge(qk_split, 4 * b.n + 3)
                    for r in range(3, 5):
                        sp.dma_start(k_to[:, r:r + 1], k_part[:, 1:2]).then_inc(rows_out[b.par], 16)
                    sp.wait_ge(qk_split, 4 * b.n + 4)
                    sp.dma_start(q_to[:, 0:3], q_part[:, 0:3]).then_inc(rows_out[b.par], 16)
                    sp.dma_start(q_to[:, 3:5], q_part[:, 0:2]).then_inc(rows_out[b.par], 16)
                    sp.dma_start(q_to[:, 5:6], q_part[:, 0:1]).then_inc(rows_out[b.par], 16)
                    sp.dma_start(k_to[:, 5:6], k_part[:, 2:3]).then_inc(rows_out[b.par], 16)
                    sp.wait_ge(rows_out[b.par], 144 * (b.half + 1))
                    load_stacks(b, 0)
                b = Batch(u, c, 1)
                if b.exists():
                    load_max(b, 0)
                b = Batch(u, c, 0)
                if b.exists():
                    load_stacks(b, 1)
                load_for_moe(sp, a, u, c)

            run_steps(sp, step)

        @block.gpsimd
        def _(pool):
            make_empty_row(nc, pool, a)
            nc.gpsimd.memset(zero_rows[:], 0.0).then_inc(consts_made, 1)
            nc.gpsimd.memset(one_rows[:], 1.0).then_inc(consts_made, 1)
            nc.gpsimd.memset(ident[:], 0.0).then_inc(consts_made, 1)
            nc.gpsimd.memset(q_stack[:].rearrange("p b h t -> p (b h t)").bitcast(F32), 0.0).then_inc(consts_made, 1)
            nc.gpsimd.memset(minus_half[:], -0.5).then_inc(consts_made, 1)
            pool.wait_ge(consts_made, 5)
            nc.gpsimd.affine_select(out=ident[:], in_=ident[:], compare_op=ALU.not_equal, fill=1.0, base=0,
                                    pattern=[[-1, P]], channel_multiplier=1).then_inc(consts_made, 1)
            pool.wait_ge(consts_made, 6)
            nc.gpsimd.tensor_copy(ident16[:], ident[:]).then_inc(consts_made, 1)

            def split_max(b, half):
                heads = slice(half * HALF, (half + 1) * HALF)
                largest = row_max[:, heads].rearrange("p h t -> p (h t)")
                rest, parts = max_rest[:, half], max_parts[:, half]
                done = (2 * b.n + half) * 4
                wait_first(pool, max_done, HEADS * b.n + (half + 1) * HALF)
                if b.since(1):
                    wait_first(pool, max_turned, 2 * b.n + half - 1)
                nc.gpsimd.tensor_scalar(parts[:, 0], largest, 1.0, 1.0, ALU.mult, ALU.mult).then_inc(max_split, 1)
                pool.wait_ge(max_split, done + 1)
                nc.gpsimd.tensor_tensor(rest, largest, parts[:, 0], ALU.subtract).then_inc(max_split, 1)
                wait_first(pool, max_split, done + 2)
                nc.gpsimd.tensor_scalar(parts[:, 1], rest, 1.0, 1.0, ALU.mult, ALU.mult).then_inc(max_split, 1)
                pool.wait_ge(max_split, done + 3)
                nc.gpsimd.tensor_tensor(parts[:, 2], rest, parts[:, 1], ALU.subtract).then_inc(max_split, 1)

            def split_qk(b):
                parts = qk_parts[:, b.par]
                wait_first(pool, qk_evacuated, 2 * b.n + 2)
                if b.since(2):
                    wait_first(pool, rows_out[b.par], 144 * b.half)
                nc.gpsimd.tensor_scalar(parts[:, :, 0], qk[:], 1.0, 1.0, ALU.mult, ALU.mult).then_inc(qk_split, 1)
                pool.wait_ge(qk_split, 4 * b.n + 1)
                nc.gpsimd.tensor_tensor(qk_rest[:], qk[:], parts[:, :, 0], ALU.subtract).then_inc(qk_split, 1)
                wait_first(pool, qk_split, 4 * b.n + 2)
                nc.gpsimd.tensor_scalar(parts[:, :, 1], qk_rest[:], 1.0, 1.0, ALU.mult, ALU.mult).then_inc(qk_split, 1)
                pool.wait_ge(qk_split, 4 * b.n + 3)
                nc.gpsimd.tensor_tensor(parts[:, :, 2], qk_rest[:], parts[:, :, 1], ALU.subtract).then_inc(qk_split, 1)

            def step(u, c):
                b = Batch(u, c, 2)
                if b.exists():
                    split_max(b, 1)
                b = Batch(u, c, 0)
                if b.exists():
                    split_qk(b)
                b = Batch(u, c, 3)
                if b.exists():
                    pool.wait_ge(x_loaded[b.par], 16 * (b.half + 1))
                    if b.since(1):
                        pool.wait_ge(z_made, b.n)
                    else:
                        pool.wait_ge(bias_made, 1)
                    nc.gpsimd.tensor_tensor(xb[:], x_in[:, b.par], out_bias[:].unsqueeze(1).to_broadcast([P, TILES, D]),
                                            ALU.add).then_inc(xb_made, 1)
                b = Batch(u, c, 1)
                if b.exists():
                    split_max(b, 0)
                b = Batch(u, c, 3)
                if b.exists():
                    wait_first(pool, stats_done, 4 * b.n + 4)
                    if b.since(1):
                        wait_first(pool, x1_made, 2 * b.n)
                    nc.gpsimd.tensor_scalar(var_eps[:], mean_var[:, :, 1], EPS, None, ALU.add).then_inc(scale_done, 1)
                    pool.wait_ge(scale_done, 4 * b.n + 1)
                    nc.gpsimd.tensor_tensor(rstd[:], var_eps[:], minus_half[:], ALU.pow).then_inc(scale_done, 1)
                    pool.wait_ge(scale_done, 4 * b.n + 2)
                    nc.gpsimd.tensor_tensor(scaled_mean[:], mean_var[:, :, 0], rstd[:], ALU.mult).then_inc(scale_done, 1)
                    wait_first(pool, scale_done, 4 * b.n + 3)
                    nc.gpsimd.tensor_scalar(shift[:], scaled_mean[:], -1.0, 1.0, ALU.mult, ALU.mult).then_inc(scale_done, 1)

            run_steps(pool, step)

        @block.scalar
        def _(act):
            def exp_pair(b, p):
                act.wait_ge(shifted_ready, PAIRS * b.n + p + 1)
                if b.since(1) or p >= 4:
                    act.wait_ge(quad_done, 4 * b.n + p // 2 - 1)
                nc.scalar.activation(probs[:, p % 4], st_ps[:, p % 2], ACT.Exp, scale=SCORE_SCALE).then_inc(exp_done, 1)

            def evacuate_max(b, half):
                rows = 3 * HALF * TILES
                act.wait_ge(max_turned, 2 * b.n + half + 1)
                if b.since(1):
                    act.wait_ge(max_in[half], 48 * b.n)
                nc.scalar.activation(max_t[:, half], misc16[0:rows, 0:P], ACT.Copy).then_inc(max_evacuated, 1)

            def step(u, c):
                b = Batch(u, c, 0)
                if b.exists():
                    act.wait_ge(qk_projected, b.n + 1)
                    if b.since(1):
                        act.wait_ge(qk_split, 4 * b.n)
                    for side, bias in ((0, bq), (1, bk)):
                        nc.scalar.activation(qk[:, side], misc_ps[:, side * SEQ:(side + 1) * SEQ], ACT.Identity,
                                             bias=bias[:]).then_inc(qk_evacuated, 1)
                now, last = Batch(u, c, 2), Batch(u, c, 3)
                if now.exists():
                    exp_pair(now, 0)
                    evacuate_max(now, 1)
                if last.exists():
                    act.wait_ge(quad_done, 4 * last.n + 4)
                    if last.since(1):
                        act.wait_ge(av_turned, last.n)
                    nc.scalar.activation(av[:], av_ps[:], ACT.Copy).then_inc(av_evacuated, 1)
                b = Batch(u, c, 1)
                if b.exists():
                    act.wait_ge(v_projected, b.n + 1)
                    if b.since(2):
                        act.wait_ge(quad_done, 4 * (b.n - 1))
                    for s in range(2):
                        to = v_aug[:, b.par, :, s * HALF:(s + 1) * HALF, 16 * s:16 * s + DH]
                        of = misc_ps[:, 0:SEQ].rearrange("p (t s h d) -> p t s h d", t=TILES, s=2, d=DH)[:, :, s]
                        nc.scalar.activation(to, of, ACT.Copy).then_inc(v_evacuated, 1)
                if now.exists():
                    exp_pair(now, 1)
                    exp_pair(now, 2)
                if last.exists():
                    act.wait_ge(heads_turned, last.n + 1)
                    if last.since(1):
                        act.wait_ge(y_ready, last.n)
                    nc.scalar.activation(heads_t[:], misc_ps[:, 0:SEQ], ACT.Copy).then_inc(heads_evacuated, 1)
                if now.exists():
                    exp_pair(now, 3)
                    exp_pair(now, 4)
                if b.exists():
                    evacuate_max(b, 0)
                if now.exists():
                    exp_pair(now, 5)
                    exp_pair(now, 6)
                if now.exists():
                    exp_pair(now, 7)
                if last.exists():
                    act.wait_ge(scale_done, 4 * last.n + 4)
                    for t in range(TILES):
                        tile = last.n * TILES + t
                        to = x1_all[:, tile] if last.fixed else x1_all[:, bass.ds(tile, 1)].rearrange("p o d -> p (o d)")
                        nc.scalar.activation(to, z[:, t], ACT.Identity,
                                             scale=rstd[:, t:t + 1], bias=shift[:, t:t + 1]).then_inc(x1_made, 1)

            act.wait_ge(weights_in, 128)
            run_steps(act, step)

        @block.vector
        def _(dve):
            nc.vector.memset(k_stack[:].rearrange("p b h t -> p (b h t)").bitcast(F32), 0.0).then_inc(k_cleared, 1)
            nc.vector.memset(v_aug[:], 0.0).then_inc(bv_made, 1)
            dve.wait_ge(bv_made, 1)
            for s in range(2):
                nc.vector.memset(v_aug[:, :, :, s * HALF:(s + 1) * HALF, 16 * s + DH:16 * s + DH + 1], 1.0).then_inc(bv_made, 1)
            dve.wait_ge(weights_in, 128)
            nc.vector.tensor_tensor(bv_masked[:], bv[:].to_broadcast([D, P]), mask_col[:].to_broadcast([D, P]), ALU.mult)\
              .then_inc(bv_made, 1)
            dve.wait_ge(bias_ps, 1)
            dve.wait_ge(bcast_in, 32)
            nc.vector.tensor_tensor(out_bias[:], misc_ps[:, 0:D], bo_row[:], ALU.add).then_inc(bias_made, 1)

            def maxima(b, heads):
                for h in heads:
                    dve.wait_ge(scores_ready, HEADS * b.n + h + 1)
                    if h % HALF == 0 and b.since(1):
                        dve.wait_ge(max_split, (2 * b.n + h // HALF - 1) * 4)
                    nc.vector.tensor_reduce(row_max[:, h], s1_ps[:, h % 2], AX_X, ALU.max, negate=True).then_inc(max_done, 1)

            def step(u, c):
                now, last = Batch(u, c, 1), Batch(u, c, 3)
                if now.exists():
                    maxima(now, range(5))
                if last.exists():
                    blocks = misc_ps[:].rearrange("p (n r) -> p n r", r=16)
                    dve.wait_ge(av_turned, last.n + 1)
                    if last.since(1):
                        dve.wait_ge(heads_turned, last.n)
                    nc.vector.reciprocal(sum_inv[:].unsqueeze(2), blocks[:, :, DH:DH + 1]).then_inc(normalised, 1)
                    dve.wait_ge(normalised, 3 * last.n + 1)
                    nc.vector.tensor_tensor(sum_scale[:].rearrange("p (t h) -> p t h", t=TILES),
                                            sum_inv[:].rearrange("p (t h) -> p t h", t=TILES),
                                            mask_row[:].unsqueeze(1).to_broadcast([P, TILES, HEADS]), ALU.mult)\
                      .then_inc(normalised, 1)
                    dve.wait_ge(normalised, 3 * last.n + 2)
                    nc.vector.tensor_tensor(heads_out[:].rearrange("p t (h d) -> p (t h) d", d=DH), blocks[:, :, 0:DH],
                                            sum_scale[:].unsqueeze(2).to_broadcast([P, 2 * HEADS, DH]), ALU.mult)\
                      .then_inc(normalised, 1)
                if now.exists():
                    maxima(now, range(5, 13))
                if last.exists():
                    dve.wait_ge(y_ready, last.n + 1)
                    if last.since(1):
                        dve.wait_ge(scale_done, 4 * last.n)
                        dve.wait_ge(x1_made, 2 * last.n)
                    dve.wait_ge(xb_made, last.n + 1)
                    nc.vector.tensor_tensor(z[:], misc_ps[:, 0:SEQ].rearrange("p (t d) -> p t d", d=D), xb[:], ALU.add)\
                      .then_inc(z_made, 1)
                    dve.wait_ge(z_made, last.n + 1)
                    for t in range(TILES):
                        nc.vector.bn_stats(stats[:, t], z[:, t]).then_inc(stats_done, 1)
                    wait_first(dve, stats_done, 4 * last.n + 2)
                    for t in range(TILES):
                        nc.vector.bn_aggr(mean_var[:, t], stats[:, t]).then_inc(stats_done, 1)
                if now.exists():
                    maxima(now, range(13, HEADS))

            run_steps(dve, step)

        @block.tensor
        def _(pe):
            pe.wait_ge(bv_made, 4)
            pe.wait_ge(weights_in, 128)
            nc.tensor.matmul(misc_ps[:, 0:D], bv_masked[:], wo[:], start=True, stop=True).then_inc(bias_ps, 1)

            def scores(b, h):
                if h % HALF == 0:
                    pe.wait_ge(stacks_in[b.par][h // HALF], 32 * (b.half + 1))
                if b.since(1) or h >= 2:
                    pe.wait_ge(max_done, HEADS * b.n + h - 1)
                for t in range(TILES):
                    mm = nc.tensor.matmul(s1_ps[:, h % 2, t], q_stack[:, b.par, h, t * P:(t + 1) * P], k_stack[:, b.par, h],
                                          start=True, stop=True)
                mm.then_inc(scores_ready, 1)

            def shifted_scores(b, h):
                p = h // 2
                if h % HALF == 0:
                    pe.wait_ge(max_in[h // HALF], 48 * (b.n + 1))
                if h % 2 == 0 and (b.since(1) or p >= 2):
                    pe.wait_ge(exp_done, PAIRS * b.n + p - 1)
                for t in range(TILES):
                    mm = nc.tensor.matmul(st_ps[:, p % 2, h % 2, t], k_stack[:, b.par, h, t * P:(t + 1) * P],
                                          q_stack[:, b.par, h], start=True, stop=True)
                if h % 2:
                    mm.then_inc(shifted_ready, 1)

            def quad(b, g):
                r, s = g // 2, g % 2
                pe.wait_ge(exp_done, PAIRS * b.n + 2 * g + 2)
                if g == 0:
                    pe.wait_ge(v_evacuated, 2 * b.n + 2)
                    if b.since(1):
                        pe.wait_ge(av_evacuated, b.n)
                for t in range(TILES):
                    for j in range(4):
                        mm = nc.tensor.matmul(av_ps[32 * j:32 * j + 32, r], v_aug[:, b.par, t, s * HALF + r * 4 + j],
                                              probs[:, (2 * g + j // 2) % 4, j % 2, t], start=(s == 0 and t == 0),
                                              stop=(s == 1 and t == 1))
                mm.then_inc(quad_done, 1)

            def turn_max(b, half):
                rows = 3 * HALF * TILES
                wait_first(pe, max_split, (2 * b.n + half) * 4 + 4)
                nc.tensor.transpose(misc16[0:rows, 0:P], max_parts[:, half].rearrange("p r n -> p (r n)"), ident16[:])\
                  .then_inc(max_turned, 1)

            def step(u, c):
                new, now, late, last = (Batch(u, c, back) for back in range(4))
                for slot in range(HEADS):
                    if slot == 0 and new.exists():
                        pe.wait_ge(xt_in[new.par], 16 * (new.half + 1))
                        if last.exists():
                            pe.wait_ge(z_made, last.n)
                        if late.exists():
                            pe.wait_ge(max_evacuated, 2 * late.n + 1)
                        elif now.exists():
                            pe.wait_ge(qk_evacuated, 2 * new.n)
                        else:
                            pe.wait_ge(bias_made, 1)
                        nc.tensor.matmul(misc_ps[:, 0:SEQ], wq[:], x_t[:, new.par], start=True, stop=True)
                        nc.tensor.matmul(misc_ps[:, SEQ:2 * SEQ], wk[:], x_t[:, new.par], start=True, stop=True)\
                          .then_inc(qk_projected, 1)
                    if slot == 2 and late.exists():
                        if new.exists():
                            pe.wait_ge(qk_evacuated, 2 * new.n + 2)
                        else:
                            pe.wait_ge(max_evacuated, 2 * late.n + 1)
                            if last.exists():
                                pe.wait_ge(z_made, last.n)
                        turn_max(late, 1)
                    if slot == 2 and last.exists():
                        quad(last, 3)
                    if slot == 3 and now.exists():
                        if late.exists():
                            pe.wait_ge(max_evacuated, 2 * late.n + 2)
                        elif new.exists():
                            pe.wait_ge(qk_evacuated, 2 * new.n + 2)
                        for t in range(TILES):
                            mm = nc.tensor.matmul(misc_ps[:, t * D:(t + 1) * D], x_t[:, now.par, t * P:(t + 1) * P], wv[:],
                                                  start=True, stop=True)
                        mm.then_inc(v_projected, 1)
                    if slot == 5 and last.exists():
                        if now.exists():
                            pe.wait_ge(v_evacuated, 2 * now.n + 2)
                        elif late.exists():
                            pe.wait_ge(max_evacuated, 2 * late.n + 2)
                        else:
                            pe.wait_ge(z_made, last.n)
                        pe.wait_ge(av_evacuated, last.n + 1)
                        for t in range(TILES):
                            for r in range(2):
                                mm = nc.tensor.transpose(misc_ps[:, (t * 2 + r) * P:(t * 2 + r + 1) * P],
                                                         av[:, r, t * P:(t + 1) * P], ident[:])
                        mm.then_inc(av_turned, 1)
                    if slot == 8 and last.exists():
                        pe.wait_ge(normalised, 3 * last.n + 3)
                        for t in range(TILES):
                            mm = nc.tensor.transpose(misc_ps[:, t * P:(t + 1) * P], heads_out[:, t], ident[:])
                        mm.then_inc(heads_turned, 1)
                    if slot == 11 and now.exists():
                        if last.exists():
                            pe.wait_ge(heads_evacuated, last.n + 1)
                        else:
                            pe.wait_ge(v_evacuated, 2 * now.n + 2)
                        turn_max(now, 0)
                    if slot == 13 and last.exists():
                        pe.wait_ge(heads_evacuated, last.n + 1)
                        if now.exists():
                            pe.wait_ge(max_evacuated, 2 * now.n + 1)
                        for t in range(TILES):
                            mm = nc.tensor.matmul(misc_ps[:, t * D:(t + 1) * D], heads_t[:, t * P:(t + 1) * P], wo[:],
                                                  start=True, stop=True)
                        mm.then_inc(y_ready, 1)
                    if now.exists():
                        scores(now, slot)
                    if late.exists():
                        shifted_scores(late, slot)
                        if slot in (6, 10, 14):
                            quad(late, (slot - 6) // 4)

            pe.wait_ge(consts_made, 7)
            run_steps(pe, step)


F16 = mybir.dt.float16
I32 = mybir.dt.int32
U32 = mybir.dt.uint32

EXPERTS = 8
SHARED = EXPERTS
ALL = EXPERTS + 1
HIDDEN = 512
CHUNKS = HIDDEN // P
FC, PROJ = 0, HIDDEN
BOTH = HIDDEN + CHUNKS * D
TOP = 2
TOKEN_TILES = TOKENS // P
GROUP = 4
GROUPS = TOKEN_TILES // GROUP
EARLY_PLACED = 3
EMPTY_TILES = 12
BLOCK = 2 * P
SLOT_BLOCKS = TOP * TOKENS // BLOCK + EXPERTS - 1
SLOT_TILES = 2 * SLOT_BLOCKS
ROW = D + 2
ROW16 = 2 * ROW
TABLE_LEN = -(-(SLOT_BLOCKS + 4) // 4) * 4
GATE, DEST = D, D + 1
NOWHERE = 1 << 20
X_UNIT = 64.0
W_UNIT = 2048.0
UNIT = X_UNIT * W_UNIT
FAR_BELOW = -3.0e38


class Tile:

    def __init__(self, u, c, back, count):
        self.n = u * 4 + (c - back)
        self.buf = (c - back) % 4
        self.count = count
        self.fixed = isinstance(u, int)

    def exists(self):
        return not self.fixed or 0 <= self.n < self.count

    def since(self, n):
        return not self.fixed or self.n >= n


def run_tiles(eng, step, steps, loop_end):
    for s in range(8):
        step(s // 4, s % 4)
    with eng.Fori(2, loop_end) as u:
        for c in range(4):
            step(u, c)
    for s in range(4 * loop_end, steps):
        step(s // 4, s % 4)


def make_moe_buffers(nc, a, ctx):
    def sb(name, shape, dt=F32):
        return ctx.enter_context(nc.sbuf_tensor(name, shape, dt))

    a["x1_all"] = sb("x1_all", [P, TOKEN_TILES, D])
    a["w32_or_slots"] = sb("w32_or_slots", [P, max(ALL * BOTH, SLOT_TILES * ROW)])
    a["w32"] = a["w32_or_slots"][:, 0:ALL * BOTH].rearrange("p (e c) -> p e c", c=BOTH)
    a["empty_row"] = sb("empty_row", [P, ROW])
    a["slots"] = nc.dram_tensor("slots", [SLOT_TILES * P, ROW], F32, kind="Internal").ap()
    a["results"] = nc.dram_tensor("results", [TOP * TOKENS, D], F32, kind="Internal").ap()
    a["moe_weights_in"] = ctx.enter_context(nc.semaphore("moe_weights_in"))
    a["empty_made"] = ctx.enter_context(nc.semaphore("empty_made"))
    a["rows_placed"] = ctx.enter_context(nc.semaphore("rows_placed"))
    a["slots_emptied"] = ctx.enter_context(nc.semaphore("slots_emptied"))


def load_for_moe(sp, a, u, c):
    def weights(e):
        sp.dma_start(a["w32"][:, e, FC:FC + HIDDEN], a["w_fc"][:, e]).then_inc(a["moe_weights_in"], 16)
        sp.dma_start(a["w32"][:, e, PROJ:BOTH], a["w_proj"][:, e]).then_inc(a["moe_weights_in"], 16)

    def empty(lo, tiles):
        sp.dma_start(a["slots"][lo].rearrange("(s p) r -> p s r", p=P),
                     a["empty_row"][:].unsqueeze(1).to_broadcast([P, tiles, ROW])).then_inc(a["slots_emptied"], 16)

    after = FIRST_LOOP + LOOPS
    if not isinstance(u, int):
        if c == 0:
            weights(bass.ds(u - FIRST_LOOP, 1))
        else:
            empty(bass.ds((u - FIRST_LOOP) * (EMPTY_TILES * P), EMPTY_TILES * P), EMPTY_TILES)
    elif u >= after:
        step = 2 * (u - after) + c
        if LOOPS + step < ALL:
            weights(slice(LOOPS + step, LOOPS + step + 1))
        lo = (LOOPS + step) * EMPTY_TILES
        if lo < SLOT_TILES:
            hi = min(SLOT_TILES, lo + EMPTY_TILES)
            empty(slice(lo * P, hi * P), hi - lo)
    elif 2 * u + c == 3:
        sp.wait_ge(a["empty_made"], 2)


def make_empty_row(nc, pool, a):
    empty = a["empty_row"]
    nc.gpsimd.memset(empty[:], 0.0).then_inc(a["empty_made"], 1)
    pool.wait_ge(a["empty_made"], 1)
    nc.gpsimd.iota(empty[:].bitcast(I32)[:, DEST:DEST + 1], pattern=[[0, 1]], base=NOWHERE, channel_multiplier=0)\
      .then_inc(a["empty_made"], 1)


def build_moe(nc, a, ctx):
    def sb(name, shape, dt=F32):
        return ctx.enter_context(nc.sbuf_tensor(name, shape, dt))

    x1_all, w32 = a["x1_all"], a["w32"]
    rows1 = sb("rows1", [P, TOKEN_TILES, ROW])
    rows2 = sb("rows2", [P, TOKEN_TILES, ROW])
    w16 = sb("w16", [P, 2, ALL, BOTH], F16)
    b32 = sb("b32", [P, 2, ALL, P])
    b16 = sb("b16", [P, 2, ALL, P], F16)
    pick = sb("pick", [P, CHUNKS, P], F16)
    x16 = sb("x16", [D, TOKEN_TILES, 2, P], F16)
    ident_h = sb("ident_h", [P, P], F16)
    b_units = sb("b_units", [P, ALL, CHUNKS])
    slot_at = sb("slot_at", [P, TOP, TOKEN_TILES], U32)
    expert_of = sb("expert_of", [1, TABLE_LEN], I32)

    route_tokens(nc, a, dict(x1_all=x1_all, rows1=rows1, rows2=rows2, w32=w32, w16=w16, b32=b32, b16=b16, pick=pick, x16=x16,
                             ident_h=ident_h, slot_at=slot_at, expert_of=expert_of, b_units=b_units))
    shared_expert(nc, a, x1_all, rows1, rows2, w32, w16, b16, pick, x16, slot_at)
    routed_experts(nc, a, w16, b16, pick, ident_h, expert_of, b_units)
    add_and_normalise(nc, a, x1_all)


def place_rows(nc, a, rows1, rows2, slot_at, tiles):
    for t in tiles:
        for k, rows in enumerate((rows1, rows2)):
            nc.gpsimd.indirect_dma_start(out=a["slots"][:, :], out_offset=bass.IndirectOffsetOnAxis(
                ap=slot_at[:, k, t:t + 1], axis=0), in_=rows[:, t], in_offset=None).then_inc(a["rows_placed"], 16)


def fc_bias(nc, h_ps, b16, pick, e):
    nc.tensor.matmul(h_ps, one_of(b16[:, 0], e, 0, P), pick[:], start=True, stop=False)


def fc_matmuls(nc, h_ps, w16, e, x_hi, x_lo, width, onto_bias):
    for c in range(CHUNKS):
        lo, hi = FC + c * P, FC + (c + 1) * P
        to = h_ps[:, c * width:(c + 1) * width]
        nc.tensor.matmul(to, one_of(w16[:, 0], e, lo, hi), x_hi, start=not onto_bias, stop=False)
        nc.tensor.matmul(to, one_of(w16[:, 0], e, lo, hi), x_lo, start=False, stop=False)
        mm = nc.tensor.matmul(to, one_of(w16[:, 1], e, lo, hi), x_hi, start=False,
                              stop=(c == CHUNKS - 1 or not onto_bias))
    return mm


def proj_matmuls(nc, y_ps, w16, b16, pick, e, h_hi, h_lo, width):
    nc.tensor.matmul(y_ps, pick[:, 0, 0:P], one_of(b16[:, 1], e, 0, D), start=True, stop=False)
    for c in range(CHUNKS):
        lo, hi = PROJ + c * D, PROJ + (c + 1) * D
        units = slice(c * width, c * width + P)
        nc.tensor.matmul(y_ps, h_hi[:, units], one_of(w16[:, 0], e, lo, hi), start=False, stop=False)
        nc.tensor.matmul(y_ps, h_hi[:, units], one_of(w16[:, 1], e, lo, hi), start=False, stop=False)
        mm = nc.tensor.matmul(y_ps, h_lo[:, units], one_of(w16[:, 0], e, lo, hi), start=False, stop=(c == CHUNKS - 1))
    return mm


def one_of(weights, e, lo, hi):
    if isinstance(e, int):
        return weights[:, e, lo:hi]
    return weights[:, bass.ds(e, 1), lo:hi].rearrange("p o c -> p (o c)")


def route_tokens(nc, a, t):
    x1_all, rows1, rows2, w32, w16, b32, b16, pick, x16, ident_h, slot_at, expert_of = (
        t[k] for k in ("x1_all", "rows1", "rows2", "w32", "w16", "b32", "b16", "pick", "x16", "ident_h", "slot_at",
                       "expert_of"))
    parts1 = rows1[:].bitcast(F16)
    ctx = ExitStack()
    with ctx:
        def sb(name, shape, dt=F32):
            return ctx.enter_context(nc.sbuf_tensor(name, shape, dt))

        def ps(name, shape, dt=F32):
            return ctx.enter_context(nc.psum_tensor(name, shape, dt))

        def sem(name):
            return ctx.enter_context(nc.semaphore(name))

        TE = [P, TOKEN_TILES, EXPERTS]
        ET = [P, EXPERTS, TOKEN_TILES]
        w_r = sb("w_r", [D, EXPERTS])
        wr16 = sb("wr16", [D, 2, EXPERTS], F16)
        before = sb("before", [P, P], BF16)
        ones16 = sb("ones16", [P, P], BF16)
        counting = sb("counting", [P, TABLE_LEN], I32)
        number = sb("number", [P, TABLE_LEN])
        from_end = sb("from_end", [P, EXPERTS])
        block_start = sb("block_start", [P, TOKEN_TILES])
        not_first = sb("not_first", ET)
        logits = sb("logits", TE)
        logits2 = sb("logits2", TE)
        best = sb("best", [P, TOP, TOKEN_TILES])
        equal = sb("equal", TE)
        score = sb("score", TE)
        first = sb("first", [P, TOKEN_TILES])
        hot = sb("hot", [P, TOP] + TE[1:])
        chosen = sb("chosen", TE, BF16)
        gap = sb("gap", [P, TOKEN_TILES])
        exp_gap = sb("exp_gap", [P, TOKEN_TILES])
        exp_sum = sb("exp_sum", [P, TOKEN_TILES])
        gate1 = sb("gate1", [P, TOKEN_TILES])
        in_tile = sb("in_tile", ET)
        up_to = sb("up_to", ET)
        filled = sb("filled", ET)
        blocks_of = sb("blocks_of", [P, EXPERTS])
        blocks_up_to = sb("blocks_up_to", [P, EXPERTS])
        block_base = sb("block_base", [P, EXPERTS])
        base = sb("base", ET)
        base2 = sb("base2", ET)
        place = sb("place", TE)
        at_expert = sb("at_expert", TE)
        slot_f = sb("slot_f", [P, TOP, TOKEN_TILES])
        passed_block = sb("passed_block", [1, TABLE_LEN, EXPERTS])
        expert_f = sb("expert_f", [1, TABLE_LEN])
        expert_capped = sb("expert_capped", [1, TABLE_LEN])

        turn_ps = ps("turn_ps", [P, 4, GROUP * P])
        turn16 = turn_ps[:].bitcast(F16)
        logit_ps = ps("logit_ps", [P, 512])
        before_ps = ps("before_ps", [P, 512])
        total_ps = ps("total_ps", [P, 512])

        QUARTERS = 4
        CUT = TOKEN_TILES // QUARTERS
        router_in = sem("router_in")
        rows_copied = sem("rows_copied")
        x_turned = [sem("x_turned_act"), sem("x_turned_dve")]
        biases_in = sem("biases_in")
        cleared = sem("cleared")
        routing_consts = sem("routing_consts")
        turned = sem("turned")
        x_high = sem("x_high")
        x_low = sem("x_low")
        router_split = sem("router_split")
        logits_ready = sem("logits_ready")
        routed = sem("routed")
        gap_made = sem("gap_made")
        gap_exp = sem("gap_exp")
        chosen_made = sem("chosen_made")
        counts_ready = sem("counts_ready")
        slots_known = sem("slots_known")
        weights_high = sem("weights_high")
        weights_low = sem("weights_low")

        block = ctx.enter_context(nc.Block())

        @block.sync
        def _(sp):
            sp.dma_start(w_r[:], a["w_r"]).then_inc(router_in, 16)
            sp.dma_start(t["b_units"][:], a["b_units"]).then_inc(biases_in, 16)
            sp.wait_ge(cleared, 1)
            for row in (0, 32):
                sp.dma_start(b32[row:row + CHUNKS, 0], a["b_fc"].rearrange("e (c m) -> c e m", m=P)).then_inc(biases_in, 16)
                sp.dma_start(b32[row:row + 1, 1], a["b_proj"].unsqueeze(0)).then_inc(biases_in, 16)
            sp.wait_ge(x_low, QUARTERS)
            sp.dma_start(rows2[:, :, 0:D], rows1[:, :, 0:D]).then_inc(rows_copied, 16)
            sp.wait_ge(rows_copied, 16)

        @block.gpsimd
        def _(pool):
            nc.gpsimd.memset(ident_h[:], 0.0).then_inc(routing_consts, 1)
            nc.gpsimd.memset(b32[:], 0.0).then_inc(cleared, 1)
            pool.wait_ge(routing_consts, 1)
            nc.gpsimd.affine_select(out=ident_h[:], in_=ident_h[:], compare_op=ALU.not_equal, fill=1.0, base=0,
                                    pattern=[[-1, P]], channel_multiplier=1).then_inc(routing_consts, 1)
            nc.gpsimd.memset(before[:], 1.0).then_inc(routing_consts, 1)
            nc.gpsimd.memset(ones16[:], 1.0).then_inc(routing_consts, 1)
            nc.gpsimd.memset(pick[:], 0.0).then_inc(routing_consts, 1)
            nc.gpsimd.memset(not_first[:], 1.0).then_inc(routing_consts, 1)
            nc.gpsimd.iota(counting[:], pattern=[[1, TABLE_LEN]], base=0, channel_multiplier=0).then_inc(routing_consts, 1)
            nc.gpsimd.iota(rows1[:].bitcast(I32)[:, :, DEST:DEST + 1], pattern=[[P, TOKEN_TILES], [0, 1]], base=0,
                           channel_multiplier=1).then_inc(routing_consts, 1)
            nc.gpsimd.iota(rows2[:].bitcast(I32)[:, :, DEST:DEST + 1], pattern=[[P, TOKEN_TILES], [0, 1]], base=TOKENS,
                           channel_multiplier=1).then_inc(routing_consts, 1)
            pool.wait_ge(routing_consts, 9)
            nc.gpsimd.affine_select(out=before[:], in_=before[:], compare_op=ALU.is_gt, fill=0.0, base=0,
                                    pattern=[[1, P]], channel_multiplier=-1).then_inc(routing_consts, 1)
            nc.gpsimd.memset(not_first[:, :, 0:1], 0.0).then_inc(routing_consts, 1)
            nc.gpsimd.tensor_copy(number[:], counting[:]).then_inc(routing_consts, 1)
            for n, row in enumerate((0, 32)):
                nc.gpsimd.affine_select(out=pick[:], in_=pick[:], compare_op=ALU.not_equal, fill=X_UNIT, base=-row,
                                        pattern=[[-1, CHUNKS], [0, P]], channel_multiplier=1).then_inc(routing_consts, 1)
                pool.wait_ge(routing_consts, 13 + n)
            nc.gpsimd.tensor_scalar(from_end[:], number[:, 0:EXPERTS], -1.0, float(EXPERTS), ALU.mult, ALU.add)\
              .then_inc(routing_consts, 1)
            nc.gpsimd.tensor_scalar(block_start[:], number[:, 0:TOKEN_TILES], float(BLOCK), 0.0, ALU.mult, ALU.add)\
              .then_inc(routing_consts, 1)
            pool.wait_ge(a["slots_emptied"], 16 * -(-SLOT_TILES // EMPTY_TILES))
            pool.wait_ge(rows_copied, 16)
            pool.wait_ge(slots_known, 1)
            place_rows(nc, a, rows1, rows2, slot_at, range(EARLY_PLACED))

        @block.scalar
        def _(act):
            act.wait_ge(router_in, 16)
            nc.scalar.activation(wr16[:, 0], w_r[:], ACT.Copy, scale=W_UNIT).then_inc(router_split, 1)
            for q in range(QUARTERS):
                tiles = slice(q * CUT, (q + 1) * CUT)
                nc.scalar.activation(parts1[:, tiles, 0:D], x1_all[:, tiles], ACT.Copy, scale=X_UNIT).then_inc(x_high, 1)
            for g in range(0, GROUPS, 2):
                act.wait_ge(turned, g + 1)
                nc.scalar.activation(x16[:, g * GROUP:(g + 1) * GROUP].rearrange("p t k n -> p (t k n)"), turn16[:, g % 4],
                                     ACT.Copy).then_inc(x_turned[0], 1)
            act.wait_ge(a["moe_weights_in"], 32 * ALL)
            act.wait_ge(biases_in, 80)
            nc.scalar.activation(w16[:, 0, SHARED], w32[:, SHARED], ACT.Copy, scale=W_UNIT).then_inc(weights_high, 1)
            nc.scalar.activation(b16[:], b32[:], ACT.Copy, scale=W_UNIT).then_inc(weights_high, 1)
            act.wait_ge(gap_made, 1)
            nc.scalar.activation(exp_gap[:], gap[:], ACT.Exp, scale=1.0 / UNIT).then_inc(gap_exp, 1)
            for e in range(0, EXPERTS, 2):
                nc.scalar.activation(w16[:, 0, e:e + 2], w32[:, e:e + 2], ACT.Copy, scale=W_UNIT).then_inc(weights_high, 1)

        @block.tensor
        def _(pe):
            pe.wait_ge(routing_consts, 2)

            def turn(g):
                pe.wait_ge(x_high, g * GROUP // CUT + 1)
                pe.wait_ge(x_low, g * GROUP // CUT + 1)
                if g >= 4:
                    pe.wait_ge(x_turned[g % 2], g // 2 - 1)
                for k in range(GROUP):
                    for part in range(2):
                        mm = nc.tensor.transpose(turn16[:, g % 4, (2 * k + part) * P:(2 * k + part + 1) * P],
                                                 parts1[:, g * GROUP + k, part * D:(part + 1) * D], ident_h[:])
                mm.then_inc(turned, 1)

            def router(g):
                pe.wait_ge(x_turned[g % 2], g // 2 + 1)
                pe.wait_ge(router_split, 2)
                for k in range(GROUP):
                    n = g * GROUP + k
                    to = logit_ps[:, n * EXPERTS:(n + 1) * EXPERTS]
                    nc.tensor.matmul(to, x16[:, n, 0], wr16[:, 0], start=True, stop=False)
                    nc.tensor.matmul(to, x16[:, n, 0], wr16[:, 1], start=False, stop=False)
                    mm = nc.tensor.matmul(to, x16[:, n, 1], wr16[:, 0], start=False, stop=True)
                mm.then_inc(logits_ready, 1)

            for g in range(GROUPS + 2):
                if g < GROUPS:
                    turn(g)
                if g >= 2:
                    router(g - 2)
            pe.wait_ge(chosen_made, 1)
            pe.wait_ge(routing_consts, 10)
            used = chosen[:].rearrange("p t e -> p (t e)")
            nc.tensor.matmul(before_ps[:, 0:TOKEN_TILES * EXPERTS], before[:], used, start=True, stop=True).then_inc(counts_ready, 1)
            nc.tensor.matmul(total_ps[:, 0:TOKEN_TILES * EXPERTS], ones16[:], used, start=True, stop=True).then_inc(counts_ready, 1)

        @block.vector
        def _(dve):
            done = [0]

            def then(instruction):
                instruction.then_inc(routed, 1)
                done[0] += 1
                dve.wait_ge(routed, done[0])

            dve.wait_ge(router_split, 1)
            nc.vector.scalar_tensor_tensor(out=wr16[:, 1], in0=w_r[:], scalar=W_UNIT, in1=wr16[:, 0], op0=ALU.mult,
                                           op1=ALU.subtract).then_inc(router_split, 1)
            for q in range(QUARTERS):
                tiles = slice(q * CUT, (q + 1) * CUT)
                dve.wait_ge(x_high, q + 1)
                nc.vector.scalar_tensor_tensor(out=parts1[:, tiles, D:2 * D], in0=x1_all[:, tiles], scalar=X_UNIT,
                                               in1=parts1[:, tiles, 0:D], op0=ALU.mult, op1=ALU.subtract).then_inc(x_low, 1)
            for g in range(1, GROUPS, 2):
                dve.wait_ge(turned, g + 1)
                nc.vector.tensor_copy(x16[:, g * GROUP:(g + 1) * GROUP].rearrange("p t k n -> p (t k n)"), turn16[:, g % 4])\
                  .then_inc(x_turned[1], 1)
            dve.wait_ge(logits_ready, GROUPS)
            dve.wait_ge(routing_consts, 16)
            then(nc.vector.tensor_copy(logits[:], logit_ps[:, 0:TOKEN_TILES * EXPERTS].rearrange("p (t e) -> p t e", e=EXPERTS)))
            for k, of in enumerate((logits, logits2)):
                if k == 1:
                    then(nc.vector.scalar_tensor_tensor(out=logits2[:], in0=hot[:, 0], scalar=FAR_BELOW, in1=logits[:],
                                                        op0=ALU.mult, op1=ALU.add))
                then(nc.vector.tensor_reduce(best[:, k], of[:], AX_X, ALU.max))
                if k == 1:
                    then(nc.vector.tensor_tensor(gap[:], best[:, 1], best[:, 0], ALU.subtract))
                    dve.sem_inc(gap_made, 1)
                then(nc.vector.tensor_tensor(equal[:], of[:], best[:, k].unsqueeze(2).to_broadcast(TE), ALU.is_equal))
                then(nc.vector.tensor_tensor(score[:], equal[:], from_end[:].unsqueeze(1).to_broadcast(TE), ALU.mult))
                then(nc.vector.tensor_reduce(first[:], score[:], AX_X, ALU.max))
                then(nc.vector.tensor_tensor(hot[:, k], score[:], first[:].unsqueeze(2).to_broadcast(TE), ALU.is_equal))
            then(nc.vector.tensor_tensor(chosen[:], hot[:, 0], hot[:, 1], ALU.add))
            dve.sem_inc(chosen_made, 1)
            dve.wait_ge(gap_exp, 1)
            then(nc.vector.tensor_scalar(exp_sum[:], exp_gap[:], UNIT, UNIT, ALU.mult, ALU.add))
            then(nc.vector.reciprocal(gate1[:], exp_sum[:]))
            then(nc.vector.tensor_tensor(rows2[:, :, GATE:GATE + 1], gate1[:].unsqueeze(2), exp_gap[:].unsqueeze(2), ALU.mult))
            then(nc.vector.tensor_copy(rows1[:, :, GATE:GATE + 1], gate1[:].unsqueeze(2)))
            dve.wait_ge(counts_ready, 2)
            then(nc.vector.tensor_copy(in_tile[:], total_ps[:, 0:TOKEN_TILES * EXPERTS].rearrange("p (t e) -> p e t", e=EXPERTS)))
            then(nc.vector.tensor_tensor_scan(up_to[:].rearrange("p e t -> p (e t)"), not_first[:].rearrange("p e t -> p (e t)"),
                                              in_tile[:].rearrange("p e t -> p (e t)"), 0.0, ALU.mult, ALU.add))
            then(nc.vector.tensor_tensor(filled[:], up_to[:, :, TOKEN_TILES - 1:TOKEN_TILES].to_broadcast(ET),
                                         block_start[:].unsqueeze(1).to_broadcast(ET), ALU.is_gt))
            then(nc.vector.tensor_reduce(blocks_of[:], filled[:], AX_X, ALU.add))
            then(nc.vector.tensor_tensor_scan(blocks_up_to[:], not_first[:, 0, 1:EXPERTS + 1], blocks_of[:], 0.0, ALU.mult, ALU.add))
            then(nc.vector.tensor_tensor(block_base[:], blocks_up_to[:], blocks_of[:], ALU.subtract))
            then(nc.vector.tensor_tensor(base[:], up_to[:], in_tile[:], ALU.subtract))
            then(nc.vector.scalar_tensor_tensor(out=base2[:], in0=block_base[:].unsqueeze(2).to_broadcast(ET), scalar=float(BLOCK),
                                                in1=base[:], op0=ALU.mult, op1=ALU.add))
            then(nc.vector.tensor_tensor(place[:], before_ps[:, 0:TOKEN_TILES * EXPERTS].rearrange("p (t e) -> p t e", e=EXPERTS),
                                         base2[:].rearrange("p e t -> p t e"), ALU.add))
            for k in range(TOP):
                then(nc.vector.tensor_tensor(at_expert[:], place[:], hot[:, k], ALU.mult))
                then(nc.vector.tensor_reduce(slot_f[:, k], at_expert[:], AX_X, ALU.add))
            then(nc.vector.tensor_copy(slot_at[:], slot_f[:]))
            dve.sem_inc(slots_known, 1)
            TABLE = [1, TABLE_LEN, EXPERTS]
            then(nc.vector.tensor_tensor(passed_block[:], number[0:1].unsqueeze(2).to_broadcast(TABLE),
                                         blocks_up_to[0:1].unsqueeze(1).to_broadcast(TABLE), ALU.is_ge))
            then(nc.vector.tensor_reduce(expert_f[:], passed_block[:], AX_X, ALU.add))
            then(nc.vector.tensor_scalar(expert_capped[:], expert_f[:], float(EXPERTS - 1), None, ALU.min))
            then(nc.vector.tensor_copy(expert_of[:], expert_capped[:]))
            dve.wait_ge(weights_high, 2)
            nc.vector.scalar_tensor_tensor(out=w16[:, 1, SHARED], in0=w32[:, SHARED], scalar=W_UNIT, in1=w16[:, 0, SHARED],
                                           op0=ALU.mult, op1=ALU.subtract).then_inc(weights_low, 1)
            nc.vector.scalar_tensor_tensor(out=b16[32:64], in0=b32[32:64], scalar=W_UNIT, in1=b16[32:64],
                                           op0=ALU.mult, op1=ALU.subtract).then_inc(weights_low, 1)


def shared_expert(nc, a, x1_all, rows1, rows2, w32, w16, b16, pick, x16, slot_at):
    ctx = ExitStack()
    with ctx:
        def sb(name, shape, dt=F32):
            return ctx.enter_context(nc.sbuf_tensor(name, shape, dt))

        def ps(name, shape, dt=F32):
            return ctx.enter_context(nc.psum_tensor(name, shape, dt))

        def sem(name):
            return ctx.enter_context(nc.semaphore(name))

        LAG = 2
        STEPS = TOKEN_TILES + LAG
        COLS = EXPERTS * BOTH // TOKEN_TILES
        hid = sb("hid", [P, 4, HIDDEN])
        hid16 = sb("hid16", [P, 4, 2, HIDDEN], F16)
        h_ps = ps("h_ps", [P, 4, HIDDEN])
        y_ps = ps("y_ps", [P, 4, 512])
        hidden_ready, activated, hidden_high, hidden_low = (
            sem("hidden_ready"), sem("activated"), sem("hidden_high"), sem("hidden_low"))
        projected, added, expert_low = sem("projected"), sem("added"), sem("expert_low")
        block = ctx.enter_context(nc.Block())

        def at(u, c, back=0):
            return Tile(u, c, back, TOKEN_TILES)

        @block.gpsimd
        def _(pool):
            place_rows(nc, a, rows1, rows2, slot_at, range(EARLY_PLACED, TOKEN_TILES))
            pool.wait_ge(a["rows_placed"], 16 * TOP * TOKEN_TILES)

        @block.tensor
        def _(pe):
            def step(u, c):
                t = at(u, c)
                if t.exists():
                    if t.since(4):
                        pe.wait_ge(activated, t.n - 3)
                    if t.fixed:
                        x_hi, x_lo = x16[:, t.n, 0], x16[:, t.n, 1]
                    else:
                        x_hi, x_lo = (x16[:, bass.ds(t.n, 1), part].rearrange("p o n -> p (o n)") for part in range(2))
                    fc_bias(nc, h_ps[:, t.buf], b16, pick, SHARED)
                    fc_matmuls(nc, h_ps[:, t.buf], w16, SHARED, x_hi, x_lo, P, True).then_inc(hidden_ready, 1)
                t = at(u, c, LAG)
                if t.exists():
                    pe.wait_ge(hidden_low, t.n + 1)
                    if t.since(4):
                        pe.wait_ge(added, t.n - 3)
                    proj_matmuls(nc, y_ps[:, t.buf, 0:D], w16, b16, pick, SHARED, hid16[:, t.buf, 0], hid16[:, t.buf, 1], P)\
                      .then_inc(projected, 1)
            run_tiles(pe, step, STEPS, TOKEN_TILES // 4)

        @block.scalar
        def _(act):
            def step(u, c):
                t = at(u, c)
                if t.exists():
                    act.wait_ge(hidden_ready, t.n + 1)
                    if t.since(4):
                        act.wait_ge(hidden_low, t.n - 3)
                    nc.scalar.activation(hid[:, t.buf], h_ps[:, t.buf], ACT.Gelu_apprx_tanh, scale=1.0 / UNIT).then_inc(activated, 1)
                    if t.since(4):
                        act.wait_ge(projected, t.n - 3)
                    act.wait_ge(activated, t.n + 1)
                    nc.scalar.activation(hid16[:, t.buf, 0], hid[:, t.buf], ACT.Copy, scale=X_UNIT).then_inc(hidden_high, 1)
            run_tiles(act, step, TOKEN_TILES, TOKEN_TILES // 4)

        @block.vector
        def _(dve):
            w32_flat = w32.rearrange("p e c -> p (e c)")
            w_hi, w_lo = (w16[:, part].rearrange("p e c -> p (e c)") for part in range(2))

            def step(u, c):
                t = at(u, c)
                if t.exists():
                    cols = slice(t.n * COLS, (t.n + 1) * COLS) if t.fixed else bass.ds(t.n * COLS, COLS)
                    nc.vector.scalar_tensor_tensor(out=w_lo[:, cols], in0=w32_flat[:, cols], scalar=W_UNIT, in1=w_hi[:, cols],
                                                   op0=ALU.mult, op1=ALU.subtract).then_inc(expert_low, 1)
                    dve.wait_ge(hidden_high, t.n + 1)
                    if t.since(4):
                        dve.wait_ge(projected, t.n - 3)
                    nc.vector.scalar_tensor_tensor(out=hid16[:, t.buf, 1], in0=hid[:, t.buf], scalar=X_UNIT,
                                                   in1=hid16[:, t.buf, 0], op0=ALU.mult, op1=ALU.subtract).then_inc(hidden_low, 1)
                t = at(u, c, LAG)
                if t.exists():
                    rows = slice(t.n, t.n + 1) if t.fixed else bass.ds(t.n, 1)
                    dve.wait_ge(projected, t.n + 1)
                    nc.vector.scalar_tensor_tensor(out=x1_all[:, rows], in0=y_ps[:, t.buf:t.buf + 1, 0:D], scalar=1.0 / UNIT,
                                                   in1=x1_all[:, rows], op0=ALU.mult, op1=ALU.add).then_inc(added, 1)
            run_tiles(dve, step, STEPS, TOKEN_TILES // 4)


def routed_experts(nc, a, w16, b16, pick, ident_h, expert_of, b_units):
    ctx = ExitStack()
    with ctx:
        def sb(name, shape, dt=F32):
            return ctx.enter_context(nc.sbuf_tensor(name, shape, dt))

        def ps(name, shape, dt=F32):
            return ctx.enter_context(nc.psum_tensor(name, shape, dt))

        def sem(name):
            return ctx.enter_context(nc.semaphore(name))

        FC_LAG, PROJ_LAG, GATE_LAG = 1, 3, 4
        STEPS = SLOT_BLOCKS + PROJ_LAG
        EARLY = 8
        LOAD = 16
        ALL_LOADED = 16 * -(-(SLOT_TILES - 2 * EARLY) // LOAD)
        LOOP_END = SLOT_BLOCKS // 4
        WIDE = CHUNKS * BLOCK
        rows_in = a["w32_or_slots"][:, 0:SLOT_TILES * ROW].rearrange("p (s r) -> p s r", r=ROW)
        parts_in = a["w32_or_slots"][:].bitcast(F16)[:, 0:SLOT_TILES * ROW16].rearrange("p (s r) -> p s r", r=ROW16)
        rows16 = sb("rows16", [D, 4, 2, BLOCK], F16)
        dest = sb("dest", [P, 4, 2], U32)
        bias = sb("bias", [P, 4, CHUNKS])
        hid = sb("hid_r", [P, 2, WIDE])
        hid16 = sb("hid16_r", [P, 4, 2, WIDE], F16)
        gated = sb("gated", [P, 4, 2, D])
        t_ps = ps("t_ps", [P, 2, 512])
        t16 = t_ps[:].bitcast(F16)
        h_ps = ps("h_ps_r", [P, 2, WIDE])
        y_ps = ps("y_ps_r", [P, 2, 512])
        early_loaded, loaded = sem("early_loaded"), sem("loaded")
        turned, rows_turned, dest_made = sem("row_turned"), sem("rows_turned"), sem("dest_made")
        hidden_ready, activated, hidden_high, hidden_low = (
            sem("hidden_ready_r"), sem("activated_r"), sem("hidden_high_r"), sem("hidden_low_r"))
        projected, gated_made, bias_made = sem("projected_r"), sem("gated_made"), sem("hidden_bias_made")
        sent = [sem(f"sent{i}") for i in range(4)]
        block = ctx.enter_context(nc.Block())

        def at(u, c, back=0):
            t = Tile(u, c, back, SLOT_BLOCKS)
            t.turn = u + (c - back) // 4
            return t

        def load_experts(u, engine):
            start = isinstance(u, int) and u == 0
            lo = 0 if start else 4 * u - 4
            of = slice(lo, lo + 8) if isinstance(u, int) else bass.ds(lo, 8)
            _, values = nc.values_load_multi_w_load_instructions(
                expert_of[0:1, of], engines=[engine], min_val=0, max_val=EXPERTS - 1,
                skip_runtime_bounds_check_because="the table is capped at the last expert")
            return {k - (0 if start else 4): value for k, value in enumerate(values)}

        @block.sync
        def _(sp):
            slots = a["slots"].rearrange("(s p) r -> p s r", p=P)
            early = 2 * EARLY
            sp.dma_start(rows_in[:, 0:early], slots[:, 0:early]).then_inc(early_loaded, 16)
            for lo in range(early, SLOT_TILES, LOAD):
                hi = min(lo + LOAD, SLOT_TILES)
                sp.dma_start(rows_in[:, lo:hi], slots[:, lo:hi]).then_inc(loaded, 16)

        @block.gpsimd
        def _(pool):
            def step(u, c):
                t = at(u, c)
                if t.exists():
                    wait_first(pool, gated_made, t.n + 1)
                    wait_first(pool, dest_made, t.n + 1)
                    for half in range(2):
                        nc.gpsimd.indirect_dma_start(out=a["results"][:, :], out_offset=bass.IndirectOffsetOnAxis(
                            ap=dest[:, t.buf, half:half + 1], axis=0), in_=gated[:, t.buf, half], in_offset=None,
                            bounds_check=TOP * TOKENS - 1, oob_is_err=False).then_inc(sent[t.buf], 16)
            run_tiles(pool, step, SLOT_BLOCKS, LOOP_END)
            for buf in range(4):
                pool.wait_ge(sent[buf], 32 * ((SLOT_BLOCKS - 1 - buf) // 4 + 1))

        @block.tensor
        def _(pe):
            table = {}

            def step(u, c):
                t = at(u, c)
                if t.exists():
                    if t.since(2):
                        pe.wait_ge(rows_turned, t.n - 1)
                    for half in range(2):
                        tile = 2 * t.n + half
                        for part in range(2):
                            of = parts_in[:, tile if t.fixed else bass.ds(tile, 1), part * D:(part + 1) * D]
                            if not t.fixed:
                                of = of.rearrange("p o d -> p (o d)")
                            to = (2 * part + half) * P
                            mm = nc.tensor.transpose(t16[:, t.buf % 2, to:to + P], of, ident_h[:])
                    mm.then_inc(turned, 1)
                t = at(u, c, FC_LAG)
                if t.exists():
                    pe.wait_ge(rows_turned, t.n + 1)
                    if t.since(2):
                        pe.wait_ge(activated, t.n - 1)
                    fc_matmuls(nc, h_ps[:, t.buf % 2], w16, table[c - FC_LAG], rows16[:, t.buf, 0],
                               rows16[:, t.buf, 1], BLOCK, False).then_inc(hidden_ready, 1)
                t = at(u, c, PROJ_LAG)
                if t.exists():
                    pe.wait_ge(hidden_high, t.n + 1)
                    pe.wait_ge(hidden_low, t.n + 1)
                    if t.since(2):
                        pe.wait_ge(gated_made, t.n - 1)
                    for half in range(2):
                        mm = proj_matmuls(nc, y_ps[:, t.buf % 2, half * D:(half + 1) * D], w16, b16, pick, table[c - PROJ_LAG],
                                          hid16[:, t.buf, 0, half * P:], hid16[:, t.buf, 1, half * P:], BLOCK)
                    mm.then_inc(projected, 1)

            def four_steps(u):
                table.clear()
                table.update(load_experts(u, mybir.EngineType.PE))
                for c in range(4):
                    if not isinstance(u, int) or 4 * u + c < STEPS:
                        step(u, c)

            pe.wait_ge(early_loaded, 16)
            for u in range(EARLY // 4):
                four_steps(u)
            pe.wait_ge(loaded, ALL_LOADED)
            with pe.Fori(EARLY // 4, LOOP_END) as u:
                four_steps(u)
            for u in range(LOOP_END, -(-STEPS // 4)):
                four_steps(u)

        @block.scalar
        def _(act):
            def step(u, c):
                t = at(u, c, FC_LAG)
                if t.exists():
                    act.wait_ge(hidden_ready, t.n + 1)
                    if t.since(2):
                        act.wait_ge(hidden_low, t.n - 1)
                    act.wait_ge(bias_made, t.n + 1)
                    for k in range(CHUNKS):
                        cols = slice(k * BLOCK, (k + 1) * BLOCK)
                        act_ = nc.scalar.activation(hid[:, t.buf % 2, cols], h_ps[:, t.buf % 2, cols], ACT.Gelu_apprx_tanh,
                                                    scale=1.0 / UNIT, bias=bias[:, t.buf, k:k + 1])
                    act_.then_inc(activated, 1)
            run_tiles(act, step, SLOT_BLOCKS + FC_LAG, LOOP_END)

        @block.vector
        def _(dve):
            table = {}

            def step(u, c):
                t = at(u, c)
                if t.exists():
                    if t.since(4):
                        dve.wait_ge(activated, t.n - 3)
                    nc.vector.tensor_copy(bias[:, t.buf:t.buf + 1], b_units[:, bass.ds(table[c], 1)]).then_inc(bias_made, 1)
                    dve.wait_ge(turned, t.n + 1)
                    if t.since(4):
                        dve.wait_ge(hidden_ready, t.n - 3)
                    nc.vector.tensor_copy(rows16[:, t.buf].rearrange("p k n -> p (k n)"), t16[:, t.buf % 2, 0:2 * BLOCK])\
                      .then_inc(rows_turned, 1)
                t = at(u, c, GATE_LAG)
                if t.exists():
                    tiles = slice(2 * t.n, 2 * t.n + 2) if t.fixed else bass.ds(2 * t.n, 2)
                    if t.since(4):
                        dve.wait_ge(sent[t.buf], 32 * t.turn)
                    nc.vector.tensor_copy(dest[:, t.buf].unsqueeze(2), rows_in[:, tiles, DEST:DEST + 1].bitcast(U32))\
                      .then_inc(dest_made, 1)
                    dve.wait_ge(projected, t.n + 1)
                    nc.vector.tensor_tensor(gated[:, t.buf], y_ps[:, t.buf % 2, 0:2 * D].rearrange("p (k d) -> p k d", d=D),
                                            rows_in[:, tiles, GATE:GATE + 1].to_broadcast([P, 2, D]), ALU.mult)\
                      .then_inc(gated_made, 1)
                t = at(u, c, FC_LAG)
                if t.exists():
                    dve.wait_ge(activated, t.n + 1)
                    if t.since(4):
                        dve.wait_ge(projected, t.n - 3)
                    nc.vector.tensor_scalar(hid16[:, t.buf, 0], hid[:, t.buf % 2], X_UNIT, 1.0, ALU.mult, ALU.mult)\
                      .then_inc(hidden_high, 1)
                    dve.wait_ge(hidden_high, t.n + 1)
                    nc.vector.scalar_tensor_tensor(out=hid16[:, t.buf, 1], in0=hid[:, t.buf % 2], scalar=X_UNIT,
                                                   in1=hid16[:, t.buf, 0], op0=ALU.mult, op1=ALU.subtract).then_inc(hidden_low, 1)

            def four_steps(u):
                table.clear()
                table.update(load_experts(u, mybir.EngineType.DVE))
                for c in range(4):
                    if not isinstance(u, int) or 4 * u + c < SLOT_BLOCKS + GATE_LAG:
                        step(u, c)

            dve.wait_ge(early_loaded, 16)
            for u in range(EARLY // 4):
                four_steps(u)
            dve.wait_ge(loaded, ALL_LOADED)
            with dve.Fori(EARLY // 4, LOOP_END) as u:
                four_steps(u)
            for u in range(LOOP_END, -(-(SLOT_BLOCKS + GATE_LAG) // 4)):
                four_steps(u)


def add_and_normalise(nc, a, x1_all):
    ctx = ExitStack()
    with ctx:
        def sb(name, shape, dt=F32):
            return ctx.enter_context(nc.sbuf_tensor(name, shape, dt))

        def sem(name):
            return ctx.enter_context(nc.semaphore(name))

        DEEP = 4
        first, second = (sb(f"expert{k}", [P, GROUPS, GROUP, D]) for k in range(TOP))
        both = sb("both", [P, DEEP, GROUP, D])
        total = sb("total", [P, DEEP, GROUP, D])
        minus_half2 = sb("minus_half2", [P, GROUP])
        stats2 = sb("stats2", [P, GROUP, 6])
        mean_var2 = sb("mean_var2", [P, DEEP, GROUP, 2])
        var_eps2 = sb("var_eps2", [P, GROUP])
        rstd2 = sb("rstd2", [P, DEEP, GROUP])
        shift2 = sb("shift2", [P, DEEP, GROUP])
        results_in = [sem(f"results_in{g}") for g in range(GROUPS)]
        shifts_made = sem("shifts_made")
        half_made, both_made, totals, scale2_done, normed, out_written = (
            sem("half_made"), sem("both_made"), sem("totals"), sem("scale2_done"), sem("normed"), sem("out_written"))
        DVE_STEPS = 1 + 2 * GROUP
        block = ctx.enter_context(nc.Block())

        @block.sync
        def _(sp):
            for g in range(GROUPS):
                for k, to in enumerate((first, second)):
                    lo = k * TOKENS + g * GROUP * P
                    sp.dma_start(to[:, g], a["results"][lo:lo + GROUP * P].rearrange("(t p) d -> p t d", p=P))\
                      .then_inc(results_in[g], 16)
            for g in range(GROUPS):
                sp.wait_ge(normed, GROUP * (g + 1))
                sp.dma_start(a["out"][g * GROUP * P:(g + 1) * GROUP * P].rearrange("(t p) d -> p t d", p=P), first[:, g])\
                  .then_inc(out_written, 16)
            sp.wait_ge(out_written, 16 * GROUPS)

        @block.gpsimd
        def _(pool):
            nc.gpsimd.memset(minus_half2[:], -0.5).then_inc(half_made, 1)
            pool.wait_ge(half_made, 1)

            def sum_experts(g):
                pool.wait_ge(results_in[g], 32)
                if g >= DEEP:
                    pool.wait_ge(totals, DVE_STEPS * (g - DEEP) + 1)
                nc.gpsimd.tensor_tensor(both[:, g % DEEP], first[:, g], second[:, g], ALU.add).then_inc(both_made, 1)

            sum_experts(0)
            for g in range(GROUPS):
                if g + 1 < GROUPS:
                    sum_experts(g + 1)
                done = 2 * g
                pool.wait_ge(totals, DVE_STEPS * (g + 1))
                if g >= DEEP:
                    pool.wait_ge(normed, GROUP * (g - DEEP + 1))
                    pool.wait_ge(shifts_made, g - DEEP + 1)
                if g >= 1:
                    pool.wait_ge(scale2_done, done)
                nc.gpsimd.tensor_scalar(var_eps2[:], mean_var2[:, g % DEEP, :, 1], EPS, None, ALU.add).then_inc(scale2_done, 1)
                pool.wait_ge(scale2_done, done + 1)
                nc.gpsimd.tensor_tensor(rstd2[:, g % DEEP], var_eps2[:], minus_half2[:], ALU.pow).then_inc(scale2_done, 1)

        @block.vector
        def _(dve):
            def make_shift(g):
                dve.wait_ge(scale2_done, 2 * g + 2)
                nc.vector.scalar_tensor_tensor(out=shift2[:, g % DEEP].unsqueeze(2), in0=mean_var2[:, g % DEEP, :, 0:1], scalar=-1.0,
                                               in1=rstd2[:, g % DEEP].unsqueeze(2), op0=ALU.mult, op1=ALU.mult)\
                  .then_inc(shifts_made, 1)

            for g in range(GROUPS):
                dve.wait_ge(both_made, g + 1)
                if g >= DEEP:
                    dve.wait_ge(normed, GROUP * (g - DEEP + 1))
                nc.vector.tensor_tensor(total[:, g % DEEP], x1_all[:, g * GROUP:(g + 1) * GROUP], both[:, g % DEEP], ALU.add)\
                  .then_inc(totals, 1)
                dve.wait_ge(totals, DVE_STEPS * g + 1)
                for t in range(GROUP):
                    nc.vector.bn_stats(stats2[:, t], total[:, g % DEEP, t]).then_inc(totals, 1)
                dve.wait_ge(totals, DVE_STEPS * g + 1 + GROUP)
                for t in range(GROUP):
                    nc.vector.bn_aggr(mean_var2[:, g % DEEP, t], stats2[:, t]).then_inc(totals, 1)
                if g >= 1:
                    make_shift(g - 1)
            make_shift(GROUPS - 1)

        @block.scalar
        def _(act):
            for g in range(GROUPS):
                act.wait_ge(shifts_made, g + 1)
                for t in range(GROUP):
                    nc.scalar.activation(first[:, g, t], total[:, g % DEEP, t], ACT.Identity, scale=rstd2[:, g % DEEP, t:t + 1],
                                         bias=shift2[:, g % DEEP, t:t + 1]).then_inc(normed, 1)


def build_program(nc, a):
    with ExitStack() as ctx:
        PASSED[0] = ctx.enter_context(nc.semaphore("passed"))
        make_moe_buffers(nc, a, ctx)
        build_attention(nc, a)
        build_moe(nc, a, ctx)


def kernel(L0_attn_x, L0_attn_Wq, L0_attn_bq, L0_attn_Wk, L0_attn_bk, L0_attn_Wv, L0_attn_bv, L0_attn_Wo, L0_attn_bo,
           L0_attn_head_mask, L0_ffn_Wfc_s, L0_ffn_bfc_s, L0_ffn_Wproj_s, L0_ffn_bproj_s, L0_ffn_Wr, L0_ffn_Wfc,
           L0_ffn_bfc, L0_ffn_Wproj, L0_ffn_bproj):
    import numpy as np
    import concourse.bacc as bacc
    from concourse.bass_utils import run_bass_kernel_spmd

    def by_dim(w):
        return np.asarray(w).reshape(HEADS, DH, -1).transpose(1, 0, 2).reshape(D, -1)

    def by_quad(w):
        return np.asarray(w).reshape(2, 2, 4, DH, -1).transpose(1, 0, 2, 3, 4).reshape(D, -1)

    def by_column_tile(w):
        w = np.asarray(w)
        n = w.shape[0] // HEADS
        return w.reshape(2, 2, 4, n, -1).transpose(0, 2, 1, 3, 4).reshape(w.shape[0], -1)

    x = np.asarray(L0_attn_x).reshape(TOKENS, D)

    def with_shared(routed, shared):
        return np.concatenate([np.asarray(routed), np.asarray(shared)[None]])

    w_fc = with_shared(L0_ffn_Wfc, L0_ffn_Wfc_s)
    w_proj = with_shared(L0_ffn_Wproj, L0_ffn_Wproj_s)
    arrays = {
        "x": x,
        "x_t": x.T,
        "wq_t": by_dim(L0_attn_Wq).T,
        "wk_t": by_dim(L0_attn_Wk).T,
        "wv_t": by_quad(L0_attn_Wv).T,
        "wo_t": by_column_tile(np.asarray(L0_attn_Wo).T),
        "bq": by_dim(L0_attn_bq),
        "bk": by_dim(L0_attn_bk),
        "bv": by_column_tile(L0_attn_bv),
        "mask": by_column_tile(L0_attn_head_mask).reshape(HEADS),
        "bo": np.asarray(L0_attn_bo),
        "w_fc": w_fc.transpose(1, 0, 2),
        "b_fc": with_shared(L0_ffn_bfc, L0_ffn_bfc_s),
        "b_units": with_shared(L0_ffn_bfc, L0_ffn_bfc_s).reshape(ALL, CHUNKS, P).transpose(2, 0, 1),
        "w_proj": w_proj.reshape(ALL, CHUNKS, P, D).transpose(2, 0, 1, 3).reshape(P, ALL, HIDDEN),
        "w_r": np.asarray(L0_ffn_Wr),
        "b_proj": with_shared(L0_ffn_bproj, L0_ffn_bproj_s),
    }
    nc = bacc.Bacc("TRN2", target_bir_lowering=False, num_devices=1)
    maps, a = {}, {}
    for name, array in arrays.items():
        maps[f"in_{name}"] = np.ascontiguousarray(array)
        a[name] = nc.dram_tensor(f"in_{name}", maps[f"in_{name}"].shape, F32, kind="ExternalInput").ap()
    a["out"] = nc.dram_tensor("result", [TOKENS, D], F32, kind="ExternalOutput").ap()
    build_program(nc, a)
    r = run_bass_kernel_spmd(nc, [maps], core_ids=[0])
    return r.results[0]["result"].reshape(BATCHES, SEQ, D)
```

```python
from contextlib import ExitStack

import concourse.bass as bass
from concourse import mybir

F32 = mybir.dt.float32
BF16 = mybir.dt.bfloat16
ACT = mybir.ActivationFunctionType
ALU = mybir.AluOpType
AX_X = mybir.AxisListType.X

P = 128
D = 128
HEADS = 16
DH = D // HEADS
BATCHES = 16
SEQ = 256
TOKENS = BATCHES * SEQ
TILES = SEQ // P
HALF = HEADS // 2
PAIRS = HEADS // 2
QUADS = HEADS // 4
EPS = 1e-5
SCORE_SCALE = float(DH) ** -0.5
ROW_MAX = 6 * DH
TURN_STEP = BATCHES + 2
TURNS = {1: (0, 1), 4: (2, 3), 7: (4, 5), 9: (6,)}
EARLY_GROUPS = 7
FIRST_LOOP, LOOPS = 2, 5


class Batch:

    def __init__(self, u, c, back):
        self.half = u + (c - back) // 2
        self.par = (c - back) % 2
        self.n = self.half * 2 + self.par
        self.fixed = isinstance(u, int)

    def exists(self):
        return not self.fixed or 0 <= self.n < BATCHES

    def since(self, n):
        return not self.fixed or self.n >= n


def wait_first(eng, passed, semaphore, value):
    eng.wait_ge(semaphore, value)
    if not isinstance(value, int):
        eng.sem_inc(passed, 1)


def run_steps(eng, step):
    for t in range(2 * FIRST_LOOP):
        step(t // 2, t % 2)
    with eng.Fori(FIRST_LOOP, FIRST_LOOP + LOOPS) as u:
        step(u, 0)
        step(u, 1)
    for t in range(2 * (FIRST_LOOP + LOOPS), BATCHES + 3):
        step(t // 2, t % 2)


def build_attention(nc, a):
    passed = a["passed"]
    ctx = ExitStack()
    with ctx:
        def sb(name, shape, dt=F32):
            return ctx.enter_context(nc.sbuf_tensor(name, shape, dt))

        def ps(name, shape, dt=F32):
            return ctx.enter_context(nc.psum_tensor(name, shape, dt))

        def sem(name):
            return ctx.enter_context(nc.semaphore(name))

        q_rows = nc.dram_tensor("q_rows", [2, ROW_MAX + 3, HEADS, SEQ], BF16, kind="Internal").ap()
        k_rows = nc.dram_tensor("k_rows", [2, ROW_MAX, HEADS, SEQ], BF16, kind="Internal").ap()

        wq = sb("wq", [D, D])
        wk = sb("wk", [D, D])
        wv = sb("wv", [D, D])
        wo = sb("wo", [D, D])
        bq = sb("bq", [D, 1])
        bk = sb("bk", [D, 1])
        bv = sb("bv", [D, 1])
        mask_col = sb("mask_col", [D, 1])
        mask_row = sb("mask_row", [P, HEADS])
        bo_row = sb("bo_row", [P, D])
        bv_masked = sb("bv_masked", [D, P])
        out_bias = sb("out_bias", [P, D])
        ident = sb("ident", [P, P])
        ident16 = sb("ident16", [P, P], BF16)
        zero_rows = sb("zero_rows", [3, SEQ], BF16)
        one_rows = sb("one_rows", [3, SEQ], BF16)
        minus_half = sb("minus_half", [P, TILES])
        warm = sb("warm", [P, TILES])

        x_t = sb("x_t", [D, 2, SEQ])
        x_in = sb("x_in", [P, 2, TILES, D])
        xb = sb("xb", [P, TILES, D])
        z = sb("z", [P, TILES, D])
        qk = sb("qk", [D, 2, SEQ])
        qk_rest = sb("qk_rest", [D, 2, SEQ])
        qk_parts = sb("qk_parts", [D, 2, 2, 3, SEQ], BF16)
        q_stack = sb("q_stack", [P, 2, HEADS, SEQ], BF16)
        k_stack = sb("k_stack", [P, 2, HEADS, SEQ], BF16)
        v_aug = sb("v_aug", [P, 2, TILES, HEADS, 32])
        row_max = sb("row_max", [P, HEADS, TILES])
        max_rest = sb("max_rest", [P, 2, HALF * TILES])
        max_parts = sb("max_parts", [P, 2, 3, HALF * TILES], BF16)
        max_t = sb("max_t", [3 * HALF * TILES, 2, P], BF16)
        probs = sb("probs", [P, 4, 2, TILES, SEQ])
        av = sb("av", [P, 2, SEQ])
        sum_inv = sb("sum_inv", [P, 2 * HEADS])
        sum_scale = sb("sum_scale", [P, 2 * HEADS])
        heads_out = sb("heads_out", [P, TILES, D])
        heads_t = sb("heads_t", [D, SEQ])
        stats = sb("stats", [P, TILES, 6])
        mean_var = sb("mean_var", [P, TILES, 2])
        var_eps = sb("var_eps", [P, TILES])
        rstd = sb("rstd", [P, TILES])
        scaled_mean = sb("scaled_mean", [P, TILES])
        shift = sb("shift", [P, TILES])
        x1_all = a["x1_all"]

        s1_ps = ps("s1_ps", [P, 2, TILES, SEQ])
        st_ps = ps("st_ps", [P, 2, 2, TILES, SEQ])
        av_ps = ps("av_ps", [P, 2, SEQ])
        misc_ps = ps("misc_ps", [P, 512])
        bias_sum = av_ps[:, 0, 0:D]
        turned_rows = s1_ps[:].rearrange("p b t k -> p b (t k)").bitcast(F16)
        misc16 = misc_ps[:].bitcast(BF16)

        qk_weights_in = sem("qk_weights_in")
        weights_in = sem("weights_in")
        bcast_in = sem("bcast_in")
        consts_made = sem("consts_made")
        k_cleared = sem("k_cleared")
        zeros_out = sem("zeros_out")
        bv_made = sem("bv_made")
        bias_ps = sem("bias_ps")
        warmed = sem("warmed")
        bias_made = sem("bias_made")
        xt_in = [sem("xt_in0"), sem("xt_in1")]
        x_loaded = [sem("x_loaded0"), sem("x_loaded1")]
        qk_projected = sem("qk_projected")
        qk_evacuated = sem("qk_evacuated")
        qk_split = sem("qk_split")
        rows_out = [sem("rows_out0"), sem("rows_out1")]
        stacks_in = [[sem(f"stacks_in{par}{half}") for half in range(2)] for par in range(2)]
        scores_ready = sem("scores_ready")
        max_done = sem("max_done")
        max_split = sem("max_split")
        max_turned = sem("max_turned")
        max_evacuated = sem("max_evacuated")
        max_in = [sem("max_in0"), sem("max_in1")]
        shifted_ready = sem("shifted_ready")
        exp_done = sem("exp_done")
        v_projected = sem("v_projected")
        v_evacuated = sem("v_evacuated")
        quad_done = sem("quad_done")
        av_evacuated = sem("av_evacuated")
        av_turned = sem("av_turned")
        normalised = sem("normalised")
        heads_turned = sem("heads_turned")
        heads_evacuated = sem("heads_evacuated")
        xb_made = sem("xb_made")
        y_ready = sem("y_ready")
        z_made = sem("z_made")
        stats_done = sem("stats_done")
        scale_done = sem("scale_done")
        x1_made = sem("x1_made")

        block = ctx.enter_context(nc.Block())

        @block.sync
        def _(sp):
            def load_xt(b):
                sp.dma_start(x_t[:, b.par], a["x_t"][:, bass.ds(b.n * SEQ, SEQ)]).then_inc(xt_in[b.par], 16)

            load_xt(Batch(0, 0, 0))
            for tile, name in ((wq, "wq_t"), (wk, "wk_t"), (bq, "bq"), (bk, "bk")):
                sp.dma_start(tile[:], a[name]).then_inc(qk_weights_in, 16)
            for tile, name in ((bv, "bv"), (wo, "wo_t"), (wv, "wv_t")):
                sp.dma_start(tile[:], a[name]).then_inc(weights_in, 16)
            sp.dma_start(mask_col[:], a["mask"].unsqueeze(1).to_broadcast([HEADS, DH])).then_inc(weights_in, 16)
            sp.dma_start(mask_row[:], a["mask"].partition_broadcast(P)).then_inc(bcast_in, 16)
            sp.dma_start(bo_row[:], a["bo"].partition_broadcast(P)).then_inc(bcast_in, 16)
            sp.wait_ge(consts_made, 4)
            sp.wait_ge(k_cleared, 1)
            for par in range(2):
                sp.dma_start(q_rows[par, ROW_MAX:ROW_MAX + 3],
                             zero_rows[:].unsqueeze(1).to_broadcast([3, HEADS, SEQ])).then_inc(zeros_out, 16)
                sp.dma_start(k_stack[ROW_MAX:ROW_MAX + 3, par],
                             one_rows[:].unsqueeze(1).to_broadcast([3, HEADS, SEQ])).then_inc(zeros_out, 16)
            sp.wait_ge(zeros_out, 64)

            def load_max(b, half):
                sp.wait_ge(max_evacuated, 2 * b.n + half + 1)
                for part in range(3):
                    rows = HALF * TILES
                    sp.dma_start(q_stack[ROW_MAX + part:ROW_MAX + part + 1, b.par, half * HALF:(half + 1) * HALF, :]
                                 .rearrange("o h (t q) -> o (h t) q", t=TILES),
                                 max_t[part * rows:(part + 1) * rows, half, :]).then_inc(max_in[half], 16)

            def load_stacks(b, half):
                heads = slice(half * HALF, (half + 1) * HALF)
                if b.since(2):
                    sp.wait_ge(shifted_ready, PAIRS * (b.n - 2) + (half + 1) * PAIRS // 2)
                sp.dma_start(q_stack[0:ROW_MAX + 3, b.par, heads], q_rows[b.par, :, heads])\
                  .then_inc(stacks_in[b.par][half], 16)
                sp.dma_start(k_stack[0:ROW_MAX, b.par, heads], k_rows[b.par, :, heads])\
                  .then_inc(stacks_in[b.par][half], 16)

            def step(u, c):
                b = Batch(u, c, 2)
                if b.exists():
                    load_max(b, 1)
                b = Batch(u, c, -1)
                if b.exists():
                    if b.since(2):
                        sp.wait_ge(v_projected, b.n - 1)
                    load_xt(b)
                b = Batch(u, c, 2)
                if b.exists():
                    if b.since(2):
                        sp.wait_ge(xb_made, b.n - 1)
                    sp.dma_start(x_in[:, b.par], a["x"][bass.ds(b.n * SEQ, SEQ), :].rearrange("(t p) d -> p t d", p=P))\
                      .then_inc(x_loaded[b.par], 16)
                b = Batch(u, c, 0)
                if b.exists():
                    q_to = q_rows[b.par, 0:ROW_MAX].rearrange("(r d) h t -> (d h) r t", r=6)
                    k_to = k_rows[b.par].rearrange("(r d) h t -> (d h) r t", r=6)
                    q_part, k_part = qk_parts[:, b.par, 0], qk_parts[:, b.par, 1]
                    if b.since(2):
                        for half in range(2):
                            sp.wait_ge(stacks_in[b.par][half], 32 * b.half)
                    sp.wait_ge(qk_split, 4 * b.n + 1)
                    for r in range(3):
                        sp.dma_start(k_to[:, r:r + 1], k_part[:, 0:1]).then_inc(rows_out[b.par], 16)
                    sp.wait_ge(qk_split, 4 * b.n + 3)
                    for r in range(3, 5):
                        sp.dma_start(k_to[:, r:r + 1], k_part[:, 1:2]).then_inc(rows_out[b.par], 16)
                    sp.wait_ge(qk_split, 4 * b.n + 4)
                    sp.dma_start(q_to[:, 0:3], q_part[:, 0:3]).then_inc(rows_out[b.par], 16)
                    sp.dma_start(q_to[:, 3:5], q_part[:, 0:2]).then_inc(rows_out[b.par], 16)
                    sp.dma_start(q_to[:, 5:6], q_part[:, 0:1]).then_inc(rows_out[b.par], 16)
                    sp.dma_start(k_to[:, 5:6], k_part[:, 2:3]).then_inc(rows_out[b.par], 16)
                b = Batch(u, c, 1)
                if b.exists():
                    load_max(b, 0)
                b = Batch(u, c, 0)
                if b.exists():
                    sp.wait_ge(rows_out[b.par], 144 * (b.half + 1))
                    load_stacks(b, 0)
                    load_stacks(b, 1)
                load_for_moe(sp, a, u, c)

            run_steps(sp, step)

        @block.gpsimd
        def _(pool):
            make_empty_row(nc, pool, a)
            nc.gpsimd.memset(zero_rows[:], 0.0).then_inc(consts_made, 1)
            nc.gpsimd.memset(one_rows[:], 1.0).then_inc(consts_made, 1)
            nc.gpsimd.memset(ident[:], 0.0).then_inc(consts_made, 1)
            nc.gpsimd.memset(q_stack[:].rearrange("p b h t -> p (b h t)").bitcast(F32), 0.0).then_inc(consts_made, 1)
            nc.gpsimd.memset(minus_half[:], -0.5).then_inc(consts_made, 1)
            pool.wait_ge(consts_made, 5)
            nc.gpsimd.affine_select(out=ident[:], in_=ident[:], compare_op=ALU.not_equal, fill=1.0, base=0,
                                    pattern=[[-1, P]], channel_multiplier=1).then_inc(consts_made, 1)
            pool.wait_ge(consts_made, 6)
            nc.gpsimd.tensor_copy(ident16[:], ident[:]).then_inc(consts_made, 1)

            def split_max(b, half):
                heads = slice(half * HALF, (half + 1) * HALF)
                largest = row_max[:, heads].rearrange("p h t -> p (h t)")
                rest, parts = max_rest[:, half], max_parts[:, half]
                done = (2 * b.n + half) * 4
                wait_first(pool, passed, max_done, HEADS * b.n + (half + 1) * HALF)
                if b.since(1):
                    wait_first(pool, passed, max_turned, 2 * b.n + half - 1)
                nc.gpsimd.tensor_scalar(parts[:, 0], largest, 1.0, 1.0, ALU.mult, ALU.mult).then_inc(max_split, 1)
                pool.wait_ge(max_split, done + 1)
                nc.gpsimd.tensor_tensor(rest, largest, parts[:, 0], ALU.subtract).then_inc(max_split, 1)
                wait_first(pool, passed, max_split, done + 2)
                nc.gpsimd.tensor_scalar(parts[:, 1], rest, 1.0, 1.0, ALU.mult, ALU.mult).then_inc(max_split, 1)
                pool.wait_ge(max_split, done + 3)
                nc.gpsimd.tensor_tensor(parts[:, 2], rest, parts[:, 1], ALU.subtract).then_inc(max_split, 1)

            def split_qk(b):
                parts = qk_parts[:, b.par]
                wait_first(pool, passed, qk_evacuated, 2 * b.n + 2)
                if b.since(2):
                    wait_first(pool, passed, rows_out[b.par], 144 * b.half)
                nc.gpsimd.tensor_scalar(parts[:, :, 0], qk[:], 1.0, 1.0, ALU.mult, ALU.mult).then_inc(qk_split, 1)
                pool.wait_ge(qk_split, 4 * b.n + 1)
                nc.gpsimd.tensor_tensor(qk_rest[:], qk[:], parts[:, :, 0], ALU.subtract).then_inc(qk_split, 1)
                wait_first(pool, passed, qk_split, 4 * b.n + 2)
                nc.gpsimd.tensor_scalar(parts[:, :, 1], qk_rest[:], 1.0, 1.0, ALU.mult, ALU.mult)\
                  .then_inc(qk_split, 1)
                pool.wait_ge(qk_split, 4 * b.n + 3)
                nc.gpsimd.tensor_tensor(parts[:, :, 2], qk_rest[:], parts[:, :, 1], ALU.subtract)\
                  .then_inc(qk_split, 1)

            def step(u, c):
                b = Batch(u, c, 2)
                if b.exists():
                    split_max(b, 1)
                b = Batch(u, c, 0)
                if b.exists():
                    split_qk(b)
                    if b.fixed and b.n == 0:
                        make_routing_constants(nc, pool, a)
                b = Batch(u, c, 3)
                if b.exists():
                    pool.wait_ge(x_loaded[b.par], 16 * (b.half + 1))
                    if b.since(1):
                        pool.wait_ge(z_made, b.n)
                    else:
                        pool.wait_ge(bias_made, 1)
                    nc.gpsimd.tensor_tensor(xb[:], x_in[:, b.par], out_bias[:].unsqueeze(1).to_broadcast([P, TILES, D]),
                                            ALU.add).then_inc(xb_made, 1)
                b = Batch(u, c, 1)
                if b.exists():
                    split_max(b, 0)
                b = Batch(u, c, 3)
                if b.exists():
                    wait_first(pool, passed, stats_done, 4 * b.n + 4)
                    if b.since(1):
                        wait_first(pool, passed, x1_made, 2 * b.n)
                    nc.gpsimd.tensor_scalar(var_eps[:], mean_var[:, :, 1], EPS, None, ALU.add).then_inc(scale_done, 1)
                    pool.wait_ge(scale_done, 4 * b.n + 1)
                    nc.gpsimd.tensor_tensor(rstd[:], var_eps[:], minus_half[:], ALU.pow).then_inc(scale_done, 1)
                    pool.wait_ge(scale_done, 4 * b.n + 2)
                    nc.gpsimd.tensor_tensor(scaled_mean[:], mean_var[:, :, 0], rstd[:], ALU.mult)\
                      .then_inc(scale_done, 1)
                    wait_first(pool, passed, scale_done, 4 * b.n + 3)
                    nc.gpsimd.tensor_scalar(shift[:], scaled_mean[:], -1.0, 1.0, ALU.mult, ALU.mult)\
                      .then_inc(scale_done, 1)


            run_steps(pool, step)

        @block.scalar
        def _(act):
            def exp_pair(b, p):
                act.wait_ge(shifted_ready, PAIRS * b.n + p + 1)
                if b.since(1) or p >= 4:
                    act.wait_ge(quad_done, 4 * b.n + p // 2 - 1)
                nc.scalar.activation(probs[:, p % 4], st_ps[:, p % 2], ACT.Exp, scale=SCORE_SCALE)\
                  .then_inc(exp_done, 1)

            def evacuate_max(b, half):
                rows = 3 * HALF * TILES
                act.wait_ge(max_turned, 2 * b.n + half + 1)
                if b.since(1):
                    act.wait_ge(max_in[half], 48 * b.n)
                nc.scalar.activation(max_t[:, half], misc16[0:rows, 0:P], ACT.Copy).then_inc(max_evacuated, 1)

            def step(u, c):
                b = Batch(u, c, 0)
                if b.exists():
                    act.wait_ge(qk_projected, b.n + 1)
                    if b.since(1):
                        act.wait_ge(qk_split, 4 * b.n)
                    for side, bias in ((0, bq), (1, bk)):
                        nc.scalar.activation(qk[:, side], misc_ps[:, side * SEQ:(side + 1) * SEQ], ACT.Identity,
                                             bias=bias[:]).then_inc(qk_evacuated, 1)
                now, last = Batch(u, c, 2), Batch(u, c, 3)
                if now.exists():
                    exp_pair(now, 0)
                    evacuate_max(now, 1)
                if last.exists():
                    act.wait_ge(quad_done, 4 * last.n + 4)
                    if last.since(1):
                        act.wait_ge(av_turned, last.n)
                    nc.scalar.activation(av[:], av_ps[:], ACT.Copy).then_inc(av_evacuated, 1)
                b = Batch(u, c, 1)
                if b.exists():
                    act.wait_ge(v_projected, b.n + 1)
                    if b.since(2):
                        act.wait_ge(quad_done, 4 * (b.n - 1))
                    for s in range(2):
                        to = v_aug[:, b.par, :, s * HALF:(s + 1) * HALF, 16 * s:16 * s + DH]
                        of = misc_ps[:, 0:SEQ].rearrange("p (t s h d) -> p t s h d", t=TILES, s=2, d=DH)[:, :, s]
                        nc.scalar.activation(to, of, ACT.Copy).then_inc(v_evacuated, 1)
                if now.exists():
                    exp_pair(now, 1)
                    exp_pair(now, 2)
                if last.exists():
                    act.wait_ge(heads_turned, last.n + 1)
                    if last.since(1):
                        act.wait_ge(y_ready, last.n)
                    nc.scalar.activation(heads_t[:], misc_ps[:, 0:SEQ], ACT.Copy).then_inc(heads_evacuated, 1)
                if now.exists():
                    exp_pair(now, 3)
                    exp_pair(now, 4)
                if b.exists():
                    evacuate_max(b, 0)
                if now.exists():
                    exp_pair(now, 5)
                    exp_pair(now, 6)
                if now.exists():
                    exp_pair(now, 7)
                if last.exists():
                    act.wait_ge(scale_done, 4 * last.n + 4)
                    for t in range(TILES):
                        tile = last.n * TILES + t
                        to = x1_all[:, tile] if last.fixed else x1_all[:, bass.ds(tile, 1)].rearrange("p o d -> p (o d)")
                        nc.scalar.activation(to, z[:, t], ACT.Identity,
                                             scale=rstd[:, t:t + 1], bias=shift[:, t:t + 1]).then_inc(x1_made, 1)

            act.wait_ge(consts_made, 5)
            nc.scalar.activation(warm[:], minus_half[:], ACT.Exp).then_inc(warmed, 1)
            act.wait_ge(qk_weights_in, 64)
            run_steps(act, step)

        @block.vector
        def _(dve):
            nc.vector.memset(k_stack[:].rearrange("p b h t -> p (b h t)").bitcast(F32), 0.0).then_inc(k_cleared, 1)
            nc.vector.memset(v_aug[:], 0.0).then_inc(bv_made, 1)
            dve.wait_ge(bv_made, 1)
            for s in range(2):
                nc.vector.memset(v_aug[:, :, :, s * HALF:(s + 1) * HALF, 16 * s + DH:16 * s + DH + 1], 1.0)\
                  .then_inc(bv_made, 1)
            dve.wait_ge(weights_in, 64)
            nc.vector.tensor_tensor(bv_masked[:], bv[:].to_broadcast([D, P]), mask_col[:].to_broadcast([D, P]), ALU.mult)\
              .then_inc(bv_made, 1)
            dve.wait_ge(bias_ps, 1)
            dve.wait_ge(bcast_in, 32)
            nc.vector.tensor_tensor(out_bias[:], bias_sum, bo_row[:], ALU.add).then_inc(bias_made, 1)

            def maxima(b, heads):
                for h in heads:
                    dve.wait_ge(scores_ready, HEADS * b.n + h + 1)
                    if h % HALF == 0 and b.since(1):
                        dve.wait_ge(max_split, (2 * b.n + h // HALF - 1) * 4)
                    nc.vector.tensor_reduce(row_max[:, h], s1_ps[:, h % 2], AX_X, ALU.max, negate=True)\
                      .then_inc(max_done, 1)

            def step(u, c):
                now, last = Batch(u, c, 1), Batch(u, c, 3)
                cutting = isinstance(u, int) and 2 * u + c == TURN_STEP - 1
                turning = isinstance(u, int) and 2 * u + c == TURN_STEP
                if now.exists():
                    maxima(now, range(5))
                if cutting:
                    dve.wait_ge(x1_made, 2 * (TURN_STEP - 4))
                    for g in range(3):
                        cut_rows(nc, dve, a, g)
                if turning:
                    for g in range(4):
                        take_turned(nc, dve, a, turned_rows, g)
                if last.exists():
                    blocks = misc_ps[:].rearrange("p (n r) -> p n r", r=16)
                    dve.wait_ge(av_turned, last.n + 1)
                    if last.since(1):
                        dve.wait_ge(heads_turned, last.n)
                    nc.vector.reciprocal(sum_inv[:].unsqueeze(2), blocks[:, :, DH:DH + 1]).then_inc(normalised, 1)
                    dve.wait_ge(normalised, 3 * last.n + 1)
                    nc.vector.tensor_tensor(sum_scale[:].rearrange("p (t h) -> p t h", t=TILES),
                                            sum_inv[:].rearrange("p (t h) -> p t h", t=TILES),
                                            mask_row[:].unsqueeze(1).to_broadcast([P, TILES, HEADS]), ALU.mult)\
                      .then_inc(normalised, 1)
                    dve.wait_ge(normalised, 3 * last.n + 2)
                    nc.vector.tensor_tensor(heads_out[:].rearrange("p t (h d) -> p (t h) d", d=DH), blocks[:, :, 0:DH],
                                            sum_scale[:].unsqueeze(2).to_broadcast([P, 2 * HEADS, DH]), ALU.mult)\
                      .then_inc(normalised, 1)
                if now.exists():
                    maxima(now, range(5, 13))
                if cutting:
                    for g in range(3, EARLY_GROUPS):
                        cut_rows(nc, dve, a, g)
                if turning:
                    for g in range(4, EARLY_GROUPS - 1):
                        take_turned(nc, dve, a, turned_rows, g)
                if last.exists():
                    dve.wait_ge(y_ready, last.n + 1)
                    if last.since(1):
                        dve.wait_ge(scale_done, 4 * last.n)
                        dve.wait_ge(x1_made, 2 * last.n)
                    dve.wait_ge(xb_made, last.n + 1)
                    nc.vector.tensor_tensor(z[:], misc_ps[:, 0:SEQ].rearrange("p (t d) -> p t d", d=D), xb[:], ALU.add)\
                      .then_inc(z_made, 1)
                    dve.wait_ge(z_made, last.n + 1)
                    for t in range(TILES):
                        nc.vector.bn_stats(stats[:, t], z[:, t]).then_inc(stats_done, 1)
                    wait_first(dve, passed, stats_done, 4 * last.n + 2)
                    for t in range(TILES):
                        nc.vector.bn_aggr(mean_var[:, t], stats[:, t]).then_inc(stats_done, 1)
                if now.exists():
                    maxima(now, range(13, HEADS))
                if turning:
                    take_turned(nc, dve, a, turned_rows, EARLY_GROUPS - 1)

            run_steps(dve, step)

        @block.tensor
        def _(pe):
            def make_bias_sum():
                pe.wait_ge(bv_made, 4)
                pe.wait_ge(weights_in, 64)
                nc.tensor.matmul(bias_sum, bv_masked[:], wo[:], start=True, stop=True).then_inc(bias_ps, 1)
                pe.wait_ge(consts_made, 7)

            def scores(b, h):
                if h % HALF == 0:
                    pe.wait_ge(stacks_in[b.par][h // HALF], 32 * (b.half + 1))
                if b.since(1) or h >= 2:
                    pe.wait_ge(max_done, HEADS * b.n + h - 1)
                for t in range(TILES):
                    mm = nc.tensor.matmul(s1_ps[:, h % 2, t], q_stack[:, b.par, h, t * P:(t + 1) * P], k_stack[:, b.par, h],
                                          start=True, stop=True)
                mm.then_inc(scores_ready, 1)

            def shifted_scores(b, h):
                p = h // 2
                if h % HALF == 0:
                    pe.wait_ge(max_in[h // HALF], 48 * (b.n + 1))
                if h % 2 == 0 and (b.since(1) or p >= 2):
                    pe.wait_ge(exp_done, PAIRS * b.n + p - 1)
                for t in range(TILES):
                    mm = nc.tensor.matmul(st_ps[:, p % 2, h % 2, t], k_stack[:, b.par, h, t * P:(t + 1) * P],
                                          q_stack[:, b.par, h], start=True, stop=True)
                if h % 2:
                    mm.then_inc(shifted_ready, 1)

            def quad(b, g):
                r, s = g // 2, g % 2
                pe.wait_ge(exp_done, PAIRS * b.n + 2 * g + 2)
                if g == 0:
                    pe.wait_ge(v_evacuated, 2 * b.n + 2)
                    if b.since(1):
                        pe.wait_ge(av_evacuated, b.n)
                    else:
                        pe.wait_ge(bias_made, 1)
                for t in range(TILES):
                    for j in range(4):
                        mm = nc.tensor.matmul(av_ps[32 * j:32 * j + 32, r], v_aug[:, b.par, t, s * HALF + r * 4 + j],
                                              probs[:, (2 * g + j // 2) % 4, j % 2, t], start=(s == 0 and t == 0),
                                              stop=(s == 1 and t == 1))
                mm.then_inc(quad_done, 1)

            def turn_max(b, half):
                rows = 3 * HALF * TILES
                wait_first(pe, passed, max_split, (2 * b.n + half) * 4 + 4)
                nc.tensor.transpose(misc16[0:rows, 0:P], max_parts[:, half].rearrange("p r n -> p (r n)"), ident16[:])\
                  .then_inc(max_turned, 1)

            def step(u, c):
                new, now, late, last = (Batch(u, c, back) for back in range(4))
                turning = isinstance(u, int) and 2 * u + c == TURN_STEP
                for slot in range(HEADS):
                    if turning:
                        for g in TURNS.get(slot, ()):
                            turn_rows(nc, pe, a, turned_rows, g)
                    if slot == 0 and new.exists():
                        pe.wait_ge(xt_in[new.par], 16 * (new.half + 1))
                        if last.exists():
                            pe.wait_ge(z_made, last.n)
                        if late.exists():
                            pe.wait_ge(max_evacuated, 2 * late.n + 1)
                        elif now.exists():
                            pe.wait_ge(qk_evacuated, 2 * new.n)
                        nc.tensor.matmul(misc_ps[:, 0:SEQ], wq[:], x_t[:, new.par], start=True, stop=True)
                        nc.tensor.matmul(misc_ps[:, SEQ:2 * SEQ], wk[:], x_t[:, new.par], start=True, stop=True)\
                          .then_inc(qk_projected, 1)
                        if new.fixed and new.n == 0:
                            make_bias_sum()
                    if slot == 2 and late.exists():
                        if new.exists():
                            pe.wait_ge(qk_evacuated, 2 * new.n + 2)
                        else:
                            pe.wait_ge(max_evacuated, 2 * late.n + 1)
                            if last.exists():
                                pe.wait_ge(z_made, last.n)
                        turn_max(late, 1)
                    if slot == 2 and last.exists():
                        quad(last, 3)
                    if slot == 3 and now.exists():
                        if late.exists():
                            pe.wait_ge(max_evacuated, 2 * late.n + 2)
                        elif new.exists():
                            pe.wait_ge(qk_evacuated, 2 * new.n + 2)
                        for t in range(TILES):
                            mm = nc.tensor.matmul(misc_ps[:, t * D:(t + 1) * D], x_t[:, now.par, t * P:(t + 1) * P], wv[:],
                                                  start=True, stop=True)
                        mm.then_inc(v_projected, 1)
                    if slot == 5 and last.exists():
                        if now.exists():
                            pe.wait_ge(v_evacuated, 2 * now.n + 2)
                        elif late.exists():
                            pe.wait_ge(max_evacuated, 2 * late.n + 2)
                        else:
                            pe.wait_ge(z_made, last.n)
                        pe.wait_ge(av_evacuated, last.n + 1)
                        for t in range(TILES):
                            for r in range(2):
                                mm = nc.tensor.transpose(misc_ps[:, (t * 2 + r) * P:(t * 2 + r + 1) * P],
                                                         av[:, r, t * P:(t + 1) * P], ident[:])
                        mm.then_inc(av_turned, 1)
                    if slot == 8 and last.exists():
                        pe.wait_ge(normalised, 3 * last.n + 3)
                        for t in range(TILES):
                            mm = nc.tensor.transpose(misc_ps[:, t * P:(t + 1) * P], heads_out[:, t], ident[:])
                        mm.then_inc(heads_turned, 1)
                    if slot == 11 and now.exists():
                        if last.exists():
                            pe.wait_ge(heads_evacuated, last.n + 1)
                        else:
                            pe.wait_ge(v_evacuated, 2 * now.n + 2)
                        turn_max(now, 0)
                    if slot == 13 and last.exists():
                        pe.wait_ge(heads_evacuated, last.n + 1)
                        if now.exists():
                            pe.wait_ge(max_evacuated, 2 * now.n + 1)
                        for t in range(TILES):
                            mm = nc.tensor.matmul(misc_ps[:, t * D:(t + 1) * D], heads_t[:, t * P:(t + 1) * P], wo[:],
                                                  start=True, stop=True)
                        mm.then_inc(y_ready, 1)
                    if now.exists():
                        scores(now, slot)
                    if late.exists():
                        shifted_scores(late, slot)
                        if slot in (6, 10, 14):
                            quad(late, (slot - 6) // 4)

            pe.wait_ge(qk_weights_in, 64)
            run_steps(pe, step)


F16 = mybir.dt.float16
I32 = mybir.dt.int32
U32 = mybir.dt.uint32

EXPERTS = 8
SHARED = EXPERTS
ALL = EXPERTS + 1
HIDDEN = 512
CHUNKS = HIDDEN // P
FC, PROJ = 0, HIDDEN
BOTH = HIDDEN + CHUNKS * D
TOP = 2
TOKEN_TILES = TOKENS // P
GROUP = 4
GROUPS = TOKEN_TILES // GROUP
EARLY_PLACED = 1
EMPTY_TILES = 12
BLOCK = 2 * P
SLOT_BLOCKS = TOP * TOKENS // BLOCK + EXPERTS - 1
SLOT_TILES = 2 * SLOT_BLOCKS
ROW = D + 2
ROW16 = 2 * ROW
TABLE_LEN = -(-(SLOT_BLOCKS + 4) // 4) * 4
GATE, DEST = D, D + 1
NOWHERE = 1 << 20
X_UNIT = 64.0
W_UNIT = 2048.0
UNIT = X_UNIT * W_UNIT
ROUTING_CONSTS = 17
FAR_BELOW = -3.0e38


class Tile:

    def __init__(self, u, c, back, count):
        self.n = u * 4 + (c - back)
        self.buf = (c - back) % 4
        self.count = count
        self.fixed = isinstance(u, int)

    def exists(self):
        return not self.fixed or 0 <= self.n < self.count

    def since(self, n):
        return not self.fixed or self.n >= n


def run_tiles(eng, step, steps, loop_end):
    for s in range(8):
        step(s // 4, s % 4)
    with eng.Fori(2, loop_end) as u:
        for c in range(4):
            step(u, c)
    for s in range(4 * loop_end, steps):
        step(s // 4, s % 4)


def make_moe_buffers(nc, a, ctx):
    def sb(name, shape, dt=F32):
        return ctx.enter_context(nc.sbuf_tensor(name, shape, dt))

    a["x1_all"] = sb("x1_all", [P, TOKEN_TILES, D])
    a["w32_or_slots"] = sb("w32_or_slots", [P, max(ALL * BOTH, SLOT_TILES * ROW)])
    a["w32"] = a["w32_or_slots"][:, 0:ALL * BOTH].rearrange("p (e c) -> p e c", c=BOTH)
    a["rows1"] = sb("rows1", [P, TOKEN_TILES, ROW])
    a["rows2"] = sb("rows2", [P, TOKEN_TILES, ROW])
    a["b32"] = sb("b32", [P, ALL + 1, P])
    a["pick"] = sb("pick", [P, CHUNKS, P], F16)
    a["ident_h"] = sb("ident_h", [P, P], F16)
    a["before"] = sb("before", [P, P], BF16)
    a["ones16"] = sb("ones16", [P, P], BF16)
    a["counting"] = sb("counting", [P, TABLE_LEN], I32)
    a["number"] = sb("number", [P, TABLE_LEN])
    a["from_end"] = sb("from_end", [P, EXPERTS])
    a["block_start"] = sb("block_start", [P, TOKEN_TILES])
    a["not_first"] = sb("not_first", [P, EXPERTS, TOKEN_TILES])
    a["w_router"] = sb("w_router", [D, EXPERTS])
    a["router_in"] = ctx.enter_context(nc.semaphore("router_in"))
    a["routing_consts"] = ctx.enter_context(nc.semaphore("routing_consts"))
    a["empty_row"] = sb("empty_row", [P, ROW])
    a["slots"] = nc.dram_tensor("slots", [SLOT_TILES * P, ROW], F32, kind="Internal").ap()
    a["results"] = nc.dram_tensor("results", [TOP * TOKENS, D], F32, kind="Internal").ap()
    a["moe_weights_in"] = ctx.enter_context(nc.semaphore("moe_weights_in"))
    a["empty_made"] = ctx.enter_context(nc.semaphore("empty_made"))
    a["x16"] = sb("x16", [D, TOKEN_TILES, 2, P], F16)
    for name in ("x_high", "x_low", "x_turned", "rows_turned"):
        a[name] = ctx.enter_context(nc.semaphore(name))
    a["rows_placed"] = ctx.enter_context(nc.semaphore("rows_placed"))
    a["slots_emptied"] = ctx.enter_context(nc.semaphore("slots_emptied"))


def load_for_moe(sp, a, u, c):
    def weights(e):
        sp.dma_start(a["w32"][:, e, FC:FC + HIDDEN], a["w_fc"][:, e]).then_inc(a["moe_weights_in"], 16)
        sp.dma_start(a["w32"][:, e, PROJ:BOTH], a["w_proj"][:, e]).then_inc(a["moe_weights_in"], 16)

    def empty(lo, tiles):
        sp.dma_start(a["slots"][lo].rearrange("(s p) r -> p s r", p=P),
                     a["empty_row"][:].unsqueeze(1).to_broadcast([P, tiles, ROW])).then_inc(a["slots_emptied"], 16)

    after = FIRST_LOOP + LOOPS
    if not isinstance(u, int):
        if c == 0:
            weights(bass.ds(u - FIRST_LOOP, 1))
        else:
            empty(bass.ds((u - FIRST_LOOP) * (EMPTY_TILES * P), EMPTY_TILES * P), EMPTY_TILES)
    elif u >= after:
        step = 2 * (u - after) + c
        if LOOPS + step < ALL:
            weights(slice(LOOPS + step, LOOPS + step + 1))
        lo = (LOOPS + step) * EMPTY_TILES
        if lo < SLOT_TILES:
            hi = min(SLOT_TILES, lo + EMPTY_TILES)
            empty(slice(lo * P, hi * P), hi - lo)
    elif 2 * u + c == 3:
        sp.dma_start(a["w_router"][:], a["w_r"]).then_inc(a["router_in"], 16)
        sp.wait_ge(a["empty_made"], 2)


def make_routing_constants(nc, pool, a):
    ident_h, b32, before, ones16, pick, not_first, counting, number, from_end, block_start, rows1, rows2 = (
        a[k] for k in ("ident_h", "b32", "before", "ones16", "pick", "not_first", "counting", "number", "from_end",
                       "block_start", "rows1", "rows2"))
    routing_consts = a["routing_consts"]
    nc.gpsimd.memset(ident_h[:], 0.0).then_inc(routing_consts, 1)
    nc.gpsimd.memset(b32[:], 0.0).then_inc(routing_consts, 1)
    pool.wait_ge(routing_consts, 2)
    nc.gpsimd.affine_select(out=ident_h[:], in_=ident_h[:], compare_op=ALU.not_equal, fill=1.0, base=0,
                            pattern=[[-1, P]], channel_multiplier=1).then_inc(routing_consts, 1)
    nc.gpsimd.memset(before[:], 1.0).then_inc(routing_consts, 1)
    nc.gpsimd.memset(ones16[:], 1.0).then_inc(routing_consts, 1)
    nc.gpsimd.memset(pick[:], 0.0).then_inc(routing_consts, 1)
    nc.gpsimd.memset(not_first[:], 1.0).then_inc(routing_consts, 1)
    nc.gpsimd.iota(counting[:], pattern=[[1, TABLE_LEN]], base=0, channel_multiplier=0).then_inc(routing_consts, 1)
    nc.gpsimd.iota(rows1[:].bitcast(I32)[:, :, DEST:DEST + 1], pattern=[[P, TOKEN_TILES], [0, 1]], base=0,
                   channel_multiplier=1).then_inc(routing_consts, 1)
    nc.gpsimd.iota(rows2[:].bitcast(I32)[:, :, DEST:DEST + 1], pattern=[[P, TOKEN_TILES], [0, 1]], base=TOKENS,
                   channel_multiplier=1).then_inc(routing_consts, 1)
    pool.wait_ge(routing_consts, 10)
    nc.gpsimd.affine_select(out=before[:], in_=before[:], compare_op=ALU.is_gt, fill=0.0, base=0,
                            pattern=[[1, P]], channel_multiplier=-1).then_inc(routing_consts, 1)
    nc.gpsimd.memset(not_first[:, :, 0:1], 0.0).then_inc(routing_consts, 1)
    nc.gpsimd.tensor_copy(number[:], counting[:]).then_inc(routing_consts, 1)
    for n, row in enumerate((0, 32)):
        nc.gpsimd.affine_select(out=pick[:], in_=pick[:], compare_op=ALU.not_equal, fill=X_UNIT, base=-row,
                                pattern=[[-1, CHUNKS], [0, P]], channel_multiplier=1).then_inc(routing_consts, 1)
        pool.wait_ge(routing_consts, 14 + n)
    nc.gpsimd.tensor_scalar(from_end[:], number[:, 0:EXPERTS], -1.0, float(EXPERTS), ALU.mult, ALU.add)\
      .then_inc(routing_consts, 1)
    nc.gpsimd.tensor_scalar(block_start[:], number[:, 0:TOKEN_TILES], float(BLOCK), 0.0, ALU.mult, ALU.add)\
      .then_inc(routing_consts, 1)


def cut_rows(nc, dve, a, g):
    tiles = slice(g * GROUP, (g + 1) * GROUP)
    parts = a["rows1"][:].bitcast(F16)
    nc.vector.tensor_scalar(parts[:, tiles, 0:D], a["x1_all"][:, tiles], X_UNIT, 1.0, ALU.mult, ALU.mult)\
      .then_inc(a["x_high"], 1)
    dve.wait_ge(a["x_high"], g + 1)
    nc.vector.scalar_tensor_tensor(out=parts[:, tiles, D:2 * D], in0=a["x1_all"][:, tiles], scalar=X_UNIT,
                                   in1=parts[:, tiles, 0:D], op0=ALU.mult, op1=ALU.subtract).then_inc(a["x_low"], 1)


def turn_rows(nc, pe, a, turned, g):
    parts = a["rows1"][:].bitcast(F16)
    pe.wait_ge(a["routing_consts"], ROUTING_CONSTS)
    pe.wait_ge(a["x_low"], g + 1)
    if g >= 2:
        pe.wait_ge(a["x_turned"], g - 1)
    for k in range(GROUP):
        for part in range(2):
            mm = nc.tensor.transpose(turned[:, g % 2, (2 * k + part) * P:(2 * k + part + 1) * P],
                                     parts[:, g * GROUP + k, part * D:(part + 1) * D], a["ident_h"][:])
    mm.then_inc(a["rows_turned"], 1)


def take_turned(nc, dve, a, turned, g):
    dve.wait_ge(a["rows_turned"], g + 1)
    nc.vector.tensor_copy(a["x16"][:, g * GROUP:(g + 1) * GROUP].rearrange("p t k n -> p (t k n)"), turned[:, g % 2])\
      .then_inc(a["x_turned"], 1)


def make_empty_row(nc, pool, a):
    empty = a["empty_row"]
    nc.gpsimd.memset(empty[:], 0.0).then_inc(a["empty_made"], 1)
    pool.wait_ge(a["empty_made"], 1)
    nc.gpsimd.iota(empty[:].bitcast(I32)[:, DEST:DEST + 1], pattern=[[0, 1]], base=NOWHERE, channel_multiplier=1)\
      .then_inc(a["empty_made"], 1)


def build_moe(nc, a, ctx):
    def sb(name, shape, dt=F32):
        return ctx.enter_context(nc.sbuf_tensor(name, shape, dt))

    x1_all, w32, rows1, rows2, b32, pick, ident_h = (
        a[k] for k in ("x1_all", "w32", "rows1", "rows2", "b32", "pick", "ident_h"))
    w16 = sb("w16", [P, 2, ALL, BOTH], F16)
    b16 = sb("b16", [P, ALL + 1, P], F16)
    x16 = a["x16"]
    b_units = sb("b_units", [P, ALL, CHUNKS])
    slot_at = sb("slot_at", [P, TOP, TOKEN_TILES], U32)
    expert_of = sb("expert_of", [1, TABLE_LEN], I32)

    route_tokens(nc, a, dict(x1_all=x1_all, rows1=rows1, rows2=rows2, w32=w32, w16=w16, b32=b32, b16=b16, pick=pick, x16=x16,
                             ident_h=ident_h, slot_at=slot_at, expert_of=expert_of, b_units=b_units))
    shared_expert(nc, a, x1_all, rows1, rows2, w32, w16, b16, pick, x16, slot_at)
    routed_experts(nc, a, w16, b16, pick, ident_h, expert_of, b_units)
    add_and_normalise(nc, a, x1_all)


def place_rows(nc, a, rows, slot_at, k, tiles):
    for t in tiles:
        nc.gpsimd.indirect_dma_start(out=a["slots"][:, :], out_offset=bass.IndirectOffsetOnAxis(
            ap=slot_at[:, k, t:t + 1], axis=0), in_=rows[:, t], in_offset=None).then_inc(a["rows_placed"], 16)


def shared_fc_bias(nc, h_ps, b16, pick):
    nc.tensor.matmul(h_ps, b16[:, ALL], pick[:], start=True, stop=False)


def fc_matmuls(nc, h_ps, w16, e, x_hi, x_lo, width, onto_bias):
    for c in range(CHUNKS):
        lo, hi = FC + c * P, FC + (c + 1) * P
        to = h_ps[:, c * width:(c + 1) * width]
        nc.tensor.matmul(to, one_of(w16[:, 0], e, lo, hi), x_hi, start=not onto_bias, stop=False)
        nc.tensor.matmul(to, one_of(w16[:, 0], e, lo, hi), x_lo, start=False, stop=False)
        mm = nc.tensor.matmul(to, one_of(w16[:, 1], e, lo, hi), x_hi, start=False,
                              stop=(c == CHUNKS - 1 or not onto_bias))
    return mm


def proj_matmuls(nc, y_ps, w16, b16, pick, e, h_hi, h_lo, width):
    nc.tensor.matmul(y_ps, pick[:, 0, 0:P], one_of(b16, e, 0, D), start=True, stop=False)
    for c in range(CHUNKS):
        lo, hi = PROJ + c * D, PROJ + (c + 1) * D
        units = slice(c * width, c * width + P)
        nc.tensor.matmul(y_ps, h_hi[:, units], one_of(w16[:, 0], e, lo, hi), start=False, stop=False)
        nc.tensor.matmul(y_ps, h_hi[:, units], one_of(w16[:, 1], e, lo, hi), start=False, stop=False)
        mm = nc.tensor.matmul(y_ps, h_lo[:, units], one_of(w16[:, 0], e, lo, hi), start=False, stop=(c == CHUNKS - 1))
    return mm


def one_of(weights, e, lo, hi):
    if isinstance(e, int):
        return weights[:, e, lo:hi]
    return weights[:, bass.ds(e, 1), lo:hi].rearrange("p o c -> p (o c)")


def route_tokens(nc, a, t):
    x1_all, rows1, rows2, w32, w16, b32, b16, pick, x16, ident_h, slot_at, expert_of = (
        t[k] for k in ("x1_all", "rows1", "rows2", "w32", "w16", "b32", "b16", "pick", "x16", "ident_h", "slot_at",
                       "expert_of"))
    before, ones16, number, from_end, block_start, not_first = (
        a[k] for k in ("before", "ones16", "number", "from_end", "block_start", "not_first"))
    ctx = ExitStack()
    with ctx:
        def sb(name, shape, dt=F32):
            return ctx.enter_context(nc.sbuf_tensor(name, shape, dt))

        def ps(name, shape, dt=F32):
            return ctx.enter_context(nc.psum_tensor(name, shape, dt))

        def sem(name):
            return ctx.enter_context(nc.semaphore(name))

        TE = [P, TOKEN_TILES, EXPERTS]
        ET = [P, EXPERTS, TOKEN_TILES]
        w_r = a["w_router"]
        wr16 = sb("wr16", [D, 2, EXPERTS], F16)
        logits = sb("logits", TE)
        logits2 = sb("logits2", TE)
        best = sb("best", [P, TOP, TOKEN_TILES])
        equal = sb("equal", TE)
        score = sb("score", TE)
        first = sb("first", [P, TOKEN_TILES])
        hot = sb("hot", [P, TOP] + TE[1:])
        chosen = sb("chosen", TE, BF16)
        gap = sb("gap", [P, TOKEN_TILES])
        exp_gap = sb("exp_gap", [P, TOKEN_TILES])
        exp_sum = sb("exp_sum", [P, TOKEN_TILES])
        gate1 = sb("gate1", [P, TOKEN_TILES])
        in_tile = sb("in_tile", ET)
        up_to = sb("up_to", ET)
        filled = sb("filled", ET)
        blocks_of = sb("blocks_of", [P, EXPERTS])
        blocks_up_to = sb("blocks_up_to", [P, EXPERTS])
        block_base = sb("block_base", [P, EXPERTS])
        base = sb("base", ET)
        base2 = sb("base2", ET)
        place = sb("place", TE)
        at_expert = sb("at_expert", TE)
        slot_f = sb("slot_f", [P, TOP, TOKEN_TILES])
        passed_block = sb("passed_block", [1, TABLE_LEN, EXPERTS])
        expert_f = sb("expert_f", [1, TABLE_LEN])
        expert_capped = sb("expert_capped", [1, TABLE_LEN])

        turn_ps = ps("turn_ps", [P, 2, GROUP * P])
        turned16 = turn_ps[:].bitcast(F16)
        logit_ps = ps("logit_ps", [P, 512])
        before_ps = ps("before_ps", [P, 512])
        total_ps = ps("total_ps", [P, 512])

        rows_copied = sem("rows_copied")
        biases_in = sem("biases_in")
        router_split = sem("router_split")
        logits_ready = sem("logits_ready")
        routed = sem("routed")
        gap_made = sem("gap_made")
        gap_exp = sem("gap_exp")
        chosen_made = sem("chosen_made")
        counts_ready = sem("counts_ready")
        slots_known = sem("slots_known")
        weights_high = sem("weights_high")
        weights_low = sem("weights_low")

        block = ctx.enter_context(nc.Block())

        @block.sync
        def _(sp):
            sp.dma_start(t["b_units"][:], a["b_units"]).then_inc(biases_in, 16)
            for row in (0, 32):
                sp.dma_start(b32[row:row + CHUNKS, ALL], a["b_fc_shared"].rearrange("(c m) -> c m", m=P))\
                  .then_inc(biases_in, 16)
                sp.dma_start(b32[row:row + 1, 0:ALL], a["b_proj"].unsqueeze(0)).then_inc(biases_in, 16)
            sp.wait_ge(a["x_low"], GROUPS)
            sp.dma_start(rows2[:, :, 0:D], rows1[:, :, 0:D]).then_inc(rows_copied, 16)
            sp.wait_ge(rows_copied, 16)

        @block.gpsimd
        def _(pool):
            for n, (whole, cut, low) in enumerate(((w32[:, SHARED], w16[:, 0, SHARED], w16[:, 1, SHARED]),
                                                   (b32[32:64], b16[32:64], b16[32:64]))):
                pool.wait_ge(weights_high, n + 1)
                if n:
                    pool.wait_ge(weights_low, 2 * n)
                nc.gpsimd.tensor_scalar(whole, whole, W_UNIT, 1.0, ALU.mult, ALU.mult).then_inc(weights_low, 1)
                pool.wait_ge(weights_low, 2 * n + 1)
                nc.gpsimd.tensor_tensor(low, whole, cut, ALU.subtract).then_inc(weights_low, 1)
            pool.wait_ge(weights_low, 4)
            pool.wait_ge(a["slots_emptied"], 16 * -(-SLOT_TILES // EMPTY_TILES))
            pool.wait_ge(rows_copied, 16)
            for k, rows in enumerate((rows1, rows2)):
                pool.wait_ge(slots_known, k + 1)
                place_rows(nc, a, rows, slot_at, k, range(EARLY_PLACED))

        @block.scalar
        def _(act):
            act.wait_ge(a["router_in"], 16)
            nc.scalar.activation(wr16[:, 0], w_r[:], ACT.Copy, scale=W_UNIT).then_inc(router_split, 1)
            act.wait_ge(a["moe_weights_in"], 32 * ALL)
            act.wait_ge(biases_in, 80)
            nc.scalar.activation(w16[:, 0, SHARED], w32[:, SHARED], ACT.Copy, scale=W_UNIT).then_inc(weights_high, 1)
            nc.scalar.activation(b16[:], b32[:], ACT.Copy, scale=W_UNIT).then_inc(weights_high, 1)
            act.wait_ge(gap_made, 1)
            nc.scalar.activation(exp_gap[:], gap[:], ACT.Exp, scale=1.0 / UNIT).then_inc(gap_exp, 1)
            for e in range(0, EXPERTS, 2):
                nc.scalar.activation(w16[:, 0, e:e + 2], w32[:, e:e + 2], ACT.Copy, scale=W_UNIT)\
                  .then_inc(weights_high, 1)

        @block.tensor
        def _(pe):

            def router(g):
                pe.wait_ge(a["x_turned"], g + 1)
                pe.wait_ge(router_split, 2)
                for k in range(GROUP):
                    n = g * GROUP + k
                    to = logit_ps[:, n * EXPERTS:(n + 1) * EXPERTS]
                    nc.tensor.matmul(to, x16[:, n, 0], wr16[:, 0], start=True, stop=False)
                    nc.tensor.matmul(to, x16[:, n, 0], wr16[:, 1], start=False, stop=False)
                    mm = nc.tensor.matmul(to, x16[:, n, 1], wr16[:, 0], start=False, stop=True)
                mm.then_inc(logits_ready, 1)

            for g in range(EARLY_GROUPS // 2):
                router(g)
            for g in range(EARLY_GROUPS, GROUPS):
                turn_rows(nc, pe, a, turned16, g)
            for g in range(EARLY_GROUPS // 2, GROUPS):
                router(g)
            pe.wait_ge(chosen_made, 1)
            used = chosen[:].rearrange("p t e -> p (t e)")
            nc.tensor.matmul(before_ps[:, 0:TOKEN_TILES * EXPERTS], before[:], used, start=True, stop=True)\
              .then_inc(counts_ready, 1)
            nc.tensor.matmul(total_ps[:, 0:TOKEN_TILES * EXPERTS], ones16[:], used, start=True, stop=True)\
              .then_inc(counts_ready, 1)

        @block.vector
        def _(dve):
            done = [0]

            def then(instruction):
                instruction.then_inc(routed, 1)
                done[0] += 1
                dve.wait_ge(routed, done[0])

            dve.wait_ge(router_split, 1)
            nc.vector.scalar_tensor_tensor(out=wr16[:, 1], in0=w_r[:], scalar=W_UNIT, in1=wr16[:, 0], op0=ALU.mult,
                                           op1=ALU.subtract).then_inc(router_split, 1)
            for g in range(EARLY_GROUPS, GROUPS):
                cut_rows(nc, dve, a, g)
                take_turned(nc, dve, a, turned16, g)
            dve.wait_ge(logits_ready, GROUPS)
            then(nc.vector.tensor_copy(logits[:], logit_ps[:, 0:TOKEN_TILES * EXPERTS].rearrange("p (t e) -> p t e", e=EXPERTS)))
            for k, of in enumerate((logits, logits2)):
                if k == 1:
                    then(nc.vector.scalar_tensor_tensor(out=logits2[:], in0=hot[:, 0], scalar=FAR_BELOW, in1=logits[:],
                                                        op0=ALU.mult, op1=ALU.add))
                then(nc.vector.tensor_reduce(best[:, k], of[:], AX_X, ALU.max))
                if k == 1:
                    then(nc.vector.tensor_tensor(gap[:], best[:, 1], best[:, 0], ALU.subtract))
                    dve.sem_inc(gap_made, 1)
                then(nc.vector.tensor_tensor(equal[:], of[:], best[:, k].unsqueeze(2).to_broadcast(TE), ALU.is_equal))
                then(nc.vector.tensor_tensor(score[:], equal[:], from_end[:].unsqueeze(1).to_broadcast(TE), ALU.mult))
                then(nc.vector.tensor_reduce(first[:], score[:], AX_X, ALU.max))
                then(nc.vector.tensor_tensor(hot[:, k], score[:], first[:].unsqueeze(2).to_broadcast(TE), ALU.is_equal))
            then(nc.vector.tensor_tensor(chosen[:], hot[:, 0], hot[:, 1], ALU.add))
            dve.sem_inc(chosen_made, 1)
            dve.wait_ge(gap_exp, 1)
            then(nc.vector.tensor_scalar(exp_sum[:], exp_gap[:], UNIT, UNIT, ALU.mult, ALU.add))
            then(nc.vector.reciprocal(gate1[:], exp_sum[:]))
            then(nc.vector.tensor_tensor(rows2[:, :, GATE:GATE + 1], gate1[:].unsqueeze(2), exp_gap[:].unsqueeze(2), ALU.mult))
            then(nc.vector.tensor_copy(rows1[:, :, GATE:GATE + 1], gate1[:].unsqueeze(2)))
            dve.wait_ge(counts_ready, 2)
            then(nc.vector.tensor_copy(in_tile[:], total_ps[:, 0:TOKEN_TILES * EXPERTS].rearrange("p (t e) -> p e t", e=EXPERTS)))
            then(nc.vector.tensor_tensor_scan(up_to[:].rearrange("p e t -> p (e t)"), not_first[:].rearrange("p e t -> p (e t)"),
                                              in_tile[:].rearrange("p e t -> p (e t)"), 0.0, ALU.mult, ALU.add))
            then(nc.vector.tensor_tensor(filled[:], up_to[:, :, TOKEN_TILES - 1:TOKEN_TILES].to_broadcast(ET),
                                         block_start[:].unsqueeze(1).to_broadcast(ET), ALU.is_gt))
            then(nc.vector.tensor_reduce(blocks_of[:], filled[:], AX_X, ALU.add))
            then(nc.vector.tensor_tensor_scan(blocks_up_to[:], not_first[:, 0, 1:EXPERTS + 1], blocks_of[:], 0.0, ALU.mult, ALU.add))
            then(nc.vector.tensor_tensor(block_base[:], blocks_up_to[:], blocks_of[:], ALU.subtract))
            then(nc.vector.tensor_tensor(base[:], up_to[:], in_tile[:], ALU.subtract))
            then(nc.vector.scalar_tensor_tensor(out=base2[:], in0=block_base[:].unsqueeze(2).to_broadcast(ET), scalar=float(BLOCK),
                                                in1=base[:], op0=ALU.mult, op1=ALU.add))
            then(nc.vector.tensor_tensor(place[:], before_ps[:, 0:TOKEN_TILES * EXPERTS].rearrange("p (t e) -> p t e", e=EXPERTS),
                                         base2[:].rearrange("p e t -> p t e"), ALU.add))
            for k in range(TOP):
                then(nc.vector.tensor_tensor(at_expert[:], place[:], hot[:, k], ALU.mult))
                then(nc.vector.tensor_reduce(slot_f[:, k], at_expert[:], AX_X, ALU.add))
                then(nc.vector.tensor_copy(slot_at[:, k], slot_f[:, k]))
                dve.sem_inc(slots_known, 1)
            TABLE = [1, TABLE_LEN, EXPERTS]
            then(nc.vector.tensor_tensor(passed_block[:], number[0:1].unsqueeze(2).to_broadcast(TABLE),
                                         blocks_up_to[0:1].unsqueeze(1).to_broadcast(TABLE), ALU.is_ge))
            then(nc.vector.tensor_reduce(expert_f[:], passed_block[:], AX_X, ALU.add))
            then(nc.vector.tensor_scalar(expert_capped[:], expert_f[:], float(EXPERTS - 1), None, ALU.min))
            then(nc.vector.tensor_copy(expert_of[:], expert_capped[:]))


def shared_expert(nc, a, x1_all, rows1, rows2, w32, w16, b16, pick, x16, slot_at):
    ctx = ExitStack()
    with ctx:
        def sb(name, shape, dt=F32):
            return ctx.enter_context(nc.sbuf_tensor(name, shape, dt))

        def ps(name, shape, dt=F32):
            return ctx.enter_context(nc.psum_tensor(name, shape, dt))

        def sem(name):
            return ctx.enter_context(nc.semaphore(name))

        LAG = 2
        STEPS = TOKEN_TILES + LAG
        COLS = EXPERTS * BOTH // TOKEN_TILES
        hid = sb("hid", [P, 4, HIDDEN])
        hid16 = sb("hid16", [P, 4, 2, HIDDEN], F16)
        h_ps = ps("h_ps", [P, 4, HIDDEN])
        y_ps = ps("y_ps", [P, 4, 512])
        hidden_ready, activated, hidden_high, hidden_low = (
            sem("hidden_ready"), sem("activated"), sem("hidden_high"), sem("hidden_low"))
        projected, added, expert_low = sem("projected"), sem("added"), sem("expert_low")
        block = ctx.enter_context(nc.Block())

        def at(u, c, back=0):
            return Tile(u, c, back, TOKEN_TILES)

        @block.gpsimd
        def _(pool):
            for k, rows in enumerate((rows1, rows2)):
                place_rows(nc, a, rows, slot_at, k, range(EARLY_PLACED, TOKEN_TILES))
            pool.wait_ge(a["rows_placed"], 16 * TOP * TOKEN_TILES)

        @block.tensor
        def _(pe):
            def step(u, c):
                t = at(u, c)
                if t.exists():
                    if t.since(4):
                        pe.wait_ge(activated, t.n - 3)
                    if t.fixed:
                        x_hi, x_lo = x16[:, t.n, 0], x16[:, t.n, 1]
                    else:
                        x_hi, x_lo = (x16[:, bass.ds(t.n, 1), part].rearrange("p o n -> p (o n)") for part in range(2))
                    shared_fc_bias(nc, h_ps[:, t.buf], b16, pick)
                    fc_matmuls(nc, h_ps[:, t.buf], w16, SHARED, x_hi, x_lo, P, True).then_inc(hidden_ready, 1)
                t = at(u, c, LAG)
                if t.exists():
                    pe.wait_ge(hidden_low, t.n + 1)
                    if t.since(4):
                        pe.wait_ge(added, t.n - 3)
                    proj_matmuls(nc, y_ps[:, t.buf, 0:D], w16, b16, pick, SHARED, hid16[:, t.buf, 0], hid16[:, t.buf, 1], P)\
                      .then_inc(projected, 1)
            run_tiles(pe, step, STEPS, TOKEN_TILES // 4)

        @block.scalar
        def _(act):
            def step(u, c):
                t = at(u, c)
                if t.exists():
                    act.wait_ge(hidden_ready, t.n + 1)
                    if t.since(4):
                        act.wait_ge(hidden_low, t.n - 3)
                    nc.scalar.activation(hid[:, t.buf], h_ps[:, t.buf], ACT.Gelu_apprx_tanh, scale=1.0 / UNIT)\
                      .then_inc(activated, 1)
                    if t.since(4):
                        act.wait_ge(projected, t.n - 3)
                    act.wait_ge(activated, t.n + 1)
                    nc.scalar.activation(hid16[:, t.buf, 0], hid[:, t.buf], ACT.Copy, scale=X_UNIT)\
                      .then_inc(hidden_high, 1)
            run_tiles(act, step, TOKEN_TILES, TOKEN_TILES // 4)

        @block.vector
        def _(dve):
            w32_flat = w32.rearrange("p e c -> p (e c)")
            w_hi, w_lo = (w16[:, part].rearrange("p e c -> p (e c)") for part in range(2))

            def step(u, c):
                t = at(u, c)
                if t.exists():
                    cols = slice(t.n * COLS, (t.n + 1) * COLS) if t.fixed else bass.ds(t.n * COLS, COLS)
                    nc.vector.scalar_tensor_tensor(out=w_lo[:, cols], in0=w32_flat[:, cols], scalar=W_UNIT, in1=w_hi[:, cols],
                                                   op0=ALU.mult, op1=ALU.subtract).then_inc(expert_low, 1)
                    dve.wait_ge(hidden_high, t.n + 1)
                    if t.since(4):
                        dve.wait_ge(projected, t.n - 3)
                    nc.vector.scalar_tensor_tensor(out=hid16[:, t.buf, 1], in0=hid[:, t.buf], scalar=X_UNIT,
                                                   in1=hid16[:, t.buf, 0], op0=ALU.mult, op1=ALU.subtract).then_inc(hidden_low, 1)
                t = at(u, c, LAG)
                if t.exists():
                    rows = slice(t.n, t.n + 1) if t.fixed else bass.ds(t.n, 1)
                    dve.wait_ge(projected, t.n + 1)
                    nc.vector.scalar_tensor_tensor(out=x1_all[:, rows], in0=y_ps[:, t.buf:t.buf + 1, 0:D], scalar=1.0 / UNIT,
                                                   in1=x1_all[:, rows], op0=ALU.mult, op1=ALU.add).then_inc(added, 1)
            run_tiles(dve, step, STEPS, TOKEN_TILES // 4)


def routed_experts(nc, a, w16, b16, pick, ident_h, expert_of, b_units):
    passed = a["passed"]
    ctx = ExitStack()
    with ctx:
        def sb(name, shape, dt=F32):
            return ctx.enter_context(nc.sbuf_tensor(name, shape, dt))

        def ps(name, shape, dt=F32):
            return ctx.enter_context(nc.psum_tensor(name, shape, dt))

        def sem(name):
            return ctx.enter_context(nc.semaphore(name))

        FC_LAG, PROJ_LAG, GATE_LAG = 1, 3, 4
        STEPS = SLOT_BLOCKS + PROJ_LAG
        EARLY = 8
        LOAD = 16
        ALL_LOADED = 16 * -(-(SLOT_TILES - 2 * EARLY) // LOAD)
        LOOP_END = SLOT_BLOCKS // 4
        WIDE = CHUNKS * BLOCK
        rows_in = a["w32_or_slots"][:, 0:SLOT_TILES * ROW].rearrange("p (s r) -> p s r", r=ROW)
        parts_in = a["w32_or_slots"][:].bitcast(F16)[:, 0:SLOT_TILES * ROW16].rearrange("p (s r) -> p s r", r=ROW16)
        rows16 = sb("rows16", [D, 4, 2, BLOCK], F16)
        dest = sb("dest", [P, 4, 2], U32)
        bias = sb("bias", [P, 4, CHUNKS])
        hid = sb("hid_r", [P, 2, WIDE])
        hid16 = sb("hid16_r", [P, 4, 2, WIDE], F16)
        gated = sb("gated", [P, 4, 2, D])
        t_ps = ps("t_ps", [P, 2, 512])
        t16 = t_ps[:].bitcast(F16)
        h_ps = ps("h_ps_r", [P, 2, WIDE])
        y_ps = ps("y_ps_r", [P, 2, 512])
        first_loaded, early_loaded, loaded = sem("first_loaded"), sem("early_loaded"), sem("loaded")
        turned, rows_turned, dest_made = sem("slots_turned"), sem("turned_taken"), sem("dest_made")
        hidden_ready, activated, hidden_high, hidden_low = (
            sem("hidden_ready_r"), sem("activated_r"), sem("hidden_high_r"), sem("hidden_low_r"))
        projected, gated_made, bias_made = sem("projected_r"), sem("gated_made"), sem("hidden_bias_made")
        sent = [sem(f"sent{i}") for i in range(4)]
        block = ctx.enter_context(nc.Block())

        def at(u, c, back=0):
            t = Tile(u, c, back, SLOT_BLOCKS)
            t.turn = u + (c - back) // 4
            return t

        def load_experts(u, engine):
            start = isinstance(u, int) and u == 0
            lo = 0 if start else 4 * u - 4
            of = slice(lo, lo + 8) if isinstance(u, int) else bass.ds(lo, 8)
            _, values = nc.values_load_multi_w_load_instructions(
                expert_of[0:1, of], engines=[engine], min_val=0, max_val=EXPERTS - 1,
                skip_runtime_bounds_check_because="the table is capped at the last expert")
            return {k - (0 if start else 4): value for k, value in enumerate(values)}

        @block.sync
        def _(sp):
            slots = a["slots"].rearrange("(s p) r -> p s r", p=P)
            early = 2 * EARLY
            sp.dma_start(rows_in[:, 0:2], slots[:, 0:2]).then_inc(first_loaded, 16)
            sp.dma_start(rows_in[:, 2:early], slots[:, 2:early]).then_inc(early_loaded, 16)
            for lo in range(early, SLOT_TILES, LOAD):
                hi = min(lo + LOAD, SLOT_TILES)
                sp.dma_start(rows_in[:, lo:hi], slots[:, lo:hi]).then_inc(loaded, 16)

        @block.gpsimd
        def _(pool):
            def step(u, c):
                t = at(u, c)
                if t.exists():
                    wait_first(pool, passed, gated_made, t.n + 1)
                    wait_first(pool, passed, dest_made, t.n + 1)
                    for half in range(2):
                        nc.gpsimd.indirect_dma_start(out=a["results"][:, :], out_offset=bass.IndirectOffsetOnAxis(
                            ap=dest[:, t.buf, half:half + 1], axis=0), in_=gated[:, t.buf, half], in_offset=None,
                            bounds_check=TOP * TOKENS - 1, oob_is_err=False).then_inc(sent[t.buf], 16)
            run_tiles(pool, step, SLOT_BLOCKS, LOOP_END)
            for buf in range(4):
                pool.wait_ge(sent[buf], 32 * ((SLOT_BLOCKS - 1 - buf) // 4 + 1))

        @block.tensor
        def _(pe):
            table = {}

            def step(u, c):
                t = at(u, c)
                if t.exists():
                    if t.fixed and t.n == 1:
                        pe.wait_ge(early_loaded, 16)
                    if t.since(2):
                        pe.wait_ge(rows_turned, t.n - 1)
                    for half in range(2):
                        tile = 2 * t.n + half
                        for part in range(2):
                            of = parts_in[:, tile if t.fixed else bass.ds(tile, 1), part * D:(part + 1) * D]
                            if not t.fixed:
                                of = of.rearrange("p o d -> p (o d)")
                            to = (2 * part + half) * P
                            mm = nc.tensor.transpose(t16[:, t.buf % 2, to:to + P], of, ident_h[:])
                    mm.then_inc(turned, 1)
                t = at(u, c, FC_LAG)
                if t.exists():
                    pe.wait_ge(rows_turned, t.n + 1)
                    if t.since(2):
                        pe.wait_ge(activated, t.n - 1)
                    fc_matmuls(nc, h_ps[:, t.buf % 2], w16, table[c - FC_LAG], rows16[:, t.buf, 0],
                               rows16[:, t.buf, 1], BLOCK, False).then_inc(hidden_ready, 1)
                t = at(u, c, PROJ_LAG)
                if t.exists():
                    pe.wait_ge(hidden_high, t.n + 1)
                    pe.wait_ge(hidden_low, t.n + 1)
                    if t.since(2):
                        pe.wait_ge(gated_made, t.n - 1)
                    for half in range(2):
                        mm = proj_matmuls(nc, y_ps[:, t.buf % 2, half * D:(half + 1) * D], w16, b16, pick, table[c - PROJ_LAG],
                                          hid16[:, t.buf, 0, half * P:], hid16[:, t.buf, 1, half * P:], BLOCK)
                    mm.then_inc(projected, 1)

            def four_steps(u):
                table.clear()
                table.update(load_experts(u, mybir.EngineType.PE))
                for c in range(4):
                    if not isinstance(u, int) or 4 * u + c < STEPS:
                        step(u, c)

            pe.wait_ge(first_loaded, 16)
            for u in range(EARLY // 4):
                four_steps(u)
            pe.wait_ge(loaded, ALL_LOADED)
            with pe.Fori(EARLY // 4, LOOP_END) as u:
                four_steps(u)
            for u in range(LOOP_END, -(-STEPS // 4)):
                four_steps(u)

        @block.scalar
        def _(act):
            def step(u, c):
                t = at(u, c, FC_LAG)
                if t.exists():
                    act.wait_ge(hidden_ready, t.n + 1)
                    if t.since(2):
                        act.wait_ge(hidden_low, t.n - 1)
                    act.wait_ge(bias_made, t.n + 1)
                    for k in range(CHUNKS):
                        cols = slice(k * BLOCK, (k + 1) * BLOCK)
                        act_ = nc.scalar.activation(hid[:, t.buf % 2, cols], h_ps[:, t.buf % 2, cols], ACT.Gelu_apprx_tanh,
                                                    scale=1.0 / UNIT, bias=bias[:, t.buf, k:k + 1])
                    act_.then_inc(activated, 1)
            run_tiles(act, step, SLOT_BLOCKS + FC_LAG, LOOP_END)

        @block.vector
        def _(dve):
            table = {}

            def step(u, c):
                t = at(u, c)
                if t.exists():
                    if t.since(4):
                        dve.wait_ge(activated, t.n - 3)
                    nc.vector.tensor_copy(bias[:, t.buf:t.buf + 1], b_units[:, bass.ds(table[c], 1)])\
                      .then_inc(bias_made, 1)
                    dve.wait_ge(turned, t.n + 1)
                    if t.since(4):
                        dve.wait_ge(hidden_ready, t.n - 3)
                    nc.vector.tensor_copy(rows16[:, t.buf].rearrange("p k n -> p (k n)"), t16[:, t.buf % 2, 0:2 * BLOCK])\
                      .then_inc(rows_turned, 1)
                t = at(u, c, GATE_LAG)
                if t.exists():
                    tiles = slice(2 * t.n, 2 * t.n + 2) if t.fixed else bass.ds(2 * t.n, 2)
                    if t.since(4):
                        dve.wait_ge(sent[t.buf], 32 * t.turn)
                    nc.vector.tensor_copy(dest[:, t.buf].unsqueeze(2), rows_in[:, tiles, DEST:DEST + 1].bitcast(U32))\
                      .then_inc(dest_made, 1)
                    dve.wait_ge(projected, t.n + 1)
                    nc.vector.tensor_tensor(gated[:, t.buf], y_ps[:, t.buf % 2, 0:2 * D].rearrange("p (k d) -> p k d", d=D),
                                            rows_in[:, tiles, GATE:GATE + 1].to_broadcast([P, 2, D]), ALU.mult)\
                      .then_inc(gated_made, 1)
                t = at(u, c, FC_LAG)
                if t.exists():
                    dve.wait_ge(activated, t.n + 1)
                    if t.since(4):
                        dve.wait_ge(projected, t.n - 3)
                    nc.vector.tensor_scalar(hid16[:, t.buf, 0], hid[:, t.buf % 2], X_UNIT, 1.0, ALU.mult, ALU.mult)\
                      .then_inc(hidden_high, 1)
                    dve.wait_ge(hidden_high, t.n + 1)
                    nc.vector.scalar_tensor_tensor(out=hid16[:, t.buf, 1], in0=hid[:, t.buf % 2], scalar=X_UNIT,
                                                   in1=hid16[:, t.buf, 0], op0=ALU.mult, op1=ALU.subtract).then_inc(hidden_low, 1)

            def four_steps(u):
                table.clear()
                table.update(load_experts(u, mybir.EngineType.DVE))
                for c in range(4):
                    if not isinstance(u, int) or 4 * u + c < SLOT_BLOCKS + GATE_LAG:
                        step(u, c)

            dve.wait_ge(early_loaded, 16)
            for u in range(EARLY // 4):
                four_steps(u)
            dve.wait_ge(loaded, ALL_LOADED)
            with dve.Fori(EARLY // 4, LOOP_END) as u:
                four_steps(u)
            for u in range(LOOP_END, -(-(SLOT_BLOCKS + GATE_LAG) // 4)):
                four_steps(u)


def add_and_normalise(nc, a, x1_all):
    ctx = ExitStack()
    with ctx:
        def sb(name, shape, dt=F32):
            return ctx.enter_context(nc.sbuf_tensor(name, shape, dt))

        def sem(name):
            return ctx.enter_context(nc.semaphore(name))

        DEEP = 4
        first, second = (sb(f"expert{k}", [P, GROUPS, GROUP, D]) for k in range(TOP))
        both = sb("both", [P, DEEP, GROUP, D])
        total = sb("total", [P, DEEP, GROUP, D])
        minus_half2 = sb("minus_half2", [P, GROUP])
        stats2 = sb("stats2", [P, GROUP, 6])
        mean_var2 = sb("mean_var2", [P, DEEP, GROUP, 2])
        var_eps2 = sb("var_eps2", [P, DEEP, GROUP])
        rstd2 = sb("rstd2", [P, DEEP, GROUP])
        shift2 = sb("shift2", [P, DEEP, GROUP])
        results_in = [sem(f"results_in{g}") for g in range(GROUPS)]
        shifts_made = sem("shifts_made")
        half_made, both_made, totals, scale2_done, normed, out_written = (
            sem("half_made"), sem("both_made"), sem("totals"), sem("scale2_done"), sem("normed"), sem("out_written"))
        DVE_STEPS = 2 + 2 * GROUP
        block = ctx.enter_context(nc.Block())

        @block.sync
        def _(sp):
            for g in range(GROUPS):
                for k, to in enumerate((first, second)):
                    lo = k * TOKENS + g * GROUP * P
                    sp.dma_start(to[:, g], a["results"][lo:lo + GROUP * P].rearrange("(t p) d -> p t d", p=P))\
                      .then_inc(results_in[g], 16)
            for g in range(GROUPS):
                sp.wait_ge(normed, GROUP * (g + 1))
                sp.dma_start(a["out"][g * GROUP * P:(g + 1) * GROUP * P].rearrange("(t p) d -> p t d", p=P), first[:, g])\
                  .then_inc(out_written, 16)
            sp.wait_ge(out_written, 16 * GROUPS)

        @block.gpsimd
        def _(pool):
            nc.gpsimd.memset(minus_half2[:], -0.5).then_inc(half_made, 1)
            pool.wait_ge(half_made, 1)

            def sum_experts(g):
                pool.wait_ge(results_in[g], 32)
                if g >= DEEP:
                    pool.wait_ge(totals, DVE_STEPS * (g - DEEP) + 1)
                nc.gpsimd.tensor_tensor(both[:, g % DEEP], first[:, g], second[:, g], ALU.add).then_inc(both_made, 1)

            sum_experts(0)
            for g in range(GROUPS):
                if g + 1 < GROUPS:
                    sum_experts(g + 1)
                pool.wait_ge(totals, DVE_STEPS * (g + 1))
                if g >= DEEP:
                    pool.wait_ge(normed, GROUP * (g - DEEP + 1))
                    pool.wait_ge(shifts_made, g - DEEP + 1)
                nc.gpsimd.tensor_tensor(rstd2[:, g % DEEP], var_eps2[:, g % DEEP], minus_half2[:], ALU.pow)\
                  .then_inc(scale2_done, 1)

        @block.vector
        def _(dve):
            def make_shift(g):
                dve.wait_ge(scale2_done, g + 1)
                nc.vector.scalar_tensor_tensor(out=shift2[:, g % DEEP].unsqueeze(2), in0=mean_var2[:, g % DEEP, :, 0:1], scalar=-1.0,
                                               in1=rstd2[:, g % DEEP].unsqueeze(2), op0=ALU.mult, op1=ALU.mult)\
                  .then_inc(shifts_made, 1)

            for g in range(GROUPS):
                dve.wait_ge(both_made, g + 1)
                if g >= DEEP:
                    dve.wait_ge(normed, GROUP * (g - DEEP + 1))
                nc.vector.tensor_tensor(total[:, g % DEEP], x1_all[:, g * GROUP:(g + 1) * GROUP], both[:, g % DEEP], ALU.add)\
                  .then_inc(totals, 1)
                dve.wait_ge(totals, DVE_STEPS * g + 1)
                for t in range(GROUP):
                    nc.vector.bn_stats(stats2[:, t], total[:, g % DEEP, t]).then_inc(totals, 1)
                dve.wait_ge(totals, DVE_STEPS * g + 1 + GROUP)
                for t in range(GROUP):
                    nc.vector.bn_aggr(mean_var2[:, g % DEEP, t], stats2[:, t]).then_inc(totals, 1)
                dve.wait_ge(totals, DVE_STEPS * g + 1 + 2 * GROUP)
                nc.vector.tensor_scalar(var_eps2[:, g % DEEP].unsqueeze(2), mean_var2[:, g % DEEP, :, 1:2], EPS, None, ALU.add)\
                  .then_inc(totals, 1)
                if g >= 1:
                    make_shift(g - 1)
            make_shift(GROUPS - 1)

        @block.scalar
        def _(act):
            for g in range(GROUPS):
                act.wait_ge(shifts_made, g + 1)
                for t in range(GROUP):
                    nc.scalar.activation(first[:, g, t], total[:, g % DEEP, t], ACT.Identity, scale=rstd2[:, g % DEEP, t:t + 1],
                                         bias=shift2[:, g % DEEP, t:t + 1]).then_inc(normed, 1)


def build_program(nc, a):
    with ExitStack() as ctx:
        a["passed"] = ctx.enter_context(nc.semaphore("passed"))
        make_moe_buffers(nc, a, ctx)
        build_attention(nc, a)
        build_moe(nc, a, ctx)


def kernel(L0_attn_x, L0_attn_Wq, L0_attn_bq, L0_attn_Wk, L0_attn_bk, L0_attn_Wv, L0_attn_bv, L0_attn_Wo, L0_attn_bo,
           L0_attn_head_mask, L0_ffn_Wfc_s, L0_ffn_bfc_s, L0_ffn_Wproj_s, L0_ffn_bproj_s, L0_ffn_Wr, L0_ffn_Wfc,
           L0_ffn_bfc, L0_ffn_Wproj, L0_ffn_bproj):
    import numpy as np
    import concourse.bacc as bacc
    from concourse.bass_utils import run_bass_kernel_spmd

    def by_dim(w):
        return np.asarray(w).reshape(HEADS, DH, -1).transpose(1, 0, 2).reshape(D, -1)

    def by_quad(w):
        return np.asarray(w).reshape(2, 2, 4, DH, -1).transpose(1, 0, 2, 3, 4).reshape(D, -1)

    def by_column_tile(w):
        w = np.asarray(w)
        n = w.shape[0] // HEADS
        return w.reshape(2, 2, 4, n, -1).transpose(0, 2, 1, 3, 4).reshape(w.shape[0], -1)

    x = np.asarray(L0_attn_x).reshape(TOKENS, D)

    def with_shared(routed, shared):
        return np.concatenate([np.asarray(routed), np.asarray(shared)[None]])

    w_fc = with_shared(L0_ffn_Wfc, L0_ffn_Wfc_s)
    w_proj = with_shared(L0_ffn_Wproj, L0_ffn_Wproj_s)
    arrays = {
        "x": x,
        "x_t": x.T,
        "wq_t": by_dim(L0_attn_Wq).T,
        "wk_t": by_dim(L0_attn_Wk).T,
        "wv_t": by_quad(L0_attn_Wv).T,
        "wo_t": by_column_tile(np.asarray(L0_attn_Wo).T),
        "bq": by_dim(L0_attn_bq),
        "bk": by_dim(L0_attn_bk),
        "bv": by_column_tile(L0_attn_bv),
        "mask": by_column_tile(L0_attn_head_mask).reshape(HEADS),
        "bo": np.asarray(L0_attn_bo),
        "w_fc": w_fc.transpose(1, 0, 2),
        "b_fc_shared": np.asarray(L0_ffn_bfc_s),
        "b_units": with_shared(L0_ffn_bfc, L0_ffn_bfc_s).reshape(ALL, CHUNKS, P).transpose(2, 0, 1),
        "w_proj": w_proj.reshape(ALL, CHUNKS, P, D).transpose(2, 0, 1, 3).reshape(P, ALL, HIDDEN),
        "w_r": np.asarray(L0_ffn_Wr),
        "b_proj": with_shared(L0_ffn_bproj, L0_ffn_bproj_s),
    }
    nc = bacc.Bacc("TRN2", target_bir_lowering=False, num_devices=1)
    maps, a = {}, {}
    for name, array in arrays.items():
        maps[f"in_{name}"] = np.ascontiguousarray(array)
        a[name] = nc.dram_tensor(f"in_{name}", maps[f"in_{name}"].shape, F32, kind="ExternalInput").ap()
    a["out"] = nc.dram_tensor("result", [TOKENS, D], F32, kind="ExternalOutput").ap()
    build_program(nc, a)
    r = run_bass_kernel_spmd(nc, [maps], core_ids=[0])
    return r.results[0]["result"].reshape(BATCHES, SEQ, D)
```
